# Optimizing a Trainium2 kernel written in Bass

```python
import numpy as np
import jax
import jax.numpy as jnp

def _softmax(x, axis=-1):
    return jax.nn.softmax(x, axis=axis)

def _gelu(x):
    return jax.nn.gelu(x, approximate=True)

def _silu(x):
    return jax.nn.silu(x)

def _sigmoid(x):
    return jax.nn.sigmoid(x)

def _layernorm(x, axis=-1, eps=1e-05):
    m = jnp.mean(x, axis=axis, keepdims=True)
    v = jnp.var(x, axis=axis, keepdims=True)
    return (x - m) / jnp.sqrt(v + eps)

def _scatter_add(tgt, idx, src, axis=0):
    return tgt.at[idx].add(src)

def _segment_sum(src, seg, n):
    return jax.ops.segment_sum(src, seg, n)
kernel_name = 'mk_gnn_resnorm_d4_gnn_r8_37ecbc'

def setup_inputs(seed: int=0):
    np.random.seed(seed)
    _w = jnp.asarray

    def _rec_inputs():
        import jax
        import jax.numpy as jnp
        _gk = jax.random.key(seed)
        x = -0.0005121 + 1.001 * jax.random.normal(jax.random.fold_in(_gk, 1), (12500, 32), jnp.float32)
        src = jax.random.randint(jax.random.fold_in(_gk, 2), (400000,), 0, 12500, jnp.int32)
        dst = jax.random.randint(jax.random.fold_in(_gk, 3), (400000,), 0, 12500, jnp.int32)
        _o = jnp.argsort(dst, stable=True)
        src = src[_o]
        dst = dst[_o]
        edge_attr_10 = jax.random.uniform(jax.random.fold_in(_gk, 13), (400000, 10), jnp.float32, 0.0, 0.999998)
        edge_attr_3 = 0.00158508 + 0.999651 * jax.random.normal(jax.random.fold_in(_gk, 14), (400000, 3), jnp.float32)
        edge_attr_32 = 0.000196303 + 1.00016 * jax.random.normal(jax.random.fold_in(_gk, 15), (400000, 32), jnp.float32)
        edge_weight = jax.random.uniform(jax.random.fold_in(_gk, 17), (400000,), jnp.float32, 0.0, 0.999997)
        return (x, src, dst, edge_attr_10, edge_attr_3, edge_attr_32, edge_weight)
    x, src, dst, edge_attr_10, edge_attr_3, edge_attr_32, edge_weight = _rec_inputs()

    def _L0_gnn_setup():
        import jax, jax.numpy as jnp
        import numpy as np
        N_NODES = 12500
        key = jax.random.key(seed)
        k1, k2, k3 = jax.random.split(key, 3)
        in_feat = jax.random.normal(k1, (N_NODES, 32), dtype=jnp.float32)
        src = jax.random.randint(k2, (200000,), 0, N_NODES, dtype=jnp.int64)
        dst = jax.random.randint(k3, (200000,), 0, N_NODES, dtype=jnp.int64)
        return {'in_feat': in_feat, 'src': src, 'dst': dst}
    _L0_gnn_all = _L0_gnn_setup()
    _L0_gnn_in = {k: v for k, v in _L0_gnn_all.items() if k in ()}
    del _L0_gnn_all

    def _L1_gnn_setup():
        import jax, jax.numpy as jnp
        import numpy as np
        N = 12500
        E = 100000
        NF = 32
        EF = 32
        L = 64
        ENTRY = NF + EF
        SECOND = NF + L
        SLOPE = 0.1
        EPS = 1e-05

        def _bn(h, g, b):
            m = h.mean(0)
            v = ((h - m) ** 2).mean(0)
            return (h - m) * jax.lax.rsqrt(v + EPS) * g + b

        def _lrelu(h):
            return jnp.where(h > 0, h, SLOPE * h)
        key = jax.random.key(seed)
        ks = jax.random.split(key, 16)

        def w(k, i, o):
            return jax.random.normal(k, (i, o), jnp.float32) / np.float32(np.sqrt(i))

        def bvec(k, o):
            return jax.random.normal(k, (o,), jnp.float32) * 0.01
        inp = {'x': jax.random.normal(ks[0], (N, NF), jnp.float32), 'edge_index': jax.random.randint(ks[1], (2, E), 0, N), 'edge_attr': jax.random.normal(ks[2], (E, EF), jnp.float32), 'u': jax.random.normal(ks[3], (1, 4), jnp.float32), 'batch': jnp.zeros((N,), jnp.int32), 'm1_g1': jnp.ones((ENTRY,), jnp.float32), 'm1_b1': jnp.zeros((ENTRY,), jnp.float32), 'm1_w1': w(ks[4], ENTRY, L), 'm1_c1': bvec(ks[5], L), 'm1_g2': jnp.ones((L,), jnp.float32), 'm1_b2': jnp.zeros((L,), jnp.float32), 'm1_w2': w(ks[6], L, L), 'm1_c2': bvec(ks[7], L), 'm1_g3': jnp.ones((L,), jnp.float32), 'm1_b3': jnp.zeros((L,), jnp.float32), 'm1_w3': w(ks[8], L, L), 'm1_c3': bvec(ks[9], L), 'm2_g1': jnp.ones((SECOND,), jnp.float32), 'm2_b1': jnp.zeros((SECOND,), jnp.float32), 'm2_w1': w(ks[10], SECOND, SECOND), 'm2_c1': bvec(ks[11], SECOND), 'm2_g2': jnp.ones((SECOND,), jnp.float32), 'm2_b2': jnp.zeros((SECOND,), jnp.float32), 'm2_w2': w(ks[12], SECOND, SECOND), 'm2_c2': bvec(ks[13], SECOND), 'm2_g3': jnp.ones((SECOND,), jnp.float32), 'm2_b3': jnp.zeros((SECOND,), jnp.float32), 'm2_w3': w(ks[14], SECOND, NF), 'm2_c3': bvec(ks[15], NF)}
        return inp
    _L1_gnn_all = _L1_gnn_setup()
    _L1_gnn_in = {k: v for k, v in _L1_gnn_all.items() if k in ('u', 'm1_g1', 'm1_b1', 'm1_w1', 'm1_c1', 'm1_g2', 'm1_b2', 'm1_w2', 'm1_c2', 'm1_g3', 'm1_b3', 'm1_w3', 'm1_c3', 'm2_g1', 'm2_b1', 'm2_w1', 'm2_c1', 'm2_g2', 'm2_b2', 'm2_w2', 'm2_c2', 'm2_g3', 'm2_b3', 'm2_w3', 'm2_c3')}
    del _L1_gnn_all

    def _L2_gnn_setup():
        import jax, jax.numpy as jnp
        import numpy as np
        N_NODES = 6250
        DEG = 16
        N_HEAD = 4
        F_IN = 32
        F_OUT = 32
        key = jax.random.key(seed)
        k_h, k_w, k_fw, k_fb = jax.random.split(key, 4)
        h = jax.random.normal(k_h, (N_NODES, F_IN), dtype=jnp.float32)
        src = jnp.repeat(jnp.arange(N_NODES, dtype=jnp.int64), DEG)
        offs = (jnp.arange(DEG, dtype=jnp.int64) + 1) * 97
        dst = (src.reshape(N_NODES, DEG) + offs[None, :]).reshape(-1) % N_NODES
        edge_index = jnp.stack([src, dst], axis=0)
        gain = 1.414
        bound_w = gain * np.sqrt(6.0 / (F_IN + F_OUT))
        w = jax.random.uniform(k_w, (N_HEAD, F_IN, F_OUT), jnp.float32, -bound_w, bound_w)
        bound_fc = np.sqrt(1.0 / (2 * F_OUT))
        fc_w = jax.random.uniform(k_fw, (1, 2 * F_OUT), jnp.float32, -bound_fc, bound_fc)
        fc_b = jax.random.uniform(k_fb, (1,), jnp.float32, -bound_fc, bound_fc)
        bias = jnp.zeros((F_OUT,), jnp.float32)
        return {'h': h, 'edge_index': edge_index, 'w': w, 'fc_w': fc_w, 'fc_b': fc_b, 'bias': bias}
    _L2_gnn_all = _L2_gnn_setup()
    _L2_gnn_in = {k: v for k, v in _L2_gnn_all.items() if k in ('w', 'fc_w', 'fc_b', 'bias')}
    del _L2_gnn_all

    def _L3_gnn_setup():
        import jax, jax.numpy as jnp
        import numpy as np
        SQRT3 = 3.0 ** 0.5

        def _mlp(emb, w1, w2):
            h = jax.nn.relu(emb @ w1 / jnp.sqrt(jnp.float32(w1.shape[0])))
            return h @ w2 / jnp.sqrt(jnp.float32(w2.shape[0]))
        key = jax.random.key(seed)
        ks = jax.random.split(key, 10)
        N, E = (1250, 20000)
        x = jax.random.normal(ks[0], (N, 32), jnp.float32)
        edge_src = jax.random.randint(ks[1], (E,), 0, N)
        edge_dst = jax.random.randint(ks[2], (E,), 0, N)
        edge_vec = jax.random.normal(ks[3], (E, 3), jnp.float32)
        emb = jax.random.uniform(ks[4], (E, 10), jnp.float32)
        norm = jax.random.uniform(ks[5], (E,), jnp.float32)
        fc1_w1 = jax.random.normal(ks[6], (10, 16), jnp.float32)
        fc1_w2 = jax.random.normal(ks[7], (16, 512), jnp.float32)
        fc2_w1 = jax.random.normal(ks[8], (10, 16), jnp.float32)
        fc2_w2 = jax.random.normal(ks[9], (16, 384), jnp.float32)
        return dict(x=x, edge_src=edge_src, edge_dst=edge_dst, edge_vec=edge_vec, emb=emb, norm=norm, num_nodes=N, fc1_w1=fc1_w1, fc1_w2=fc1_w2, fc2_w1=fc2_w1, fc2_w2=fc2_w2)
    _L3_gnn_all = _L3_gnn_setup()
    _L3_gnn_in = {k: v for k, v in _L3_gnn_all.items() if k in ('fc1_w1', 'fc1_w2', 'fc2_w1', 'fc2_w2')}
    del _L3_gnn_all
    return {'x': x, 'src': src, 'dst': dst, 'edge_attr_10': edge_attr_10, 'edge_attr_3': edge_attr_3, 'edge_attr_32': edge_attr_32, 'edge_weight': edge_weight, 'L1_gnn_u': _L1_gnn_in['u'], 'L1_gnn_m1_g1': _L1_gnn_in['m1_g1'], 'L1_gnn_m1_b1': _L1_gnn_in['m1_b1'], 'L1_gnn_m1_w1': _L1_gnn_in['m1_w1'], 'L1_gnn_m1_c1': _L1_gnn_in['m1_c1'], 'L1_gnn_m1_g2': _L1_gnn_in['m1_g2'], 'L1_gnn_m1_b2': _L1_gnn_in['m1_b2'], 'L1_gnn_m1_w2': _L1_gnn_in['m1_w2'], 'L1_gnn_m1_c2': _L1_gnn_in['m1_c2'], 'L1_gnn_m1_g3': _L1_gnn_in['m1_g3'], 'L1_gnn_m1_b3': _L1_gnn_in['m1_b3'], 'L1_gnn_m1_w3': _L1_gnn_in['m1_w3'], 'L1_gnn_m1_c3': _L1_gnn_in['m1_c3'], 'L1_gnn_m2_g1': _L1_gnn_in['m2_g1'], 'L1_gnn_m2_b1': _L1_gnn_in['m2_b1'], 'L1_gnn_m2_w1': _L1_gnn_in['m2_w1'], 'L1_gnn_m2_c1': _L1_gnn_in['m2_c1'], 'L1_gnn_m2_g2': _L1_gnn_in['m2_g2'], 'L1_gnn_m2_b2': _L1_gnn_in['m2_b2'], 'L1_gnn_m2_w2': _L1_gnn_in['m2_w2'], 'L1_gnn_m2_c2': _L1_gnn_in['m2_c2'], 'L1_gnn_m2_g3': _L1_gnn_in['m2_g3'], 'L1_gnn_m2_b3': _L1_gnn_in['m2_b3'], 'L1_gnn_m2_w3': _L1_gnn_in['m2_w3'], 'L1_gnn_m2_c3': _L1_gnn_in['m2_c3'], 'L2_gnn_w': _L2_gnn_in['w'], 'L2_gnn_fc_w': _L2_gnn_in['fc_w'], 'L2_gnn_fc_b': _L2_gnn_in['fc_b'], 'L2_gnn_bias': _L2_gnn_in['bias'], 'L3_gnn_fc1_w1': _L3_gnn_in['fc1_w1'], 'L3_gnn_fc1_w2': _L3_gnn_in['fc1_w2'], 'L3_gnn_fc2_w1': _L3_gnn_in['fc2_w1'], 'L3_gnn_fc2_w2': _L3_gnn_in['fc2_w2']}

def reference(x, src, dst, edge_attr_10, edge_attr_3, edge_attr_32, edge_weight, L1_gnn_u, L1_gnn_m1_g1, L1_gnn_m1_b1, L1_gnn_m1_w1, L1_gnn_m1_c1, L1_gnn_m1_g2, L1_gnn_m1_b2, L1_gnn_m1_w2, L1_gnn_m1_c2, L1_gnn_m1_g3, L1_gnn_m1_b3, L1_gnn_m1_w3, L1_gnn_m1_c3, L1_gnn_m2_g1, L1_gnn_m2_b1, L1_gnn_m2_w1, L1_gnn_m2_c1, L1_gnn_m2_g2, L1_gnn_m2_b2, L1_gnn_m2_w2, L1_gnn_m2_c2, L1_gnn_m2_g3, L1_gnn_m2_b3, L1_gnn_m2_w3, L1_gnn_m2_c3, L2_gnn_w, L2_gnn_fc_w, L2_gnn_fc_b, L2_gnn_bias, L3_gnn_fc1_w1, L3_gnn_fc1_w2, L3_gnn_fc2_w1, L3_gnn_fc2_w2):
    import jax
    import jax.numpy as jnp

    def _L0_gnn_ref(in_feat, src, dst):
        import jax, jax.numpy as jnp
        import numpy as np
        N_NODES = 12500
        n = in_feat.shape[0]
        ones = jnp.ones(src.shape[0], dtype=in_feat.dtype)
        out_deg = jax.ops.segment_sum(ones, src, num_segments=n)
        in_deg = jax.ops.segment_sum(ones, dst, num_segments=n)
        out_norm = jax.lax.rsqrt(jnp.maximum(out_deg, 1.0))
        in_norm = jax.lax.rsqrt(jnp.maximum(in_deg, 1.0))
        h = in_feat * out_norm[:, None]
        msg = h[src]
        agg = jax.ops.segment_sum(msg, dst, num_segments=n)
        return agg * in_norm[:, None]

    def _L1_gnn_ref(x, edge_index, edge_attr, u, batch, m1_g1, m1_b1, m1_w1, m1_c1, m1_g2, m1_b2, m1_w2, m1_c2, m1_g3, m1_b3, m1_w3, m1_c3, m2_g1, m2_b1, m2_w1, m2_c1, m2_g2, m2_b2, m2_w2, m2_c2, m2_g3, m2_b3, m2_w3, m2_c3):
        import jax, jax.numpy as jnp
        import numpy as np
        N = 12500
        E = 100000
        NF = 32
        EF = 32
        L = 64
        ENTRY = NF + EF
        SECOND = NF + L
        SLOPE = 0.1
        EPS = 1e-05

        def _bn(h, g, b):
            m = h.mean(0)
            v = ((h - m) ** 2).mean(0)
            return (h - m) * jax.lax.rsqrt(v + EPS) * g + b

        def _lrelu(h):
            return jnp.where(h > 0, h, SLOPE * h)
        row, col = (edge_index[0], edge_index[1])
        h = jnp.concatenate([x[row], edge_attr], axis=1)
        h = _lrelu(_bn(h, m1_g1, m1_b1) @ m1_w1 + m1_c1)
        h = _lrelu(_bn(h, m1_g2, m1_b2) @ m1_w2 + m1_c2)
        h = _bn(h, m1_g3, m1_b3) @ m1_w3 + m1_c3
        agg = jax.ops.segment_sum(h, col, num_segments=x.shape[0])
        h2 = jnp.concatenate([x, agg], axis=1)
        h2 = _lrelu(_bn(h2, m2_g1, m2_b1) @ m2_w1 + m2_c1)
        h2 = _lrelu(_bn(h2, m2_g2, m2_b2) @ m2_w2 + m2_c2)
        out = _bn(h2, m2_g3, m2_b3) @ m2_w3 + m2_c3
        return out

    def _L2_gnn_ref(h, edge_index, w, fc_w, fc_b, bias):
        import jax, jax.numpy as jnp
        import numpy as np
        N_NODES = 6250
        DEG = 16
        N_HEAD = 4
        F_IN = 32
        F_OUT = 32
        n_head, f_in, f_out = w.shape
        n = h.shape[0]
        src, dst = (edge_index[0], edge_index[1])
        hp = jnp.einsum('nf,hfo->hno', h, w)
        w_src = fc_w[0, :f_out]
        w_dst = fc_w[0, f_out:]
        a_src = jnp.einsum('hnf,f->hn', hp, w_src)
        a_dst = jnp.einsum('hnf,f->hn', hp, w_dst)
        e = a_src[:, src] + a_dst[:, dst] + fc_b[0]
        e = jax.nn.leaky_relu(e, negative_slope=0.2)
        seg_max = jax.ops.segment_max(e.T, src, num_segments=n)
        e = jnp.exp(e - seg_max.T[:, src])
        seg_sum = jax.ops.segment_sum(e.T, src, num_segments=n)
        att = e / seg_sum.T[:, src]
        msg = att[:, :, None] * hp[:, dst, :]
        agg = jax.vmap(lambda m: jax.ops.segment_sum(m, src, num_segments=n))(msg)
        out = agg.mean(axis=0) + bias
        return out

    def _L3_gnn_ref(x, edge_src, edge_dst, edge_vec, emb, norm, num_nodes, fc1_w1, fc1_w2, fc2_w1, fc2_w2):
        import jax, jax.numpy as jnp
        import numpy as np
        SQRT3 = 3.0 ** 0.5

        def _mlp(emb, w1, w2):
            h = jax.nn.relu(emb @ w1 / jnp.sqrt(jnp.float32(w1.shape[0])))
            return h @ w2 / jnp.sqrt(jnp.float32(w2.shape[0]))
        E = edge_vec.shape[0]
        r = edge_vec / jnp.linalg.norm(edge_vec, axis=1, keepdims=True)
        sh1 = SQRT3 * r
        xs, xd = (x[edge_src], x[edge_dst])
        s1 = jnp.concatenate([xs[:, :8], xd[:, :8]], axis=1)
        v1 = jnp.concatenate([xs[:, 8:].reshape(E, 8, 3), xd[:, 8:].reshape(E, 8, 3)], axis=1)
        w = _mlp(emb, fc1_w1, fc1_w2)
        Wss = w[:, 0:128].reshape(E, 16, 8)
        Wvv = w[:, 128:256].reshape(E, 16, 8)
        Wsv = w[:, 256:384].reshape(E, 16, 8)
        Wvs = w[:, 384:512].reshape(E, 16, 8)
        a1 = 1.0 / jnp.sqrt(32.0)
        vdot1 = jnp.einsum('euk,ek->eu', v1, sh1) / SQRT3
        s_t = a1 * (jnp.einsum('eu,euw->ew', s1, Wss) + jnp.einsum('eu,euw->ew', vdot1, Wvv))
        v_t = a1 * (jnp.einsum('eu,euw->ew', s1, Wsv)[:, :, None] * sh1[:, None, :] + jnp.einsum('euk,euw->ewk', v1, Wvs))
        w2 = _mlp(emb, fc2_w1, fc2_w2)
        Ass = w2[:, 0:64].reshape(E, 8, 8)
        Avv = w2[:, 64:128].reshape(E, 8, 8)
        Bss = w2[:, 128:192].reshape(E, 8, 8)
        Bvv = w2[:, 192:256].reshape(E, 8, 8)
        Csv = w2[:, 256:320].reshape(E, 8, 8)
        Cvs = w2[:, 320:384].reshape(E, 8, 8)
        a2 = 1.0 / jnp.sqrt(16.0)
        vdot2 = jnp.einsum('euk,ek->eu', v_t, sh1) / SQRT3
        scal = a2 * (jnp.einsum('eu,euw->ew', s_t, Ass) + jnp.einsum('eu,euw->ew', vdot2, Avv))
        gates = a2 * (jnp.einsum('eu,euw->ew', s_t, Bss) + jnp.einsum('eu,euw->ew', vdot2, Bvv))
        vecs = a2 * (jnp.einsum('eu,euw->ew', s_t, Csv)[:, :, None] * sh1[:, None, :] + jnp.einsum('euk,euw->ewk', v_t, Cvs))
        edge_out = jnp.concatenate([jnp.tanh(scal), (vecs * jnp.tanh(gates)[:, :, None]).reshape(E, 24)], axis=1)
        edge_out = edge_out * norm[:, None]
        return jax.ops.segment_sum(edge_out, edge_dst, num_segments=num_nodes)
    edge_index = jnp.stack([src, dst])
    batch0 = jnp.zeros((12500,), jnp.int32)
    x = _layernorm(x + _L0_gnn_ref(x, src, dst), axis=-1)
    x = _layernorm(x + _L1_gnn_ref(x, edge_index, edge_attr_32, L1_gnn_u, batch0, L1_gnn_m1_g1, L1_gnn_m1_b1, L1_gnn_m1_w1, L1_gnn_m1_c1, L1_gnn_m1_g2, L1_gnn_m1_b2, L1_gnn_m1_w2, L1_gnn_m1_c2, L1_gnn_m1_g3, L1_gnn_m1_b3, L1_gnn_m1_w3, L1_gnn_m1_c3, L1_gnn_m2_g1, L1_gnn_m2_b1, L1_gnn_m2_w1, L1_gnn_m2_c1, L1_gnn_m2_g2, L1_gnn_m2_b2, L1_gnn_m2_w2, L1_gnn_m2_c2, L1_gnn_m2_g3, L1_gnn_m2_b3, L1_gnn_m2_w3, L1_gnn_m2_c3), axis=-1)
    x = _layernorm(x + _L2_gnn_ref(x, edge_index, L2_gnn_w, L2_gnn_fc_w, L2_gnn_fc_b, L2_gnn_bias), axis=-1)
    x = _layernorm(x + _L3_gnn_ref(x, src, dst, edge_attr_3, edge_attr_10, edge_weight, 12500, L3_gnn_fc1_w1, L3_gnn_fc1_w2, L3_gnn_fc2_w1, L3_gnn_fc2_w2), axis=-1)
    return x

_drawn_inputs = setup_inputs


def setup_inputs(seed=0):
    import zlib

    import numpy as np

    out = dict(_drawn_inputs(seed))
    spreads = {'L1_gnn_m1_g1': (1.0, 0.2),
     'L1_gnn_m1_b1': (0.0, 0.1),
     'L1_gnn_m1_g2': (1.0, 0.2),
     'L1_gnn_m1_b2': (0.0, 0.1),
     'L1_gnn_m1_g3': (1.0, 0.2),
     'L1_gnn_m1_b3': (0.0, 0.1),
     'L1_gnn_m2_g1': (1.0, 0.2),
     'L1_gnn_m2_b1': (0.0, 0.1),
     'L1_gnn_m2_g2': (1.0, 0.2),
     'L1_gnn_m2_b2': (0.0, 0.1),
     'L1_gnn_m2_g3': (1.0, 0.2),
     'L1_gnn_m2_b3': (0.0, 0.1),
     'L2_gnn_bias': (0.0, 0.1)}
    factors = {'L1_gnn_m1_c1': 8.0,
     'L1_gnn_m1_c2': 8.0,
     'L1_gnn_m1_c3': 6.013,
     'L1_gnn_m2_c1': 8.0,
     'L1_gnn_m2_c2': 8.0,
     'L1_gnn_m2_c3': 7.648}
    for name, (base, spread) in spreads.items():
        noise = np.random.default_rng([zlib.crc32(name.encode()), seed]).standard_normal(out[name].shape)
        drawn = base * np.exp(spread * noise) if base else spread * noise
        out[name] = jnp.asarray(drawn.astype(out[name].dtype))
    for name, factor in factors.items():
        out[name] = (out[name] * factor).astype(out[name].dtype)
    return out
```

```python
from contextlib import ExitStack

import numpy as np

import concourse.bass as bass
from concourse import mybir

P = 128
T = 5
SLOTS = 5
N, E, F = 12500, 400000, 32
NB = -(-N // P)
NP = NB * P
GROUPS = E // (P * T)
ITERS = GROUPS // SLOTS
COLS = E // P
GC = GROUPS // SLOTS
C2 = 2 * F
assert GROUPS * P * T == E and ITERS * SLOTS == GROUPS

ALU = mybir.AluOpType
ACT = mybir.ActivationFunctionType
F32 = mybir.dt.float32
BF16 = mybir.dt.bfloat16
I32 = mybir.dt.int32
AX = mybir.AxisListType
EPS = 1e-5


ONE, FULL = 1, 16
FROM_ZERO = ("loaded", "x_loaded", "attr_in", "stored", "indexed", "row_in", "pair_in", "a1_in", "emb_in", "weights", "step",
             "gathered", "moved")
RECYCLED = ("a1_out", "rows_out")


class Chain:

    def __init__(self, eng, sem):
        self.eng, self.sem, self.n, self.base = eng, sem, 0, 0

    def __call__(self, ins):
        self.n += 1
        ins.then_inc(self.sem, 1)
        self.eng.wait_ge(self.sem, self.base + self.n)

    def enter(self, i, steps):
        self.before, self.steps = self.n, steps
        self.base, self.n = i * steps + self.before, 0

    def leave(self, turns):
        assert self.n == self.steps, (self.n, self.steps)
        self.base, self.n = 0, self.before + turns * self.steps


def rep(ap, axis, n):
    a = ap.unsqueeze(axis)
    shape = list(a.shape)
    shape[axis] = n
    return a.broadcast_to(shape)


def cut(ap, **sizes):
    return ap.rearrange("p (t w) -> p t w", **sizes)


def reciprocal_root(nc, dve, link, s, turn, root):
    nc.vector.nop().then_inc(s["to_root"], 1)
    dve.wait_ge(s["rooted"], ONE + turn)
    link(nc.vector.reciprocal(root, root))


def roots_act(nc, act, s, turns, root):
    for turn in range(1, turns + 1):
        act.wait_ge(s["to_root"], ONE + turn)
        nc.scalar.activation(root, root, ACT.Sqrt).then_inc(s["rooted"], 1)


def layer_norm(nc, dve, link, s, turn, x, tmp, mean, root):
    link(nc.vector.tensor_reduce(mean, x, AX.X, ALU.add))
    link(nc.vector.tensor_scalar(mean, mean, 1.0 / F, None, ALU.mult))
    link(nc.vector.tensor_tensor(x, x, rep(mean, 2, F), ALU.subtract))
    link(nc.vector.tensor_tensor(tmp, x, x, ALU.mult))
    link(nc.vector.tensor_reduce(root, tmp, AX.X, ALU.add))
    link(nc.vector.tensor_scalar(root, root, 1.0 / F, EPS, ALU.mult, ALU.add))
    reciprocal_root(nc, dve, link, s, turn, root)
    link(nc.vector.tensor_tensor(x, x, rep(root, 2, F), ALU.mult))




def visits_dve(nc, dve, m, s, g, acc, width):
    n = dve.value_load(m["window"][0:1, bass.ds(3 * g, 1)], min_val=1, max_val=NB)
    first = dve.value_load(m["window"][0:1, bass.ds(3 * g + 1, 1)], min_val=0, max_val=NB - 1)
    before = dve.value_load(m["window"][0:1, bass.ds(3 * g + 2, 1)], min_val=0, max_val=GROUPS * NB)
    keys = m["keys"][:, bass.ds(T * g, T)]
    with dve.Fori(0, n) as k:
        at = nc.s_assert_within(first + k, 0, NB - 1, skip_runtime_bounds_check_because="first + n <= NB")
        dve.wait_ge(s["summed"], ONE + before + k)
        nc.vector.tensor_tensor(cut(m["onehot"][:, :], t=T), rep(keys, 2, P),
                                rep(m["iota"][:, bass.ds(at * P, P)], 1, T),
                                ALU.is_equal).then_inc(s["onehot"], 1)
        dve.wait_ge(s["summed"], ONE + before + k + 1)
        block = acc[:, bass.ds(at * width, width)]
        nc.vector.tensor_tensor(block, block, m["ps"][7][:, 0:width], ALU.add).then_inc(s["added"], 1)


def sums_done(dve, m, s):
    last = m["window"][0:1, 3 * GROUPS - 3:3 * GROUPS]
    n = dve.value_load(last[:, 0:1], min_val=1, max_val=NB)
    before = dve.value_load(last[:, 2:3], min_val=0, max_val=GROUPS * NB)
    dve.wait_ge(s["added"], ONE + before + n)


def visits_pe(nc, pe, m, s, g, rows, width):
    n = pe.value_load(m["window"][0:1, bass.ds(3 * g, 1)], min_val=1, max_val=NB)
    before = pe.value_load(m["window"][0:1, bass.ds(3 * g + 2, 1)], min_val=0, max_val=GROUPS * NB)
    with pe.Fori(0, n) as k:
        pe.wait_ge(s["onehot"], ONE + before + k + 1)
        pe.wait_ge(s["added"], ONE + before + k)
        for t in range(T):
            mm = nc.tensor.matmul(m["ps"][7][:, 0:width], m["onehot"][:, t * P:(t + 1) * P], rows[:, t, :],
                                  start=t == 0, stop=t == T - 1)
        mm.then_inc(s["summed"], 1)



def stage_windows(nc, m, of_pairs, s):
    with nc.Block() as block:

        @block.gpsimd
        def _(pool):
            nc.gpsimd.iota(m["iota"][:, :], [[1, NP]], base=0, channel_multiplier=0, allow_small_or_imprecise_dtypes=True)

        @block.vector
        def _(dve):
            link = Chain(dve, s["step"])
            keys_int = m["keys_int"][:, :]
            dve.wait_ge(s["loaded"], 16 * SLOTS if of_pairs else 16)
            if of_pairs:
                link(nc.vector.tensor_copy(keys_int, m["pairs_in"][:, :].rearrange("p (c k) -> p c k", k=2)[:, :, 0]))
            link(nc.vector.tensor_single_scalar(m["ints"][:, :], keys_int, 7, ALU.arith_shift_right))
            link(nc.vector.tensor_copy(m["floats"][:, :], m["ints"][:, :]))
            link(nc.vector.tensor_copy(m["keys"][:, :], keys_int))
            grouped = m["floats"][:, :].rearrange("p (g t) -> p g t", t=T)
            nc.vector.tensor_reduce(m["least"][:, :], grouped, AX.X, ALU.min)
            link(nc.vector.tensor_reduce(m["most"][:, :], grouped, AX.X, ALU.max))
            nc.vector.nop().then_inc(s["extremes"], 1)
            dve.wait_ge(s["turned"], ONE + 1)
            for c in range(SLOTS):
                nc.vector.tensor_reduce(m["win"][0:GC, 3 * c + 1:3 * c + 2], m["ps"][c][0:GC, 0:P], AX.X, ALU.min)
                link(nc.vector.tensor_reduce(m["wide"][0:GC, c:c + 1], m["ps"][c][0:GC, P:2 * P], AX.X, ALU.max))
            firsts = m["win"][0:GC, :].rearrange("q (c w) -> q c w", w=3)[:, :, 1]
            counts = m["win"][0:GC, :].rearrange("q (c w) -> q c w", w=3)[:, :, 0]
            link(nc.vector.tensor_tensor(m["wide"][0:GC, :], m["wide"][0:GC, :], firsts, ALU.subtract))
            link(nc.vector.tensor_scalar(m["wide"][0:GC, :], m["wide"][0:GC, :], 1.0, None, ALU.add))
            link(nc.vector.tensor_copy(counts, m["wide"][0:GC, :]))
            nc.vector.nop().then_inc(s["counted"], 1)
            dve.wait_ge(s["prefixed"], ONE + 1)
            link(nc.vector.tensor_copy(m["wide"][0:GC, :], m["ps"][6][0:GC, 0:SLOTS]))
            for c in range(SLOTS):
                before = m["win"][0:GC, 3 * c + 2:3 * c + 3]
                link(nc.vector.tensor_copy(before, m["ps"][5][0:GC, c:c + 1]))
                for k in range(c):
                    link(nc.vector.tensor_tensor(before, before, m["wide"][0:GC, k:k + 1], ALU.add))
            nc.vector.tensor_copy(m["win_int"][0:GC, :], m["win"][0:GC, :]).then_inc(s["tabled"], 1)

        @block.tensor
        def _(pe):
            pe.wait_ge(s["extremes"], ONE + 1)
            for c in range(SLOTS):
                cols = slice(c * GC, (c + 1) * GC)
                nc.tensor.transpose(m["ps"][c][0:GC, 0:P], m["least"][:, cols], m["ident"][:, :])
                mm = nc.tensor.transpose(m["ps"][c][0:GC, P:2 * P], m["most"][:, cols], m["ident"][:, :])
            mm.then_inc(s["turned"], 1)
            pe.wait_ge(s["counted"], ONE + 1)
            nc.tensor.matmul(m["ps"][5][0:GC, 0:SLOTS], m["before"][0:GC, 0:GC], m["wide"][0:GC, :], start=True, stop=True)
            nc.tensor.matmul(m["ps"][6][0:GC, 0:SLOTS], m["ones"][0:GC, 0:GC], m["wide"][0:GC, :],
                             start=True, stop=True).then_inc(s["prefixed"], 1)

        @block.sync
        def _(sp):
            if of_pairs:
                with sp.Fori(0, SLOTS) as c:
                    sp.dma_start(m["pairs_in"][:, bass.ds(c * GC * 2 * T, GC * 2 * T)].rearrange("p (g k) -> p g k", g=GC),
                                 m["sorted_pairs"].rearrange("(g p t) k -> p g (t k)", p=P, t=T)[:, bass.ds(c * GC, GC), :]
                                 ).then_inc(s["loaded"], 16)
            else:
                sp.dma_start(m["keys_int"][:, :], m["dst"]).then_inc(s["loaded"], 16)
            sp.wait_ge(s["tabled"], ONE + 1)
            sp.dma_start(m["window_dram"].rearrange("(c q) w -> q c w", q=GC),
                         m["win_int"][0:GC, :].rearrange("q (c w) -> q c w", w=3)).then_inc(s["stored"], 16)
            sp.wait_ge(s["stored"], 16)
            sp.dma_start(m["window"][0:1, :], m["window_dram"].rearrange("g w -> (g w)").unsqueeze(0)).then_inc(s["stored"], 16)
            sp.wait_ge(s["stored"], 32)


def stage_setup(nc, m, s):
    with nc.Block() as block:

        @block.sync
        def _(sp):
            sp.dma_start(m["src_int"][:, :], m["src"]).then_inc(s["loaded"], 16)
            sp.dma_start(m["x"][:, :], m["x_in"]).then_inc(s["x_loaded"], 16)
            sp.wait_ge(s["x_loaded"], 16)
            with sp.Fori(0, ITERS) as i:
                for j in range(SLOTS):
                    sp.wait_ge(s["attr_used"][j], ONE + i)
                    sp.dma_start(m["attr"][j][:, :], m["edge_attr"][:, bass.ds((SLOTS * i + j) * T * F, T * F)]
                                 ).then_inc(s["attr_in"][j], 16)

        @block.scalar
        def _(act):
            with act.Fori(0, ITERS) as i:
                for j in range(SLOTS):
                    act.wait_ge(s["attr_in"][j], 16 * (i + 1))
                    act.wait_ge(s["attr_used"][j], ONE + i)
                    nc.scalar.square(m["attr_square"][j][:, :], m["attr"][j][:, :]).then_inc(s["squared"], 1)

        @block.gpsimd
        def _(pool):
            nc.gpsimd.iota(m["iota"][:, :], [[1, NP]], base=0, channel_multiplier=0,
                           allow_small_or_imprecise_dtypes=True).then_inc(s["iota"], 1)
            nc.gpsimd.iota(m["part"][:, :], [[0, 1]], base=0, channel_multiplier=1,
                           allow_small_or_imprecise_dtypes=True).then_inc(s["iota"], 1)

        @block.vector
        def _(dve):
            link = Chain(dve, s["step"])
            nc.vector.memset(m["ones"][:, :], 1.0)
            nc.vector.memset(m["zero_row"][:, :], 0.0)
            nc.vector.memset(m["zeros"][:, :], 0.0).then_inc(s["zero"], 1)
            dve.wait_ge(s["iota"], ONE + 2)
            nc.vector.tensor_copy(m["ramp"][:, :], m["iota"][:, 0:P])
            nc.vector.tensor_scalar(m["ident"][:, :], m["iota"][:, 0:P], m["part"][:, :], None, ALU.is_equal)
            nc.vector.tensor_scalar(m["before"][:, :], m["iota"][:, 0:P], m["part"][:, :], None, ALU.is_gt)
            dve.wait_ge(s["loaded"], 16)
            link(nc.vector.tensor_single_scalar(m["ints"][:, :], m["src_int"][:, :], P - 1, ALU.bitwise_and))
            link(nc.vector.tensor_copy(m["low"][:, :], m["ints"][:, :]))
            link(nc.vector.tensor_single_scalar(m["ints"][:, :], m["src_int"][:, :], 7, ALU.arith_shift_right))
            link(nc.vector.tensor_copy(m["high"][:, :], m["ints"][:, :]))
            with dve.Fori(0, ITERS) as i:
                for j in range(SLOTS):
                    dve.wait_ge(s["counted"][j], ONE + i)
                    cols = bass.ds((SLOTS * i + j) * T, T)
                    nc.vector.tensor_tensor(cut(m["hot_low"][j][:, :], t=T), rep(m["low"][:, cols], 2, P),
                                            rep(m["iota"][:, 0:P], 1, T), ALU.is_equal)
                    nc.vector.tensor_tensor(cut(m["hot_high"][j][:, :], t=T), rep(m["high"][:, cols], 2, NB),
                                            rep(m["iota"][:, 0:NB], 1, T), ALU.is_equal).then_inc(s["hot"], 1)
            dve.wait_ge(s["histogram"], ONE + 1)
            nc.vector.tensor_copy(m["out_deg"][:, :], m["ps"][0][:, 0:NB])
            by_feature = lambda bank: bank[:, 0:T * F].rearrange("p (t f) -> p f t", f=F)
            nc.vector.tensor_reduce(m["attr_sum"][:, 0:F], by_feature(m["ps"][1]), AX.X, ALU.add)
            nc.vector.tensor_reduce(m["attr_sum"][:, F:2 * F], by_feature(m["ps"][2]), AX.X, ALU.add)

        @block.tensor
        def _(pe):
            pe.wait_ge(s["zero"], ONE + 1)
            for k in (1, 2):
                nc.tensor.matmul(m["ps"][k][:, 0:T * F], m["zeros"][:, :], m["zero_row"][:, 0:T * F], start=True, stop=False,
                                 skip_group_check=True)
            nc.tensor.matmul(m["ps"][0][:, 0:NB], m["zeros"][:, :], m["zeros"][:, 0:NB], start=True, stop=False, skip_group_check=True)
            with pe.Fori(0, ITERS) as i:
                for j in range(SLOTS):
                    pe.wait_ge(s["hot"], ONE + SLOTS * i + j + 1)
                    for t in range(T):
                        mm = nc.tensor.matmul(m["ps"][0][:, 0:NB], m["hot_low"][j][:, t * P:(t + 1) * P],
                                              m["hot_high"][j][:, t * NB:(t + 1) * NB],
                                              start=False, stop=False, skip_group_check=True)
                    mm.then_inc(s["counted"][j], 1)
                    pe.wait_ge(s["squared"], ONE + SLOTS * i + j + 1)
                    nc.tensor.matmul(m["ps"][1][:, 0:T * F], m["ones"][:, :], m["attr"][j][:, :],
                                     start=False, stop=False, skip_group_check=True)
                    nc.tensor.matmul(m["ps"][2][:, 0:T * F], m["ones"][:, :], m["attr_square"][j][:, :],
                                     start=False, stop=False, skip_group_check=True).then_inc(s["attr_used"][j], 1)
            nc.tensor.matmul(m["ps"][0][:, 0:NB], m["zeros"][:, :], m["zeros"][:, 0:NB], start=False, stop=True,
                             skip_group_check=True).then_inc(s["histogram"], 1)


def stage_convolve(nc, m, s):
    W = F + 1
    x = m["x"][:, :].rearrange("p (b f) -> p b f", f=F)
    with nc.Block() as block:

        @block.vector
        def _(dve):
            link = Chain(dve, s["step"])
            link(nc.vector.tensor_scalar(m["root"][:, :], m["out_deg"][:, :], 1.0, None, ALU.max))
            reciprocal_root(nc, dve, link, s, 1, m["root"][:, :])
            nc.vector.tensor_tensor(m["tmp"][:, :].rearrange("p (b f) -> p b f", f=F), x, rep(m["root"][:, :], 2, F),
                                    ALU.mult).then_inc(s["scaled"], 1)
            link(nc.vector.memset(m["acc"][:, 0:NB * W], 0.0))
            for j in range(SLOTS):
                nc.vector.memset(m["rows"][j][:, :], 1.0).then_inc(s["cleared"], 1)
            with dve.Fori(0, ITERS) as i:
                for j in range(SLOTS):
                    visits_dve(nc, dve, m, s, SLOTS * i + j, m["acc"], W)
                    nc.vector.nop().then_inc(s["used"][j], 1)
            sums_done(dve, m, s)
            dve.wait_ge(s["stored"], 16)
            acc = m["acc"][:, 0:NB * W].rearrange("p (b w) -> p b w", w=W)
            link(nc.vector.tensor_copy(m["in_deg"][:, :], acc[:, :, F]))
            link(nc.vector.tensor_scalar(m["root"][:, :], m["in_deg"][:, :], 1.0, None, ALU.max))
            reciprocal_root(nc, dve, link, s, 2, m["root"][:, :])
            tmp = m["tmp"][:, :].rearrange("p (b f) -> p b f", f=F)
            link(nc.vector.tensor_tensor(tmp, acc[:, :, 0:F], rep(m["root"][:, :], 2, F), ALU.mult))
            link(nc.vector.tensor_tensor(x, x, tmp, ALU.add))
            layer_norm(nc, dve, link, s, 3, x, tmp, m["mean"][:, :], m["root"][:, :])

        @block.scalar
        def _(act):
            roots_act(nc, act, s, 3, m["root"][:, :])

        @block.tensor
        def _(pe):
            with pe.Fori(0, ITERS) as i:
                for j in range(SLOTS):
                    pe.wait_ge(s["gathered"][j], 16 * T * (i + 1))
                    visits_pe(nc, pe, m, s, SLOTS * i + j, m["rows"][j][:, 0:T * W].rearrange("p (t w) -> p t w", w=W), W)

        @block.sync
        def _(sp):
            sp.wait_ge(s["scaled"], ONE + 1)
            sp.dma_start(m["x_table"].rearrange("(b p) f -> p b f", p=P),
                         m["tmp"][:, :].rearrange("p (b f) -> p b f", f=F)).then_inc(s["stored"], 16)
            with sp.Fori(0, ITERS) as i:
                for j in range(SLOTS):
                    sp.wait_ge(s["used"][j], ONE + i)
                    sp.dma_start(m["index"][j][:, :], m["src"][:, bass.ds((SLOTS * i + j) * T, T)]).then_inc(s["indexed"][j], 16)
            sp.wait_ge(s["stored"], 16)

        @block.gpsimd
        def _(pool):
            pool.wait_ge(s["stored"], 16)
            pool.wait_ge(s["cleared"], ONE + SLOTS)
            with pool.Fori(0, ITERS) as i:
                for j in range(SLOTS):
                    pool.wait_ge(s["indexed"][j], 16 * (i + 1))
                    pool.wait_ge(s["used"][j], ONE + i)
                    pool.sem_inc(s["going"], 1)
                    for t in range(T):
                        nc.gpsimd.indirect_dma_start(
                            out=m["rows"][j][:, t * W:t * W + F], out_offset=None, in_=m["x_table"],
                            in_offset=bass.IndirectOffsetOnAxis(ap=m["index"][j][:, t:t + 1], axis=0),
                        ).then_inc(s["gathered"][j], 16)


def stage_sort(nc, m, s):
    with nc.Block() as block:

        @block.sync
        def _(sp):
            sp.dma_start(m["src_int"][:, :], m["src"]).then_inc(s["loaded"], 16)
            with sp.Fori(0, ITERS) as i:
                for j in range(SLOTS):
                    g = SLOTS * i + j
                    sp.wait_ge(s["compared"][j], ONE + i)
                    sp.dma_start(m["src_row"][j][:, :],
                                 m["src_rows"][bass.ds(g, 1), :].broadcast_to([P, T * P])).then_inc(s["row_in"][j], 16)
                    sp.wait_ge(s["freed"][j], ONE + i)
                    sp.dma_start(m["pair"][j][:, :], m["pairs"][:, bass.ds(g * 2 * T, 2 * T)]).then_inc(s["pair_in"][j], 16)

        @block.vector
        def _(dve):
            link = Chain(dve, s["step"])
            dve.wait_ge(s["loaded"], 16)
            link(nc.vector.tensor_copy(m["src_float"][:, :], m["src_int"][:, :]))
            link(nc.vector.tensor_single_scalar(m["ints"][:, :], m["src_int"][:, :], P - 1, ALU.bitwise_and))
            link(nc.vector.tensor_copy(m["low"][:, :], m["ints"][:, :]))
            link(nc.vector.tensor_single_scalar(m["ints"][:, :], m["src_int"][:, :], 7, ALU.arith_shift_right))
            link(nc.vector.tensor_copy(m["high"][:, :], m["ints"][:, :]))
            link(nc.vector.tensor_copy(m["ident_half"][:, :], m["ident"][:, :]))
            dve.wait_ge(s["sums"], ONE + 1)
            nc.vector.tensor_copy(m["sums"][0:NB, :], m["ps"][1][0:NB, 0:P]).then_inc(s["sums_out"], 1)
            with dve.Fori(0, ITERS) as i:
                for j in range(SLOTS):
                    g = SLOTS * i + j
                    cols = bass.ds(g * T, T)
                    dve.wait_ge(s["placed"][j], ONE + i)
                    nc.vector.tensor_tensor(cut(m["hot_low"][j][:, :], t=T), rep(m["low"][:, cols], 2, P),
                                            rep(m["ramp"][:, 0:P], 1, T), ALU.is_equal).then_inc(s["hot_lows"], 1)
                    nc.vector.tensor_tensor(cut(m["hot_high"][j][:, :], t=T), rep(m["high"][:, cols], 2, NB),
                                            rep(m["ramp"][:, 0:NB], 1, T), ALU.is_equal).then_inc(s["hot_highs"], 1)
                    dve.wait_ge(s["row_in"][j], 16 * (i + 1))
                    for t in range(T):
                        ins = nc.vector.scalar_tensor_tensor(
                            m["same"][j][:, t * P:(t + 1) * P], m["src_row"][j][:, t * P:(t + 1) * P],
                            m["src_float"][:, bass.ds(g * T + t, 1)], m["before"][:, :], ALU.is_equal, ALU.mult)
                    ins.then_inc(s["compared"][j], 1)
                    for t in range(T):
                        dve.wait_ge(s["looked"], ONE + g * T + t + 1)
                        ins = nc.vector.tensor_tensor_reduce(
                            m["picked"][:, t * NB:(t + 1) * NB], m["ps"][2 + t % 2][:, 0:NB], m["hot_high"][j][:, t * NB:(t + 1) * NB], 1.0, 0.0,
                            ALU.mult, ALU.add, m["place"][j][:, t:t + 1])
                        ins.then_inc(s["picked"], 1)
                    dve.wait_ge(s["picked"], ONE + (g + 1) * T)
                    dve.wait_ge(s["freed"][j], ONE + i)
                    nc.vector.tensor_copy(m["place_int"][j][:, :], m["place"][j][:, :]).then_inc(s["placed"][j], 1)

        @block.scalar
        def _(act):
            act.wait_ge(s["begun"], ONE + 1)
            nc.scalar.copy(m["counts"][:, :], m["ps"][0][:, 0:NB]).then_inc(s["counts_out"], 1)
            with act.Fori(0, ITERS) as i:
                for j in range(SLOTS):
                    act.wait_ge(s["turned"], ONE + SLOTS * i + j + 1)
                    nc.scalar.copy(m["turned"][:, :], m["ps_turn"][:, 0:T * P]).then_inc(s["turned_out"], 1)
                    for t in range(T):
                        act.wait_ge(s["counted"], ONE + (SLOTS * i + j) * T + t + 1)
                        nc.scalar.copy(m["counts"][:, :], m["ps"][0][:, 0:NB]).then_inc(s["counts_out"], 1)

        @block.tensor
        def _(pe):
            nc.tensor.matmul(m["ps"][1][0:NB, 0:P], m["out_deg"][:, :], m["ones"][:, :], start=True, stop=True).then_inc(s["sums"], 1)
            nc.tensor.matmul(m["ps"][0][:, 0:NB], m["before"][:, :], m["out_deg"][:, :], start=True, stop=False, skip_group_check=True)
            pe.wait_ge(s["sums_out"], ONE + 1)
            nc.tensor.matmul(m["ps"][0][:, 0:NB], m["sums"][0:NB, :], m["before"][0:NB, 0:NB], start=False, stop=False,
                             skip_group_check=True).then_inc(s["begun"], 1)
            with pe.Fori(0, ITERS) as i:
                for j in range(SLOTS):
                    g = SLOTS * i + j
                    pe.wait_ge(s["hot_lows"], ONE + g + 1)
                    pe.wait_ge(s["turned_out"], ONE + g)
                    for t in range(T):
                        mm = nc.tensor.transpose(m["ps_turn"][:, t * P:(t + 1) * P], m["hot_low"][j][:, t * P:(t + 1) * P],
                                                 m["ident_half"][:, :])
                    mm.then_inc(s["turned"], 1)
                    pe.wait_ge(s["hot_highs"], ONE + g + 1)
                    pe.wait_ge(s["compared"][j], ONE + i + 1)
                    pe.wait_ge(s["turned_out"], ONE + g + 1)
                    for t in range(T):
                        look, tile = m["ps"][2 + t % 2][:, 0:NB], slice(t * P, (t + 1) * P)
                        high = m["hot_high"][j][:, t * NB:(t + 1) * NB]
                        pe.wait_ge(s["picked"], ONE + g * T + max(t - 1, 0))
                        nc.tensor.matmul(look, m["same"][j][:, tile], high, start=True, stop=False)
                        pe.wait_ge(s["counts_out"], ONE + g * T + t + 1)
                        nc.tensor.matmul(look, m["turned"][:, tile], m["counts"][:, :], start=False, stop=True).then_inc(s["looked"], 1)
                        nc.tensor.matmul(m["ps"][0][:, 0:NB], m["hot_low"][j][:, tile], high, start=False, stop=False,
                                         skip_group_check=True).then_inc(s["counted"], 1)

        @block.gpsimd
        def _(pool):
            with pool.Fori(0, ITERS) as i:
                for j in range(SLOTS):
                    pool.wait_ge(s["placed"][j], ONE + i + 1)
                    pool.wait_ge(s["pair_in"][j], 16 * (i + 1))
                    pool.sem_inc(s["going"], 1)
                    for t in range(T):
                        nc.gpsimd.indirect_dma_start(
                            out=m["sorted_pairs"], out_offset=bass.IndirectOffsetOnAxis(ap=m["place_int"][j][:, t:t + 1], axis=0),
                            in_=m["pair"][j][:, 2 * t:2 * t + 2], in_offset=None,
                        ).then_inc(s["moved"][j], 16)
                    for slot in ([j - 1] if j else []) + ([j] if j == SLOTS - 1 else []):
                        pool.wait_ge(s["moved"][slot], 16 * T * (i + 1))
                        pool.sem_inc(s["freed"][slot], 1)


H = 64
W96 = F + H
CHUNK = 500
NCHUNKS = N // CHUNK
SLOPE = 0.1


def norm_columns(nc, dve, link, s, turn, c, count, gain, shift_in, d):
    mean, var, scale, shift = (c[0:d, k:k + 1] for k in range(4))
    if count:
        link(nc.vector.tensor_scalar(c[0:d, 0:2], c[0:d, 0:2], 1.0 / count, None, ALU.mult))
        link(nc.vector.tensor_tensor(scale, mean, mean, ALU.mult))
        link(nc.vector.tensor_tensor(var, var, scale, ALU.subtract))
        link(nc.vector.tensor_scalar(var, var, 0.0, None, ALU.max))
    link(nc.vector.tensor_scalar(var, var, EPS, None, ALU.add))
    reciprocal_root(nc, dve, link, s, turn, var)
    link(nc.vector.tensor_tensor(scale, gain, var, ALU.mult))
    link(nc.vector.tensor_tensor(var, mean, scale, ALU.mult))
    link(nc.vector.tensor_tensor(shift, shift_in, var, ALU.subtract))


def stage_edges_first(nc, m, s):
    x = m["x"][:, :].rearrange("p (b f) -> p b f", f=F)
    tmp = m["tmp"][:, :].rearrange("p (b f) -> p b f", f=F)
    with nc.Block() as block:

        @block.sync
        def _(sp):
            sp.dma_start(m["x_table"].rearrange("(b p) f -> p b f", p=P), x).then_inc(s["stored"], 16)
            for k, name in enumerate(("m1_w1", "m1_c1", "m1_g1", "m1_b1")):
                sp.dma_start(m["sb_" + name][:, :], m[name]).then_inc(s["weights"], 16)
            with sp.Fori(0, ITERS) as i:
                for j in range(SLOTS):
                    g = SLOTS * i + j
                    sp.wait_ge(s["turned"][j], ONE + i)
                    sp.dma_start(m["index"][j][:, :], m["src"][:, bass.ds(g * T, T)]).then_inc(s["indexed"][j], 16)
                    sp.dma_start(cut(m["rows"][j][:, :], t=T)[:, :, F:C2],
                                 cut(m["edge_attr"][:, bass.ds(g * T * F, T * F)], t=T)).then_inc(s["attr_in"][j], 16)
            sp.wait_ge(s["stored"], 16)

        @block.gpsimd
        def _(pool):
            pool.wait_ge(s["stored"], 16)
            with pool.Fori(0, ITERS) as i:
                for j in range(SLOTS):
                    pool.wait_ge(s["indexed"][j], 16 * (i + 1))
                    pool.wait_ge(s["turned"][j], ONE + i)
                    pool.sem_inc(s["going"], 1)
                    for t in range(T):
                        nc.gpsimd.indirect_dma_start(
                            out=m["rows"][j][:, t * C2:t * C2 + F], out_offset=None, in_=m["x_table"],
                            in_offset=bass.IndirectOffsetOnAxis(ap=m["index"][j][:, t:t + 1], axis=0),
                        ).then_inc(s["gathered"][j], 16)

        @block.vector
        def _(dve):
            link = Chain(dve, s["step"])
            link(nc.vector.tensor_tensor(tmp, x, rep(m["out_deg"][:, :], 2, F), ALU.mult))
            link(nc.vector.tensor_reduce(m["sums"][:, 0:F], m["tmp"][:, :].rearrange("p (b f) -> p f b", f=F), AX.X, ALU.add))
            link(nc.vector.tensor_tensor(tmp, tmp, x, ALU.mult))
            nc.vector.tensor_reduce(m["sums"][:, F:C2], m["tmp"][:, :].rearrange("p (b f) -> p f b", f=F), AX.X,
                                    ALU.add).then_inc(s["node_sums"], 1)
            dve.wait_ge(s["totals"], ONE + 1)
            for k in range(2):
                row = m["total_row"][0:1, k * C2:(k + 1) * C2]
                nc.vector.tensor_copy(row[:, 0:F], m["ps"][0][0:1, k * F:(k + 1) * F])
                ins = nc.vector.tensor_copy(row[:, F:C2], m["attr_sum"][0:1, k * F:(k + 1) * F])
            ins.then_inc(s["rowed"], 1)
            dve.wait_ge(s["columns"], ONE + 1)
            link(nc.vector.tensor_copy(m["bn"][0:C2, 0:2], m["ps"][0][0:C2, 0:2]))
            dve.wait_ge(s["weights"], 64)
            norm_columns(nc, dve, link, s, 1, m["bn"], E, m["sb_m1_g1"][:, :], m["sb_m1_b1"][:, :], C2)
            nc.vector.tensor_scalar(m["w"][0:C2, 0:H], m["sb_m1_w1"][:, :], m["bn"][0:C2, 2:3], None, ALU.mult).then_inc(s["folded"], 1)
            dve.wait_ge(s["shifted"], ONE + 1)
            nc.vector.tensor_tensor(m["bias"][0:H, :], m["sb_m1_c1"][:, :], m["ps"][0][0:H, 0:1], ALU.add).then_inc(s["biased"], 1)
            with dve.Fori(0, ITERS) as i:
                for j in range(SLOTS):
                    g = SLOTS * i + j
                    dve.wait_ge(s["turned"][j], ONE + i + 1)
                    dve.wait_ge(s["multiplied"], ONE + g)
                    nc.vector.tensor_copy(m["flipped"][:, 0:512], m["ps"][0][0:C2, :])
                    nc.vector.tensor_copy(m["flipped"][:, 512:], m["ps"][1][0:C2, 0:P]).then_inc(s["flipped"], 1)
                    dve.wait_ge(s["lifted"], ONE + g + 1)
                    dve.wait_ge(s["a1_out"][j], FULL + 16 * i)
                    a1 = m["a1"][j]
                    nc.vector.scalar_tensor_tensor(a1[:, :], m["lift"][j % 2][:, :], SLOPE, m["lift"][j % 2][:, :],
                                                   ALU.mult, ALU.max).then_inc(s["a1_made"], 1)
                    dve.wait_ge(s["a1_made"], ONE + g + 1)
                    nc.vector.bn_stats(m["stats"][:, bass.ds(g * 12, 6)], a1[:, 0:512])
                    nc.vector.bn_stats(m["stats"][:, bass.ds(g * 12 + 6, 6)], a1[:, 512:]).then_inc(s["counted"], 1)
            dve.wait_ge(s["counted"], ONE + GROUPS)
            nc.vector.bn_aggr(m["a1_stats"][0:H, 0:2], m["stats"][:, :])

        @block.scalar
        def _(act):
            roots_act(nc, act, s, 1, m["bn"][0:C2, 1:2])
            act.wait_ge(s["biased"], ONE + 1)
            with act.Fori(0, ITERS) as i:
                for j in range(SLOTS):
                    g = SLOTS * i + j
                    act.wait_ge(s["multiplied"], ONE + g + 1)
                    act.wait_ge(s["a1_made"], ONE + (g if j == 0 else SLOTS * i + j - 1))
                    nc.scalar.activation(m["lift"][j % 2][:, 0:512], m["ps"][2][0:H, :], ACT.Identity, bias=m["bias"][0:H, :])
                    nc.scalar.activation(m["lift"][j % 2][:, 512:], m["ps"][3][0:H, 0:P], ACT.Identity,
                                         bias=m["bias"][0:H, :]).then_inc(s["lifted"], 1)
                    act.wait_ge(s["a1_made"], ONE + g + 1)
                    act.dma_start(m["a1_dram"][bass.ds(g, 1)].rearrange("g h e -> (g h) e"), m["a1"][j][:, :]).then_inc(s["a1_out"][j], 16)
            for j in range(SLOTS):
                act.wait_ge(s["a1_out"][j], FULL + 16 * ITERS)

        @block.tensor
        def _(pe):
            pe.wait_ge(s["node_sums"], ONE + 1)
            nc.tensor.matmul(m["ps"][0][:, 0:C2], m["ones"][:, :], m["sums"][:, :], start=True, stop=True).then_inc(s["totals"], 1)
            pe.wait_ge(s["rowed"], ONE + 1)
            for k in range(2):
                mm = nc.tensor.matmul(m["ps"][0][0:C2, k:k + 1], m["total_row"][0:1, k * C2:(k + 1) * C2], m["ones"][0:1, 0:1],
                                      start=True, stop=True)
            mm.then_inc(s["columns"], 1)
            pe.wait_ge(s["folded"], ONE + 1)
            nc.tensor.matmul(m["ps"][0][0:H, 0:1], m["sb_m1_w1"][:, :], m["bn"][0:C2, 3:4], start=True, stop=True).then_inc(s["shifted"], 1)
            pe.wait_ge(s["biased"], ONE + 1)
            with pe.Fori(0, ITERS) as i:
                for j in range(SLOTS):
                    g = SLOTS * i + j
                    pe.wait_ge(s["gathered"][j], 16 * T * (i + 1))
                    pe.wait_ge(s["attr_in"][j], 16 * (i + 1))
                    pe.wait_ge(s["flipped"], ONE + g)
                    pe.sem_inc(s["going"], 1)
                    for t in range(T):
                        to = m["ps"][t // 4][0:C2, (t % 4) * P:(t % 4 + 1) * P]
                        mm = nc.tensor.transpose(to, m["rows"][j][:, t * C2:(t + 1) * C2], m["ident"][:, :])
                    mm.then_inc(s["turned"][j], 1)
                    pe.wait_ge(s["flipped"], ONE + g + 1)
                    pe.wait_ge(s["lifted"], ONE + g)
                    pe.sem_inc(s["going"], 1)
                    nc.tensor.matmul(m["ps"][2][0:H, :], m["w"][0:C2, 0:H], m["flipped"][:, 0:512], start=True, stop=True)
                    nc.tensor.matmul(m["ps"][3][0:H, 0:P], m["w"][0:C2, 0:H], m["flipped"][:, 512:],
                                     start=True, stop=True).then_inc(s["multiplied"], 1)


def stage_edges_second(nc, m, s):
    W = H + 1
    with nc.Block() as block:

        @block.sync
        def _(sp):
            for name in ("m1_w2", "m1_g2", "m1_b2"):
                sp.dma_start(m["sb_" + name][:, :], m[name]).then_inc(s["weights"], 16)
            sp.dma_start(m["sb_m1_c2"][:, :], m["m1_c2"].broadcast_to([P, H])).then_inc(s["weights"], 16)
            with sp.Fori(0, ITERS) as i:
                for j in range(SLOTS):
                    sp.wait_ge(s["products"][j], ONE + i)
                    sp.dma_start(m["a1"][j][:, :], m["a1_dram"][bass.ds(SLOTS * i + j, 1)].rearrange("g h e -> (g h) e")
                                 ).then_inc(s["a1_in"][j], 16)

        @block.scalar
        def _(act):
            roots_act(nc, act, s, 1, m["a1_stats"][0:H, 1:2])
            with act.Fori(0, ITERS) as i:
                for j in range(SLOTS):
                    act.wait_ge(s["a2_made"], ONE + SLOTS * i + j + 1)
                    act.wait_ge(s["squares_used"], ONE + SLOTS * i + j)
                    nc.scalar.square(cut(m["squares"][:, :], t=T), cut(m["rows"][j][:, 0:T * W], t=T)[:, :, 0:H]).then_inc(s["squared"], 1)

        @block.vector
        def _(dve):
            link = Chain(dve, s["step"])
            link(nc.vector.memset(m["acc"][:, 0:NB * W], 0.0))
            for j in range(SLOTS):
                link(nc.vector.memset(m["rows"][j][:, 0:T * W], 1.0))
            dve.wait_ge(s["weights"], 64)
            norm_columns(nc, dve, link, s, 1, m["a1_stats"], None, m["sb_m1_g2"][:, :], m["sb_m1_b2"][:, :], H)
            link(nc.vector.tensor_scalar(m["w"][0:H, 0:H], m["sb_m1_w2"][:, :], m["a1_stats"][0:H, 2:3], None, ALU.mult))
            nc.vector.tensor_copy(m["wide_shift"][0:H, :], m["a1_stats"][0:H, 3:4].broadcast_to([H, P])).then_inc(s["folded"], 1)
            dve.wait_ge(s["shifted"], ONE + 1)
            link(nc.vector.tensor_tensor(m["bias_row"][:, :], m["sb_m1_c2"][:, :], m["ps"][0][:, 0:H], ALU.add))
            nc.vector.nop().then_inc(s["biased"], 1)
            with dve.Fori(0, ITERS) as i:
                for j in range(SLOTS):
                    g = SLOTS * i + j
                    dve.wait_ge(s["products"][j], ONE + i + 1)
                    dve.wait_ge(s["squared"], ONE + g)
                    nc.vector.tensor_tensor(cut(m["lift2"][:, :], t=T), cut(m["ps"][j % 2][:, 0:T * H], t=T),
                                            rep(m["bias_row"][:, :], 1, T), ALU.add).then_inc(s["lifted"], 1)
                    dve.wait_ge(s["lifted"], ONE + g + 1)
                    lift = cut(m["lift2"][:, :], t=T)
                    nc.vector.scalar_tensor_tensor(cut(m["rows"][j][:, 0:T * W], t=T)[:, :, 0:H], lift, SLOPE, lift,
                                                   ALU.mult, ALU.max).then_inc(s["a2_made"], 1)
                    visits_dve(nc, dve, m, s, g, m["acc"], W)
            sums_done(dve, m, s)
            dve.wait_ge(s["squares_used"], ONE + GROUPS)
            nc.vector.tensor_copy(m["square_sum"][0:H, :], m["ps"][2][0:H, 0:1])

        @block.tensor
        def _(pe):
            pe.wait_ge(s["folded"], ONE + 1)
            nc.tensor.matmul(m["ps"][0][:, 0:H], m["wide_shift"][0:H, :], m["sb_m1_w2"][:, :], start=True, stop=True).then_inc(s["shifted"], 1)
            nc.tensor.matmul(m["ps"][2][0:H, 0:1], m["zeros"][:, 0:H], m["zero_row"][:, 0:1], start=True, stop=False, skip_group_check=True)
            pe.wait_ge(s["biased"], ONE + 1)
            with pe.Fori(0, ITERS) as i:
                for j in range(SLOTS):
                    g = SLOTS * i + j
                    pe.wait_ge(s["a1_in"][j], 16 * (i + 1))
                    pe.wait_ge(s["lifted"], ONE + (g if j == 0 else SLOTS * i + j - 1))
                    for t in range(T):
                        mm = nc.tensor.matmul(m["ps"][j % 2][:, t * H:(t + 1) * H], m["a1"][j][:, t * P:(t + 1) * P],
                                              m["w"][0:H, 0:H], start=True, stop=True)
                    mm.then_inc(s["products"][j], 1)
                    pe.wait_ge(s["squared"], ONE + g + 1)
                    for t in range(T):
                        mm = nc.tensor.matmul(m["ps"][2][0:H, 0:1], m["squares"][:, t * H:(t + 1) * H], m["ones"][:, 0:1],
                                              start=False, stop=False, skip_group_check=True)
                    mm.then_inc(s["squares_used"], 1)
                    visits_pe(nc, pe, m, s, g, cut(m["rows"][j][:, 0:T * W], t=T), W)


SLAB = 7
SLABS = NB // SLAB
assert SLABS * SLAB == NB and NCHUNKS * CHUNK == N


def stage_nodes(nc, m, s):
    W = H + 1
    SW = SLAB * P
    with nc.Block() as block:

        @block.sync
        def _(sp):
            for name in m["node_weights"]:
                sp.dma_start(m["sb_" + name][:, :], m[name]).then_inc(s["weights"], 16)
            sp.wait_ge(s["cleared"], ONE + 1)
            sp.dma_start(m["c3_row"][H:H + 1, :], m["m1_c3"]).then_inc(s["weights"], 16)

        @block.scalar
        def _(act):
            roots_act(nc, act, s, 1, m["bn3"][0:H, 1:2])
            with act.Fori(0, SLABS) as i:
                act.wait_ge(s["turned"], ONE + i)
                nc.scalar.copy(m["acc_slab"][:, :], m["acc"][:, bass.ds(i * SLAB * W, SLAB * W)])
                nc.scalar.copy(m["x_slab"][:, :], m["x"][:, bass.ds(i * SLAB * F, SLAB * F)]).then_inc(s["slab"], 1)
            roots = [m["bn_agg"][0:H, 1:2], m["bn_x"][0:F, 1:2], m["bn_h"][0:W96, 1:2], m["bn_h"][0:W96, 1:2]]
            for layer in range(3):
                for turn in ((2, 3), (4,), (5,))[layer]:
                    act.wait_ge(s["to_root"], ONE + turn)
                    nc.scalar.activation(roots[turn - 2], roots[turn - 2], ACT.Sqrt).then_inc(s["rooted"], 1)
                act.wait_ge(s["biased"], ONE + layer + 1)
                with act.Fori(0, NCHUNKS) as c:
                    act.wait_ge(s["product"], ONE + layer * NCHUNKS + c + 1)
                    if layer < 2:
                        act.wait_ge(s["bent"], ONE + layer * NCHUNKS + c)
                        nc.scalar.activation(m["node_lift"][:, :], m["ps"][0][0:W96, 0:CHUNK], ACT.Identity,
                                             bias=m["bias96"][0:W96, :]).then_inc(s["lifted"], 1)
                    else:
                        nc.scalar.activation(m["x_turned"][:, bass.ds(c * CHUNK, CHUNK)], m["ps"][0][0:F, 0:CHUNK],
                                             ACT.Identity, bias=m["bias96"][0:F, :]).then_inc(s["lifted"], 1)
            act.wait_ge(s["lifted"], ONE + 3 * NCHUNKS)
            with act.Fori(0, SLABS) as i:
                act.wait_ge(s["turned_back"], ONE + i)
                nc.scalar.copy(m["out_slab"][:, :], m["x_turned"][:, bass.ds(i * SW, SW)]).then_inc(s["slab"], 1)
            act.wait_ge(s["to_root"], ONE + 6)
            nc.scalar.activation(m["root"][:, :], m["root"][:, :], ACT.Sqrt).then_inc(s["rooted"], 1)

        @block.vector
        def _(dve):
            link = Chain(dve, s["step"])
            nc.vector.memset(m["c3_row"][:, :], 0.0).then_inc(s["cleared"], 1)
            nc.vector.tensor_reduce(m["sums"][:, 0:H], m["acc"][:, :].rearrange("p (b w) -> p w b", w=W)[:, 0:H, :], AX.X,
                                    ALU.add).then_inc(s["summed"], 1)
            dve.wait_ge(s["totals"], ONE + 1)
            link(nc.vector.tensor_copy(m["bn3"][0:H, 0:1], m["ps"][0][0:H, 0:1]))
            link(nc.vector.tensor_copy(m["bn3"][0:H, 1:2], m["square_sum"][0:H, :]))
            dve.wait_ge(s["weights"], 16 * (len(m["node_weights"]) + 1))
            norm_columns(nc, dve, link, s, 1, m["bn3"], E, m["sb_m1_g3"][:, :], m["sb_m1_b3"][:, :], H)
            link(nc.vector.tensor_scalar(m["fold3"][:, 0:H], m["ident"][0:H, 0:H], m["bn3"][0:H, 2:3], None, ALU.mult))
            link(nc.vector.tensor_copy(m["fold3"][:, H:W], m["bn3"][0:H, 3:4]))
            nc.vector.nop().then_inc(s["folded"], 1)
            dve.wait_ge(s["w3_made"], ONE + 1)
            nc.vector.tensor_tensor(m["w3"][0:W, :], m["ps"][0][0:W, 0:H], m["c3_row"][0:W, :], ALU.add).then_inc(s["w3_out"], 1)
            with dve.Fori(0, SLABS) as i:
                dve.wait_ge(s["turned"], ONE + i + 1)
                dve.wait_ge(s["agged"], ONE + i)
                nc.vector.tensor_copy(m["acc_turned"][0:W, 0:512], m["ps"][0][0:W, :])
                nc.vector.tensor_copy(m["acc_turned"][0:W, 512:], m["ps"][1][0:W, 0:SW - 512])
                nc.vector.tensor_copy(m["x_turned"][:, bass.ds(i * SW, 512)], m["ps"][2][0:F, :])
                nc.vector.tensor_copy(m["x_turned"][:, bass.ds(i * SW + 512, SW - 512)], m["ps"][3][0:F, 0:SW - 512]
                                      ).then_inc(s["flipped"], 1)
                dve.wait_ge(s["agged"], ONE + i + 1)
                nc.vector.tensor_copy(m["h"][0:H, bass.ds(i * SW, 512)], m["ps"][4][0:H, :])
                nc.vector.tensor_copy(m["h"][0:H, bass.ds(i * SW + 512, SW - 512)], m["ps"][5][0:H, 0:SW - 512]
                                      ).then_inc(s["agg_out"], 1)
            dve.wait_ge(s["agg_out"], ONE + SLABS)
            with dve.Fori(0, NCHUNKS) as c:
                nc.vector.bn_stats(m["stats"][0:H, bass.ds(c * 6, 6)], m["h"][0:H, bass.ds(c * CHUNK, CHUNK)])
                nc.vector.bn_stats(m["stats_x"][0:F, bass.ds(c * 6, 6)], m["x_turned"][:, bass.ds(c * CHUNK, CHUNK)]
                                   ).then_inc(s["measured"], 1)
            dve.wait_ge(s["measured"], ONE + NCHUNKS)
            link(nc.vector.bn_aggr(m["bn_agg"][0:H, 0:2], m["stats"][0:H, :]))
            link(nc.vector.bn_aggr(m["bn_x"][0:F, 0:2], m["stats_x"][0:F, :]))
            norm_columns(nc, dve, link, s, 2, m["bn_agg"], None, m["sb_m2_g1a"][:, :], m["sb_m2_b1a"][:, :], H)
            norm_columns(nc, dve, link, s, 3, m["bn_x"], None, m["sb_m2_g1x"][:, :], m["sb_m2_b1x"][:, :], F)
            link(nc.vector.tensor_scalar(m["wa"][:, :], m["sb_m2_w1a"][:, :], m["bn_agg"][0:H, 2:3], None, ALU.mult))
            link(nc.vector.tensor_scalar(m["wx"][:, :], m["sb_m2_w1x"][:, :], m["bn_x"][0:F, 2:3], None, ALU.mult))
            nc.vector.nop().then_inc(s["folded"], 1)
            for layer in range(3):
                wide = W96 if layer < 2 else F
                dve.wait_ge(s["shifted"], ONE + layer + 1)
                c_in = (m["sb_m2_c1"], m["sb_m2_c2"], m["sb_m2_c3"])[layer]
                nc.vector.tensor_tensor(m["bias96"][0:wide, :], m["ps"][6][0:wide, 0:1], c_in[:, :], ALU.add).then_inc(s["biased"], 1)
                if layer == 2:
                    break
                with dve.Fori(0, NCHUNKS) as c:
                    n = layer * NCHUNKS + c
                    dve.wait_ge(s["lifted"], ONE + n + 1)
                    here = m["h"][:, bass.ds(c * CHUNK, CHUNK)]
                    nc.vector.scalar_tensor_tensor(here, m["node_lift"][:, :], SLOPE, m["node_lift"][:, :], ALU.mult,
                                                   ALU.max).then_inc(s["bent"], 1)
                    dve.wait_ge(s["bent"], ONE + n + 1)
                    nc.vector.bn_stats(m["stats"][0:W96, bass.ds(c * 6, 6)], here).then_inc(s["measured"], 1)
                dve.wait_ge(s["measured"], ONE + (layer + 2) * NCHUNKS)
                link(nc.vector.bn_aggr(m["bn_h"][0:W96, 0:2], m["stats"][0:W96, :]))
                gain, shift, w = ((m["sb_m2_g2"], m["sb_m2_b2"], m["sb_m2_w2"]), (m["sb_m2_g3"], m["sb_m2_b3"], m["sb_m2_w3"]))[layer]
                norm_columns(nc, dve, link, s, 4 + layer, m["bn_h"], None, gain[:, :], shift[:, :], W96)
                link(nc.vector.tensor_scalar(m["wh"][:, 0:w.shape[1]], w[:, :], m["bn_h"][0:W96, 2:3], None, ALU.mult))
                nc.vector.nop().then_inc(s["folded"], 1)
            with dve.Fori(0, SLABS) as i:
                dve.wait_ge(s["turned_back"], ONE + i + 1)
                here = m["x"][:, bass.ds(i * SLAB * F, SLAB * F)]
                nc.vector.tensor_tensor(here, here, m["ps"][1][:, 0:SLAB * F], ALU.add).then_inc(s["added"], 1)
            dve.wait_ge(s["added"], ONE + SLABS)
            cubed = lambda t: t[:, :].rearrange("p (b f) -> p b f", f=F)
            layer_norm(nc, dve, link, s, 6, cubed(m["x"]), cubed(m["tmp"]), m["mean"][:, :], m["root"][:, :])

        @block.tensor
        def _(pe):
            pe.wait_ge(s["summed"], ONE + 1)
            nc.tensor.matmul(m["ps"][0][0:H, 0:1], m["sums"][:, 0:H], m["ones"][:, 0:1], start=True, stop=True).then_inc(s["totals"], 1)
            pe.wait_ge(s["folded"], ONE + 1)
            nc.tensor.matmul(m["ps"][0][0:W, 0:H], m["fold3"][:, :], m["sb_m1_w3"][:, :], start=True, stop=True).then_inc(s["w3_made"], 1)
            pe.wait_ge(s["w3_out"], ONE + 1)
            with pe.Fori(0, SLABS) as i:
                pe.wait_ge(s["slab"], ONE + i + 1)
                pe.wait_ge(s["flipped"], ONE + i)
                pe.sem_inc(s["going"], 1)
                for b in range(SLAB):
                    cols = slice(b % 4 * P, (b % 4 + 1) * P)
                    nc.tensor.transpose(m["ps"][b // 4][0:W, cols], m["acc_slab"][:, b * W:(b + 1) * W], m["ident"][:, :])
                    mm = nc.tensor.transpose(m["ps"][2 + b // 4][0:F, cols], m["x_slab"][:, b * F:(b + 1) * F], m["ident"][:, :])
                mm.then_inc(s["turned"], 1)
                pe.wait_ge(s["flipped"], ONE + i + 1)
                pe.wait_ge(s["agg_out"], ONE + i)
                pe.sem_inc(s["going"], 1)
                nc.tensor.matmul(m["ps"][4][0:H, :], m["w3"][0:W, :], m["acc_turned"][0:W, 0:512], start=True, stop=True)
                nc.tensor.matmul(m["ps"][5][0:H, 0:SW - 512], m["w3"][0:W, :], m["acc_turned"][0:W, 512:],
                                 start=True, stop=True).then_inc(s["agged"], 1)
            for layer in range(3):
                wide = W96 if layer < 2 else F
                pe.wait_ge(s["folded"], ONE + layer + 2)
                if layer == 0:
                    nc.tensor.matmul(m["ps"][6][0:wide, 0:1], m["sb_m2_w1a"][:, :], m["bn_agg"][0:H, 3:4], start=True, stop=False)
                    mm = nc.tensor.matmul(m["ps"][6][0:wide, 0:1], m["sb_m2_w1x"][:, :], m["bn_x"][0:F, 3:4], start=False, stop=True)
                else:
                    w = (m["sb_m2_w2"], m["sb_m2_w3"])[layer - 1]
                    mm = nc.tensor.matmul(m["ps"][6][0:wide, 0:1], w[:, :], m["bn_h"][0:W96, 3:4], start=True, stop=True)
                mm.then_inc(s["shifted"], 1)
                with pe.Fori(0, NCHUNKS) as c:
                    cols = bass.ds(c * CHUNK, CHUNK)
                    pe.wait_ge(s["lifted"], ONE + layer * NCHUNKS + c)
                    pe.sem_inc(s["going"], 1)
                    to = m["ps"][0][0:wide, 0:CHUNK]
                    if layer == 0:
                        nc.tensor.matmul(to, m["wa"][:, :], m["h"][0:H, cols], start=True, stop=False)
                        mm = nc.tensor.matmul(to, m["wx"][:, :], m["x_turned"][:, cols], start=False, stop=True)
                    else:
                        mm = nc.tensor.matmul(to, m["wh"][:, 0:wide], m["h"][:, cols], start=True, stop=True)
                    mm.then_inc(s["product"], 1)
            with pe.Fori(0, SLABS) as i:
                pe.wait_ge(s["slab"], ONE + SLABS + i + 1)
                pe.wait_ge(s["added"], ONE + i)
                pe.sem_inc(s["going"], 1)
                for b in range(SLAB):
                    mm = nc.tensor.transpose(m["ps"][1][:, b * F:(b + 1) * F], m["out_slab"][:, b * P:(b + 1) * P], m["ident"][0:F, 0:F])
                mm.then_inc(s["turned_back"], 1)


HEADS = 4
XA = F + HEADS
ATT_SLOPE = 0.2
BIG = 1e30


def stage_attention_tables(nc, m, s):
    with nc.Block() as block:

        @block.sync
        def _(sp):
            sp.dma_start(m["sb_w_out"][:, :], m["att_w_out"]).then_inc(s["weights"], 16)
            sp.dma_start(m["sb_fc"][:, :], m["att_fc"]).then_inc(s["weights"], 16)
            sp.dma_start(m["sb_fc_b"][:, :], m["att_fc_b"].broadcast_to([P, 1])).then_inc(s["weights"], 16)
            sp.wait_ge(s["built"], ONE + 2)
            sp.dma_start(m["xa_table"].rearrange("(b p) f -> p b f", p=P), m["xa"][:, :].rearrange("p (b f) -> p b f", f=XA)).then_inc(s["stored"], 16)
            sp.dma_start(m["u_table"].rearrange("(b p) f -> p b f", p=P), m["u"][:, :].rearrange("p (b f) -> p b f", f=HEADS)).then_inc(s["stored"], 16)
            sp.wait_ge(s["stored"], 32)

        @block.tensor
        def _(pe):
            pe.wait_ge(s["weights"], 48)
            for h in range(HEADS):
                mm = nc.tensor.matmul(m["ps"][0][0:F, 2 * h:2 * h + 2], m["sb_w_out"][:, h * F:(h + 1) * F], m["sb_fc"][:, :],
                                      start=True, stop=True)
            mm.then_inc(s["vectors"], 1)
            pe.wait_ge(s["vectors_out"], ONE + 1)
            with pe.Fori(0, SLABS) as i:
                pe.wait_ge(s["slab"], ONE + i + 1)
                pe.wait_ge(s["flipped"], ONE + i)
                pe.sem_inc(s["going"], 1)
                for b in range(SLAB):
                    mm = nc.tensor.transpose(m["ps"][2 + b // 4][0:F, b % 4 * P:(b % 4 + 1) * P],
                                             m["x_slab"][:, b * F:(b + 1) * F], m["ident"][:, :])
                mm.then_inc(s["turned"], 1)
                pe.wait_ge(s["flipped"], ONE + i + 1)
                pe.wait_ge(s["logits_out"], ONE + i)
                pe.sem_inc(s["going"], 1)
                for b in range(SLAB):
                    mm = nc.tensor.matmul(m["ps"][1][:, b * 8:(b + 1) * 8], m["x_turned_slab"][:, b * P:(b + 1) * P], m["vectors"][:, :],
                                          start=True, stop=True)
                mm.then_inc(s["logits"], 1)

        @block.scalar
        def _(act):
            with act.Fori(0, SLABS) as i:
                act.wait_ge(s["turned"], ONE + i)
                nc.scalar.copy(m["x_slab"][:, :], m["x"][:, bass.ds(i * SLAB * F, SLAB * F)]).then_inc(s["slab"], 1)
                act.wait_ge(s["turned"], ONE + i + 1)
                act.wait_ge(s["logits"], ONE + i)
                nc.scalar.copy(m["x_turned_slab"][:, 0:512], m["ps"][2][0:F, :])
                nc.scalar.copy(m["x_turned_slab"][:, 512:], m["ps"][3][0:F, 0:SLAB * P - 512]).then_inc(s["flipped"], 1)

        @block.vector
        def _(dve):
            dve.wait_ge(s["vectors"], ONE + 1)
            nc.vector.tensor_copy(m["vectors"][:, :], m["ps"][0][0:F, 0:8]).then_inc(s["vectors_out"], 1)
            dve.wait_ge(s["weights"], 48)
            with dve.Fori(0, SLABS) as i:
                dve.wait_ge(s["logits"], ONE + i + 1)
                logits = m["ps"][1][:, 0:8 * SLAB].rearrange("p (b h k) -> p b h k", b=SLAB, k=2)
                nc.vector.tensor_scalar(m["u"][:, bass.ds(i * SLAB * HEADS, SLAB * HEADS)].rearrange("p (b h) -> p b h", h=HEADS),
                                        logits[:, :, :, 0], m["sb_fc_b"][:, :], None, ALU.add)
                nc.vector.tensor_copy(m["xa"][:, bass.ds(i * SLAB * XA, SLAB * XA)].rearrange("p (b f) -> p b f", f=XA)[:, :, F:XA],
                                      logits[:, :, :, 1]).then_inc(s["logits_out"], 1)
            dve.wait_ge(s["logits_out"], ONE + SLABS)
            nc.vector.nop().then_inc(s["built"], 1)
            nc.vector.tensor_copy(m["xa"][:, :].rearrange("p (b f) -> p b f", f=XA)[:, :, 0:F],
                                  m["x"][:, :].rearrange("p (b f) -> p b f", f=F)).then_inc(s["built"], 1)


def stage_attention_gather(nc, m, s):
    pairs = m["sorted_pairs"].rearrange("(p c) k -> p (c k)", p=P)
    with nc.Block() as block:

        @block.sync
        def _(sp):
            with sp.Fori(0, ITERS) as i:
                for j in range(SLOTS):
                    sp.wait_ge(s["copied"][j], ONE + i)
                    sp.dma_start(m["index2"][j][:, :], pairs[:, bass.ds((SLOTS * i + j) * 2 * T, 2 * T)]).then_inc(s["indexed"][j], 16)

        @block.gpsimd
        def _(pool):
            with pool.Fori(0, ITERS) as i:
                for j in range(SLOTS):
                    pool.wait_ge(s["indexed"][j], 16 * (i + 1))
                    pool.wait_ge(s["copied"][j], ONE + i)
                    pool.wait_ge(s["rows_out"][j], FULL + 32 * i)
                    pool.sem_inc(s["going"], 1)
                    for t in range(T):
                        nc.gpsimd.indirect_dma_start(
                            out=m["rows"][j][:, t * XA:(t + 1) * XA], out_offset=None, in_=m["xa_table"],
                            in_offset=bass.IndirectOffsetOnAxis(ap=m["index2"][j][:, 2 * t + 1:2 * t + 2], axis=0),
                        ).then_inc(s["gathered"][j], 16)
                        nc.gpsimd.indirect_dma_start(
                            out=m["rows_u"][j][:, t * HEADS:(t + 1) * HEADS], out_offset=None, in_=m["u_table"],
                            in_offset=bass.IndirectOffsetOnAxis(ap=m["index2"][j][:, 2 * t:2 * t + 1], axis=0),
                        ).then_inc(s["gathered"][j], 16)

        @block.scalar
        def _(act):
            with act.Fori(0, ITERS) as i:
                for j in range(SLOTS):
                    g = SLOTS * i + j
                    act.wait_ge(s["gathered"][j], 32 * T * (i + 1))
                    rows = cut(m["rows"][j][:, :], t=T)
                    act.dma_start(cut(m["x_sorted"].rearrange("(p c) f -> p (c f)", p=P)[:, bass.ds(g * T * F, T * F)], t=T),
                                  rows[:, :, 0:F]).then_inc(s["rows_out"][j], 16)
                    act.dma_start(m["u_sorted"][:, bass.ds(g * T * HEADS, T * HEADS)], m["rows_u"][j][:, :]).then_inc(s["rows_out"][j], 16)
                    nc.scalar.copy(cut(m["logit"][:, bass.ds(g * T * HEADS, T * HEADS)], t=T), rows[:, :, F:XA]).then_inc(s["copied"][j], 1)
            for j in range(SLOTS):
                act.wait_ge(s["rows_out"][j], FULL + 32 * ITERS)


def spread_maxima(nc, link, keys, values, mask, tmp, n, parts, width):
    for back in (False, True):
        d = 1
        while d < n:
            near, far = (slice(0, n - d), slice(d, n)) if back else (slice(d, n), slice(0, n - d))
            link(nc.vector.tensor_tensor(mask[0:parts, 0:n - d], keys[:, near], keys[:, far], ALU.is_equal))
            link(nc.vector.tensor_scalar(mask[0:parts, 0:n - d], mask[0:parts, 0:n - d], 0.5, 2 * BIG, ALU.subtract, ALU.mult))
            for h in range(width):
                link(nc.vector.tensor_tensor(tmp[0:parts, 0:n - d], values[:, far, h], mask[0:parts, 0:n - d], ALU.min))
                link(nc.vector.tensor_tensor(values[:, near, h], values[:, near, h], tmp[0:parts, 0:n - d], ALU.max))
            d *= 2


def stage_attention_weights(nc, m, s):
    with nc.Block() as block:

        @block.sync
        def _(sp):
            sp.dma_start(m["pairs_in"][:, :], m["sorted_pairs"].rearrange("(p c) k -> p (c k)", p=P)).then_inc(s["loaded"], 16)
            sp.wait_ge(s["loaded"], 16)

        @block.tensor
        def _(pe):
            pe.wait_ge(s["edged"], ONE + 1)
            for k in range(4):
                mm = nc.tensor.transpose(m["ps"][0][0:HEADS, k * P:(k + 1) * P], m["edge_cols"][:, k * HEADS:(k + 1) * HEADS], m["ident"][:, :])
            mm.then_inc(s["turned"], 1)
            pe.wait_ge(s["spread"], ONE + 1)
            for k in range(2):
                mm = nc.tensor.transpose(m["ps"][1][:, k * HEADS:(k + 1) * HEADS], m["ends"][0:HEADS, k * P:(k + 1) * P],
                                         m["ident"][0:HEADS, 0:HEADS])
            mm.then_inc(s["turned_back"], 1)

        @block.vector
        def _(dve):
            link = Chain(dve, s["step"])
            dve.wait_ge(s["loaded"], 16)
            link(nc.vector.tensor_copy(m["sorted_keys"][:, :], m["pairs_in"][:, :].rearrange("p (c k) -> p c k", k=2)[:, :, 0]))
            link(nc.vector.tensor_copy(m["most"][:, :], m["logit"][:, :]))
            most = m["most"][:, :].rearrange("p (c h) -> p c h", h=HEADS)
            spread_maxima(nc, link, m["sorted_keys"][:, :], most, m["mask"], m["tmp_col"], COLS, P, HEADS)
            keys = m["sorted_keys"]
            for k, col in enumerate((most[:, 0, :], most[:, COLS - 1, :], keys[:, 0:1].broadcast_to([P, HEADS]),
                                     keys[:, COLS - 1:COLS].broadcast_to([P, HEADS]))):
                link(nc.vector.tensor_copy(m["edge_cols"][:, k * HEADS:(k + 1) * HEADS], col))
            nc.vector.nop().then_inc(s["edged"], 1)
            dve.wait_ge(s["turned"], ONE + 1)
            row = m["end_rows"][:, :].rearrange("h (k n e) -> h k n e", k=2, e=2)
            for k in range(4):
                link(nc.vector.tensor_copy(row[:, k // 2, :, k % 2], m["ps"][0][0:HEADS, k * P:(k + 1) * P]))
            spread_maxima(nc, link, m["end_rows"][:, 2 * P:4 * P], m["end_rows"][:, 0:2 * P].unsqueeze(2), m["mask"], m["tmp_col"],
                          2 * P, HEADS, 1)
            for k in range(2):
                link(nc.vector.tensor_copy(m["ends"][0:HEADS, k * P:(k + 1) * P], row[:, 0, :, k]))
            nc.vector.nop().then_inc(s["spread"], 1)
            dve.wait_ge(s["turned_back"], ONE + 1)
            link(nc.vector.tensor_copy(m["end_cols"][:, :], m["ps"][1][:, 0:2 * HEADS]))
            for k in range(2):
                end_key = m["edge_cols"][:, (2 + k) * HEADS:(2 + k) * HEADS + 1]
                link(nc.vector.tensor_scalar(m["mask"][:, 0:COLS], keys[:, :], end_key, None, ALU.is_equal))
                link(nc.vector.tensor_scalar(m["mask"][:, 0:COLS], m["mask"][:, 0:COLS], 0.5, 2 * BIG, ALU.subtract, ALU.mult))
                for h in range(HEADS):
                    end = m["end_cols"][:, k * HEADS + h:k * HEADS + h + 1]
                    link(nc.vector.tensor_scalar(m["tmp_col"][:, 0:COLS], m["mask"][:, 0:COLS], end, None, ALU.min))
                    link(nc.vector.tensor_tensor(most[:, :, h], most[:, :, h], m["tmp_col"][:, 0:COLS], ALU.max))


def stage_attention_exp(nc, m, s):
    with nc.Block() as block:

        @block.sync
        def _(sp):
            sp.dma_start(m["u_in"][:, :], m["u_sorted"]).then_inc(s["loaded"], 16)
            sp.wait_ge(s["weighed"], ONE + 1)
            sp.dma_start(m["weight_sorted"].rearrange("(p c) h -> p (c h)", p=P), m["logit"][:, :]).then_inc(s["stored"], 16)
            sp.wait_ge(s["stored"], 16)

        @block.vector
        def _(dve):
            link = Chain(dve, s["step"])
            dve.wait_ge(s["loaded"], 16)
            for part in (m["logit"], m["most"]):
                link(nc.vector.tensor_tensor(part[:, :], part[:, :], m["u_in"][:, :], ALU.add))
                link(nc.vector.scalar_tensor_tensor(part[:, :], part[:, :], ATT_SLOPE, part[:, :], ALU.mult, ALU.max))
            nc.vector.tensor_tensor(m["logit"][:, :], m["logit"][:, :], m["most"][:, :], ALU.subtract).then_inc(s["shifted"], 1)

        @block.scalar
        def _(act):
            act.wait_ge(s["shifted"], ONE + 1)
            nc.scalar.activation(m["logit"][:, :], m["logit"][:, :], ACT.Exp).then_inc(s["weighed"], 1)


def stage_attention_sum(nc, m, s):
    HF = HEADS * F
    W = HF + HEADS
    with nc.Block() as block:

        @block.sync
        def _(sp):
            sp.dma_start(m["sb_w_in"][:, :], m["att_w_in"]).then_inc(s["weights"], 16)
            sp.dma_start(m["sb_bias"][:, :], m["att_bias"].broadcast_to([P, F])).then_inc(s["weights"], 16)
            with sp.Fori(0, ITERS) as i:
                for j in range(SLOTS):
                    g = SLOTS * i + j
                    sp.wait_ge(s["weighed"][j], ONE + i)
                    sp.dma_start(m["x_rows"][j][:, :], m["x_sorted"].rearrange("(g p t) f -> g p (t f)", p=P, t=T)[bass.ds(g, 1)]
                                 .rearrange("g p f -> (g p) f")).then_inc(s["row_in"][j], 16)
                    sp.dma_start(m["weight"][j][:, :], m["weight_sorted"].rearrange("(g p t) h -> g p (t h)", p=P, t=T)[bass.ds(g, 1)]
                                 .rearrange("g p f -> (g p) f")).then_inc(s["row_in"][j], 16)

        @block.vector
        def _(dve):
            link = Chain(dve, s["step"])
            link(nc.vector.memset(m["acc"][:, :], 0.0))
            with dve.Fori(0, ITERS) as i:
                for j in range(SLOTS):
                    g = SLOTS * i + j
                    dve.wait_ge(s["row_in"][j], 32 * (i + 1))
                    rows = cut(m["rows"][j][:, :], t=T)
                    weight = cut(m["weight"][j][:, :], t=T)
                    nc.vector.tensor_copy(rows[:, :, HF:W], weight)
                    nc.vector.tensor_tensor(rows[:, :, 0:HF].rearrange("p t (h f) -> p t h f", f=F),
                                            rep(cut(m["x_rows"][j][:, :], t=T), 2, HEADS), rep(weight, 3, F),
                                            ALU.mult).then_inc(s["weighed"][j], 1)
                    visits_dve(nc, dve, m, s, g, m["acc"], W)
            sums_done(dve, m, s)
            acc = m["acc"][:, :].rearrange("p (b w) -> p b w", w=W)
            total = m["total"][:, :].rearrange("p (b h) -> p b h", h=HEADS)
            link(nc.vector.tensor_scalar(total, acc[:, :, HF:W], 0.5, float(HEADS), ALU.max, ALU.mult))
            link(nc.vector.reciprocal(m["total"][:, :], m["total"][:, :]))
            dve.wait_ge(s["weights"], 32)
            with dve.Fori(0, SLABS) as i:
                dve.wait_ge(s["turned"], ONE + i)
                sums = m["acc"][:, bass.ds(i * SLAB * W, SLAB * W)].rearrange("p (b w) -> p b w", w=W)
                for h in range(HEADS):
                    ins = nc.vector.tensor_tensor(
                        m["slab"][:, :].rearrange("p (b f) -> p b f", b=SLAB)[:, :, h * F:(h + 1) * F],
                        sums[:, :, h * F:(h + 1) * F],
                        rep(m["total"][:, bass.ds(i * SLAB * HEADS, SLAB * HEADS)].rearrange("p (b h) -> p b h", h=HEADS)[:, :, h], 2, F),
                        ALU.mult)
                ins.then_inc(s["slab"], 1)
                dve.wait_ge(s["result"], ONE + i + 1)
                here = m["x"][:, bass.ds(i * SLAB * F, SLAB * F)]
                nc.vector.tensor_tensor(here, here, m["ps"][2][:, 0:SLAB * F], ALU.add).then_inc(s["result_out"], 1)
            dve.wait_ge(s["result_out"], ONE + SLABS)
            cubed = lambda t: t[:, :].rearrange("p (b f) -> p b f", f=F)
            link(nc.vector.tensor_tensor(cubed(m["x"]), cubed(m["x"]), rep(m["sb_bias"][:, :], 1, NB), ALU.add))
            layer_norm(nc, dve, link, s, 1, cubed(m["x"]), cubed(m["tmp"]), m["mean"][:, :], m["root"][:, :])

        @block.scalar
        def _(act):
            with act.Fori(0, SLABS) as i:
                act.wait_ge(s["turned"], ONE + i + 1)
                act.wait_ge(s["result"], ONE + i)
                nc.scalar.copy(m["slab_turned"][:, 0:512], m["ps"][0][:, :])
                nc.scalar.copy(m["slab_turned"][:, 512:], m["ps"][1][:, 0:SLAB * P - 512]).then_inc(s["flipped"], 1)
            roots_act(nc, act, s, 1, m["root"][:, :])

        @block.tensor
        def _(pe):
            with pe.Fori(0, ITERS) as i:
                for j in range(SLOTS):
                    pe.wait_ge(s["weighed"][j], ONE + i + 1)
                    visits_pe(nc, pe, m, s, SLOTS * i + j, cut(m["rows"][j][:, :], t=T), W)
            pe.wait_ge(s["weights"], 32)
            with pe.Fori(0, SLABS) as i:
                pe.wait_ge(s["slab"], ONE + i + 1)
                pe.wait_ge(s["flipped"], ONE + i)
                pe.sem_inc(s["going"], 1)
                for b in range(SLAB):
                    mm = nc.tensor.transpose(m["ps"][b // 4][:, b % 4 * P:(b % 4 + 1) * P], m["slab"][:, b * P:(b + 1) * P], m["ident"][:, :])
                mm.then_inc(s["turned"], 1)
                pe.wait_ge(s["flipped"], ONE + i + 1)
                pe.wait_ge(s["result_out"], ONE + i)
                pe.sem_inc(s["going"], 1)
                for b in range(SLAB):
                    mm = nc.tensor.matmul(m["ps"][2][:, b * F:(b + 1) * F], m["slab_turned"][:, b * P:(b + 1) * P], m["sb_w_in"][:, :],
                                          start=True, stop=True)
                mm.then_inc(s["result"], 1)


U8, K16 = 8, 16
EMB = 10
SCALE1 = 1.0 / (EMB ** 0.5 * K16 ** 0.5 * (4 * U8) ** 0.5)
SCALE2 = 1.0 / (EMB ** 0.5 * K16 ** 0.5 * (2 * U8) ** 0.5)
ROOT3 = 3.0 ** 0.5
ST = 5 * U8


def stage_directions(nc, m, s):
    with nc.Block() as block:

        @block.sync
        def _(sp):
            sp.dma_start(m["dirs"][:, :], m["edge_vec"]).then_inc(s["loaded"], 16)
            sp.dma_start(m["strength"][:, :], m["edge_weight"]).then_inc(s["loaded"], 16)
            sp.dma_start(m["x_table"].rearrange("(b p) f -> p b f", p=P), m["x"][:, :].rearrange("p (b f) -> p b f", f=F)).then_inc(s["loaded"], 16)
            sp.dma_start(m["w_tensor"][:, :], m["conv_w1"]).then_inc(s["loaded"], 16)
            sp.dma_start(m["w_second"][:, :], m["conv_w2"]).then_inc(s["loaded"], 16)
            sp.dma_start(m["w_hidden"][:, :], m["conv_hidden"]).then_inc(s["loaded"], 16)
            sp.wait_ge(s["loaded"], 96)

        @block.vector
        def _(dve):
            link = Chain(dve, s["step"])
            dve.wait_ge(s["loaded"], 96)
            dirs = m["dirs"][:, :].rearrange("p (c k) -> p c k", k=3)
            link(nc.vector.tensor_tensor(m["squared"][:, :], m["dirs"][:, :], m["dirs"][:, :], ALU.mult))
            link(nc.vector.tensor_reduce(m["length"][:, :], m["squared"][:, :].rearrange("p (c k) -> p c k", k=3), AX.X, ALU.add))
            reciprocal_root(nc, dve, link, s, 1, m["length"][:, :])
            link(nc.vector.tensor_tensor(dirs, dirs, rep(m["length"][:, :], 2, 3), ALU.mult))
            link(nc.vector.tensor_scalar(m["w_tensor"][32:64, :], m["w_tensor"][32:64, :], ROOT3, None, ALU.mult))
            link(nc.vector.tensor_scalar(m["w_tensor"][64:80, :], m["w_tensor"][64:80, :], ROOT3, None, ALU.mult))
            link(nc.vector.tensor_scalar(m["w_second"][:, 256:320], m["w_second"][:, 256:320], ROOT3, None, ALU.mult))

        @block.scalar
        def _(act):
            roots_act(nc, act, s, 1, m["length"][:, :])


def stage_tensor_product(nc, m, s):
    W = F

    def sp_group(sp, i, j):
        g = SLOTS * i + j
        sp.wait_ge(s["prepared"][j], ONE + i)
        sp.dma_start(m["index2"][j][:, :], m["pairs"][:, bass.ds(g * 2 * T, 2 * T)]).then_inc(s["indexed"][j], 16)
        sp.wait_ge(s["hidden"][j], ONE + i)
        sp.dma_start(m["emb"][j][:, :], m["edge_emb"][:, bass.ds(g * T * P, T * P)]).then_inc(s["emb_in"][j], 16)

    def act_front(act, i, j):
        g = SLOTS * i + j
        act.wait_ge(s["gathered"][j], 32 * T * (i + 1))
        act.wait_ge(s["turned"], ONE + g)
        u = cut(m["u"][:, :], t=T)
        for half in range(2):
            rows = m["rows_x"][j][:, half * T * F:(half + 1) * T * F].rearrange("p (t f) -> p t f", t=T)
            nc.scalar.copy(u[:, :, half * U8:(half + 1) * U8], rows[:, :, 0:U8])
            ins = nc.scalar.copy(u[:, :, 80:128].rearrange("p t (c w) -> p t c w", c=3)[:, :, :, half * U8:(half + 1) * U8],
                                 rows[:, :, U8:F].rearrange("p t (w c) -> p t c w", c=3))
        ins.then_inc(s["copied"], 1)
        act.wait_ge(s["hidden"][j], ONE + i + 1)
        if not (isinstance(i, int) and i + j == 0):
            act.wait_ge(s["second"], ONE + T * (SLOTS * i + j - 1))
        nc.scalar.activation(m["h1"][j][:, :], m["ps"][1][:, P:P + T * K16], ACT.Relu, scale=SCALE1)
        nc.scalar.activation(m["h2"][j % 3][:, 0:512], m["ps"][2][0:K16, :], ACT.Relu, scale=SCALE2)
        nc.scalar.activation(m["h2"][j % 3][:, 512:], m["ps"][1][0:K16, 256:256 + P], ACT.Relu, scale=SCALE2).then_inc(s["bent"], 1)
        act.wait_ge(s["turned"], ONE + g + 1)
        nc.scalar.copy(m["u_turned"][:, 0:512], m["ps"][0][:, :])
        nc.scalar.copy(m["u_turned"][:, 512:], m["ps"][1][:, 0:P]).then_inc(s["flipped"], 1)

    def act_tanh(act, i, j):
        g = SLOTS * i + j
        act.wait_ge(s["summed_up"], ONE + g + 1)
        nc.scalar.activation(m["bounded"][:, :], m["unbounded"][:, :], ACT.Tanh).then_inc(s["bounded"], 1)

    def dve_front(dve, link, i, j):
        g = SLOTS * i + j
        dve.wait_ge(s["copied"], ONE + g + 1)
        u = cut(m["u"][:, :], t=T)
        r = m["dirs"][:, bass.ds(g * 3 * T, 3 * T)].rearrange("p (t c) -> p t c", c=3)
        parts = []
        for half in range(2):
            rows = m["rows_x"][j][:, half * T * F:(half + 1) * T * F].rearrange("p (t f) -> p t f", t=T)
            part = m["dots"][half][:, :].rearrange("p (t w c) -> p t w c", t=T, c=3)
            parts.append(part)
            ins = nc.vector.tensor_tensor(part, rows[:, :, U8:F].rearrange("p t (w c) -> p t w c", c=3), rep(r, 2, U8), ALU.mult)
        link(ins)
        for half in range(2):
            nc.vector.tensor_reduce(u[:, :, K16 + half * U8:K16 + (half + 1) * U8], parts[half], AX.X, ALU.add)
        nc.vector.tensor_tensor(u[:, :, 32:80].rearrange("p t (c w) -> p t c w", c=3), rep(u[:, :, 0:K16], 2, 3),
                                rep(r, 3, K16), ALU.mult).then_inc(s["prepared"][j], 1)

    def dve_first(dve, link, i, j):
        g = SLOTS * i + j
        r = m["dirs"][:, bass.ds(g * 3 * T, 3 * T)].rearrange("p (t c) -> p t c", c=3)
        st = cut(m["st"][:, :], t=T)
        dve.wait_ge(s["bent"], ONE + g + 1)
        for t in range(T):
            dve.wait_ge(s["brackets"], ONE + g * T + t + 1)
            nc.vector.tensor_tensor(m["wide"][:, t * 512:(t + 1) * 512].rearrange("p (w k) -> p w k", k=K16),
                                    m["ps"][3 + t % 2][:, :].rearrange("p (w k) -> p w k", k=K16),
                                    rep(m["h1"][j][:, t * K16:(t + 1) * K16], 1, 32), ALU.mult).then_inc(s["brackets_used"], 1)
        dve.wait_ge(s["brackets_used"], ONE + (g + 1) * T)
        link(nc.vector.tensor_reduce(st[:, :, 0:32], m["wide"][:, :].rearrange("p (t w k) -> p t w k", t=T, k=K16), AX.X, ALU.add))
        v = st[:, :, 0:24].rearrange("p t (c w) -> p t c w", c=3)
        part = m["dots"][2][:, :].rearrange("p (t w c) -> p t w c", t=T, c=3)
        link(nc.vector.tensor_tensor(part.rearrange("p t w c -> p t c w"), v, rep(r, 3, U8), ALU.mult))
        link(nc.vector.tensor_reduce(st[:, :, 32:40], part, AX.X, ALU.add))

    def dve_second(dve, link, i, j):
        g = SLOTS * i + j
        r = m["dirs"][:, bass.ds(g * 3 * T, 3 * T)].rearrange("p (t c) -> p t c", c=3)
        for t in range(T):
            dve.wait_ge(s["second"], ONE + g * T + t + 1)
            bank, wide = m["ps"][5 + t % 2], m["wide"][:, t * 512:(t + 1) * 512]
            st = m["st"][:, t * ST:(t + 1) * ST]
            nc.vector.tensor_tensor(wide[:, 0:256].rearrange("p (o k) -> p o k", k=K16), bank[:, 0:256].rearrange("p (o k) -> p o k", k=K16),
                                    rep(st[:, 24:40], 1, K16), ALU.mult)
            nc.vector.tensor_tensor(wide[:, 256:448].rearrange("p (c o w) -> p c o w", c=3, w=U8),
                                    rep(bank[:, 320:384].rearrange("p (o w) -> p o w", w=U8), 1, 3),
                                    rep(st[:, 0:24].rearrange("p (c w) -> p c w", c=3), 2, U8), ALU.mult)
            nc.vector.tensor_tensor(wide[:, 448:512].rearrange("p (o w) -> p o w", w=U8),
                                    bank[:, 256:320].rearrange("p (o w) -> p o w", w=U8),
                                    rep(st[:, 24:32], 1, U8), ALU.mult).then_inc(s["second_used"], 1)
        dve.wait_ge(s["second_used"], ONE + (g + 1) * T)
        link(nc.vector.tensor_reduce(m["sums"][:, :], m["wide"][:, :].rearrange("p (n w) -> p n w", w=U8), AX.X, ALU.add))
        sums = cut(m["sums"][:, :], t=T)
        nc.vector.tensor_reduce(cut(m["unbounded"][:, :], t=T), sums[:, :, 0:32].rearrange("p t (o e) -> p t o e", e=2), AX.X,
                                ALU.add).then_inc(s["summed_up"], 1)
        part = m["dots"][2][:, :].rearrange("p (t c w) -> p t c w", t=T, c=3)
        link(nc.vector.tensor_tensor(part, rep(sums[:, :, 56:64], 2, 3), rep(r, 3, U8), ALU.mult))
        link(nc.vector.tensor_tensor(part, part, sums[:, :, 32:56].rearrange("p t (c w) -> p t c w", c=3), ALU.add))
        dve.wait_ge(s["bounded"], ONE + g + 1)
        strength = m["strength"][:, bass.ds(g * T, T)]
        rows = cut(m["rows"][j][:, :], t=T)
        link(nc.vector.tensor_tensor(cut(m["gates"][:, :], t=T), cut(m["bounded"][:, :], t=T)[:, :, U8:K16], rep(strength, 2, U8), ALU.mult))
        nc.vector.tensor_tensor(rows[:, :, 0:U8], cut(m["bounded"][:, :], t=T)[:, :, 0:U8], rep(strength, 2, U8), ALU.mult)
        nc.vector.tensor_tensor(rows[:, :, U8:F].rearrange("p t (w c) -> p t c w", c=3), part,
                                rep(cut(m["gates"][:, :], t=T), 2, 3), ALU.mult).then_inc(s["edge_rows"], 1)
        visits_dve(nc, dve, m, s, g, m["acc"], W)

    def pe_front(pe, i, j):
        g = SLOTS * i + j
        pe.wait_ge(s["emb_in"][j], 16 * (i + 1))
        pe.wait_ge(s["bent"], ONE + g)
        pe.wait_ge(s["flipped"], ONE + g)
        pe.sem_inc(s["going"], 1)
        for t in range(T):
            nc.tensor.matmul(m["ps"][1][:, P + t * K16:P + (t + 1) * K16], m["emb"][j][:, t * P:(t + 1) * P], m["w_hidden"][:, 0:K16],
                             start=True, stop=True)
        nc.tensor.matmul(m["ps"][2][0:K16, :], m["w_hidden"][:, K16:2 * K16], m["emb"][j][:, 0:512], start=True, stop=True)
        nc.tensor.matmul(m["ps"][1][0:K16, 256:256 + P], m["w_hidden"][:, K16:2 * K16], m["emb"][j][:, 512:],
                         start=True, stop=True).then_inc(s["hidden"][j], 1)
        pe.wait_ge(s["prepared"][j], ONE + i + 1)
        pe.wait_ge(s["bent"], ONE + g + 1)
        pe.sem_inc(s["going"], 1)
        for t in range(T):
            mm = nc.tensor.transpose(m["ps"][t // 4][:, t % 4 * P:(t % 4 + 1) * P], m["u"][:, t * P:(t + 1) * P], m["ident"][:, :])
        mm.then_inc(s["turned"], 1)

    def pe_first(pe, i, j):
        g = SLOTS * i + j
        pe.wait_ge(s["flipped"], ONE + g + 1)
        for t in range(T):
            pe.wait_ge(s["brackets_used"], ONE + g * T + max(t - 1, 0))
            pe.sem_inc(s["going"], 1)
            nc.tensor.matmul(m["ps"][3 + t % 2][:, :], m["u_turned"][:, t * P:(t + 1) * P], m["w_tensor"][:, :],
                             start=True, stop=True).then_inc(s["brackets"], 1)

    def pe_second(pe, i, j):
        g = SLOTS * i + j
        pe.wait_ge(s["bent"], ONE + g + 1)
        for t in range(T):
            pe.wait_ge(s["second_used"], ONE + g * T + max(t - 1, 0))
            pe.sem_inc(s["going"], 1)
            mm = nc.tensor.matmul(m["ps"][5 + t % 2][:, 0:384], m["h2"][j % 3][:, t * P:(t + 1) * P], m["w_second"][:, :],
                                  start=True, stop=True)
            mm.then_inc(s["second"], 1)
        pe.wait_ge(s["edge_rows"], ONE + g + 1)
        visits_pe(nc, pe, m, s, g, cut(m["rows"][j][:, :], t=T), W)

    def in_turn(eng, own, ahead, finish):
        def turn(i, last):
            for j in range(SLOTS):
                own(i, j)
                if not (last and j == SLOTS - 1):
                    ahead(i + (j + 1) // SLOTS, (j + 1) % SLOTS)
                finish(i, j)
        ahead(0, 0)
        with eng.Fori(0, ITERS - 1) as i:
            turn(i, False)
        turn(ITERS - 1, True)

    with nc.Block() as block:

        @block.sync
        def _(sp):
            with sp.Fori(0, ITERS) as i:
                for j in range(SLOTS):
                    sp_group(sp, i, j)
            sp.wait_ge(s["finished"], ONE + 1)
            sp.dma_start(m["out"], m["x"][:, :]).then_inc(s["stored"], 16)
            sp.wait_ge(s["stored"], 16)

        @block.gpsimd
        def _(pool):
            with pool.Fori(0, ITERS) as i:
                for j in range(SLOTS):
                    pool.wait_ge(s["indexed"][j], 16 * (i + 1))
                    pool.wait_ge(s["prepared"][j], ONE + i)
                    pool.sem_inc(s["going_pool"], 1)
                    for t in range(T):
                        for half in range(2):
                            to = half * T * F + t * F
                            nc.gpsimd.indirect_dma_start(
                                out=m["rows_x"][j][:, to:to + F], out_offset=None, in_=m["x_table"],
                                in_offset=bass.IndirectOffsetOnAxis(ap=m["index2"][j][:, 2 * t + half:2 * t + half + 1], axis=0),
                            ).then_inc(s["gathered"][j], 16)

        @block.scalar
        def _(act):
            in_turn(act, lambda i, j: None, lambda i, j: act_front(act, i, j), lambda i, j: act_tanh(act, i, j))
            roots_act(nc, act, s, 1, m["root"][:, :])

        @block.vector
        def _(dve):
            link = Chain(dve, s["step"])
            link(nc.vector.memset(m["acc"][:, :], 0.0))
            LINKS = 8

            def own(i, j):
                link.base, link.n = (SLOTS * i + j) * LINKS + 2, 0
                dve_first(dve, link, i, j)

            def ahead(i, j):
                dve_front(dve, link, i, j)

            def finish(i, j):
                if isinstance(i, int) and i == ITERS - 1 and j == SLOTS - 1:
                    dve_second(dve, link, i, j)
                    assert link.n == LINKS - 1
                else:
                    dve_second(dve, link, i, j)
                    assert link.n == LINKS
            in_turn(dve, own, ahead, finish)
            sums_done(dve, m, s)
            link.base, link.n = GROUPS * LINKS + 1, 0
            cubed = lambda t: t[:, :].rearrange("p (b f) -> p b f", f=F)
            link(nc.vector.tensor_tensor(m["x"][:, :], m["x"][:, :], m["acc"][:, :], ALU.add))
            layer_norm(nc, dve, link, s, 1, cubed(m["x"]), cubed(m["tmp"]), m["mean"][:, :], m["root"][:, :])
            nc.vector.nop().then_inc(s["finished"], 1)

        @block.tensor
        def _(pe):
            in_turn(pe, lambda i, j: pe_first(pe, i, j), lambda i, j: pe_front(pe, i, j), lambda i, j: pe_second(pe, i, j))


def build(nc, d):
    with ExitStack() as ctx:
        m = dict(d)

        def sb(name, cols, dt=F32, parts=P, into=None):
            t = (into or ctx).enter_context(nc.sbuf_tensor(f"{name}_{nc.next_id()}", [parts, cols], dt))
            m[name] = t
            return t

        taken, primed = [], [0]

        def sems(stage, plain, slotted=""):
            if taken:
                nc.clear_and_free_semaphores(list(taken))
                nc.all_engine_barrier()
                taken.clear()

            def sem(name, slot=""):
                taken.append(nc.alloc_semaphore(name=f"{stage}_{name}{slot}"))
                if name in RECYCLED:
                    cell = primed[0]
                    primed[0] += 1
                    nc.sync.dma_start(m["scrap"][0:1, cell:cell + 1], m["dst"][0:1, 0:1]).then_inc(taken[-1], FULL)
                elif name not in FROM_ZERO:
                    nc.sync.sem_inc(taken[-1], ONE)
                return taken[-1]

            s = {}
            for n in plain.split():
                s[n] = sem(n)
            for n in slotted.split():
                s[n] = [sem(n, j) for j in range(SLOTS)]
            nc.all_engine_barrier()
            return s

        m["ps"] = [ctx.enter_context(nc.psum_tensor(f"bank{k}", [P, 512], F32)) for k in range(8)]
        sb("x", NB * F); sb("tmp", NB * F); sb("mean", NB); sb("root", NB)
        sb("out_deg", NB); sb("in_deg", NB)
        sb("part", 1); sb("scrap", 64, I32, parts=1); sb("ramp", P); sb("ident", P); sb("before", P); sb("ones", P); sb("zeros", P, BF16); sb("zero_row", 512, BF16); sb("attr_sum", 2 * F)
        sb("window", 3 * GROUPS, I32)
        sb("a1_stats", 8); sb("square_sum", 1); sb("w", P)

        whole = ctx.enter_context(ExitStack())
        sb("acc", NB * (H + 1), into=whole)
        with ExitStack() as scope:
            sb("iota", NP, into=scope); sb("keys", COLS, into=scope); sb("onehot", T * P, into=scope)
            with ExitStack() as inner:
                sb("ints", COLS, I32, into=inner); sb("src_int", COLS, I32, into=inner)
                sb("low", COLS, into=inner); sb("high", COLS, into=inner)
                m["hot_low"] = [inner.enter_context(nc.sbuf_tensor(f"hot_low{j}", [P, T * P], BF16)) for j in range(SLOTS)]
                m["hot_high"] = [inner.enter_context(nc.sbuf_tensor(f"hot_high{j}", [P, T * NB], BF16)) for j in range(SLOTS)]
                m["attr"] = [inner.enter_context(nc.sbuf_tensor(f"attr{j}", [P, T * F], F32)) for j in range(SLOTS)]
                m["attr_square"] = [inner.enter_context(nc.sbuf_tensor(f"attr_square{j}", [P, T * F], F32)) for j in range(SLOTS)]
                stage_setup(nc, m, sems("setup", "squared step zero loaded x_loaded iota hot histogram", "counted attr_in attr_used"))
            with ExitStack() as inner:
                sb("ints", COLS, I32, into=inner); sb("floats", COLS, into=inner); sb("keys_int", COLS, I32, into=inner)
                sb("least", GROUPS, into=inner); sb("most", GROUPS, into=inner)
                sb("wide", SLOTS, into=inner); sb("win", 3 * SLOTS, into=inner); sb("win_int", 3 * SLOTS, I32, into=inner)
                stage_windows(nc, m, False, sems("window", "loaded step extremes turned counted prefixed tabled stored"))
            with ExitStack() as inner:
                m["rows"] = [inner.enter_context(nc.sbuf_tensor(f"rows{j}", [P, T * (F + 1)], F32)) for j in range(SLOTS)]
                m["index"] = [inner.enter_context(nc.sbuf_tensor(f"index{j}", [P, T], I32)) for j in range(SLOTS)]
                stage_convolve(nc, m, sems("conv", "to_root rooted going step scaled cleared stored onehot summed added", "gathered indexed used"))
            for name, shape in (("m1_w1", [C2, H]), ("m1_c1", [H, 1]), ("m1_g1", [C2, 1]), ("m1_b1", [C2, 1]),
                                ("m1_w2", [H, H]), ("m1_g2", [H, 1]), ("m1_b2", [H, 1]), ("m1_c2", [P, H])):
                sb("sb_" + name, shape[1], parts=shape[0], into=scope)
            with ExitStack() as inner:
                def slots(name, cols, dt=F32, parts=P):
                    m[name] = [inner.enter_context(nc.sbuf_tensor(f"{name}_{nc.next_id()}", [parts, cols], dt)) for j in range(SLOTS)]
                slots("rows", T * C2); slots("index", T, I32); slots("a1", T * P, parts=H)
                m["lift"] = [inner.enter_context(nc.sbuf_tensor(f"lift{j}", [H, T * P], F32)) for j in range(2)]
                sb("flipped", T * P, parts=C2, into=inner); sb("stats", GROUPS * 12, parts=H, into=inner)
                sb("bn", 8, into=inner); sb("bias", 1, into=inner); sb("sums", C2, into=inner); sb("total_row", 2 * C2, into=inner)
                stage_edges_first(nc, m, sems("first", "step to_root rooted going stored weights node_sums totals rowed columns folded shifted biased multiplied flipped lifted a1_made counted", "gathered indexed turned attr_in a1_out"))
            with ExitStack() as inner:
                slots("rows", T * (H + 1)); slots("a1", T * P, parts=H)
                sb("squares", T * H, into=inner); sb("lift2", T * H, into=inner)
                sb("wide_shift", P, into=inner); sb("bias_row", H, into=inner)
                stage_edges_second(nc, m, sems("second", "step to_root rooted weights folded shifted biased lifted a2_made squared squares_used onehot summed added", "products a1_in"))
        with ExitStack() as inner:
            shapes = dict(m1_w3=[H, H], m1_g3=[H, 1], m1_b3=[H, 1], m2_g1a=[H, 1], m2_b1a=[H, 1], m2_w1a=[H, W96],
                          m2_g1x=[F, 1], m2_b1x=[F, 1], m2_w1x=[F, W96], m2_c1=[W96, 1], m2_g2=[W96, 1], m2_b2=[W96, 1],
                          m2_w2=[W96, W96], m2_c2=[W96, 1], m2_g3=[W96, 1], m2_b3=[W96, 1], m2_w3=[W96, F], m2_c3=[F, 1])
            m["node_weights"] = tuple(shapes)
            for name, (parts, cols) in shapes.items():
                sb("sb_" + name, cols, parts=parts, into=inner)
            sb("h", NP, parts=W96, into=inner); sb("x_turned", NP, parts=F, into=inner)
            sb("acc_slab", SLAB * (H + 1), into=inner); sb("x_slab", SLAB * F, into=inner); sb("out_slab", SLAB * P, parts=F, into=inner)
            sb("acc_turned", SLAB * P, into=inner); sb("node_lift", CHUNK, parts=W96, into=inner)
            sb("stats", NCHUNKS * 6, into=inner); sb("stats_x", NCHUNKS * 6, into=inner)
            for name in ("bn3", "bn_agg", "bn_x", "bn_h"):
                sb(name, 8, into=inner)
            sb("fold3", H + 1, parts=H, into=inner); sb("w3", H, into=inner); sb("c3_row", H, into=inner)
            sb("wa", W96, parts=H, into=inner); sb("wx", W96, parts=F, into=inner); sb("wh", W96, parts=W96, into=inner)
            sb("bias96", 1, into=inner); sb("sums", H, into=inner)
            stage_nodes(nc, m, sems("nodes", "step to_root rooted going weights cleared turned slab product bent lifted biased turned_back summed totals folded w3_made w3_out flipped agged agg_out measured shifted added"))
        whole.close()
        with ExitStack() as inner:
            def slots(name, cols, dt=F32):
                    m[name] = [inner.enter_context(nc.sbuf_tensor(f"{name}_{nc.next_id()}", [P, cols], dt)) for j in range(SLOTS)]
            slots("hot_low", T * P, BF16); slots("hot_high", T * NB, BF16); slots("same", T * P, BF16)
            slots("src_row", T * P, I32); slots("pair", 2 * T, I32); slots("place", T); slots("place_int", T, I32)
            sb("src_float", COLS, into=inner); sb("src_int", COLS, I32, into=inner); sb("ints", COLS, I32, into=inner)
            sb("low", COLS, into=inner); sb("high", COLS, into=inner)
            sb("turned", T * P, into=inner); sb("counts", NB, into=inner)
            sb("sums", P, into=inner); sb("picked", T * NB, into=inner); sb("ident_half", P, BF16, into=inner)
            m["ps_turn"] = m["ps"][4][:, :].bitcast(BF16)
            stage_sort(nc, m, sems("sort", "loaded step sums sums_out begun counts_out counted turned turned_out hot_lows hot_highs looked picked going", "compared moved freed placed row_in pair_in"))
        with ExitStack() as outer:
            sb("logit", COLS * HEADS, into=outer); sb("most", COLS * HEADS, into=outer)
            with ExitStack() as inner:
                sb("sb_w_out", HEADS * F, parts=F, into=inner); sb("sb_fc", 2, parts=F, into=inner); sb("sb_fc_b", 1, into=inner)
                sb("vectors", 8, parts=F, into=inner); sb("x_slab", SLAB * F, into=inner); sb("x_turned_slab", SLAB * P, parts=F, into=inner)
                sb("u", NB * HEADS, into=inner); sb("xa", NB * XA, into=inner)
                stage_attention_tables(nc, m, sems("tables", "weights built stored vectors vectors_out slab flipped going turned logits logits_out"))
            with ExitStack() as inner:
                for name, cols, dt in (("rows", T * XA, F32), ("rows_u", T * HEADS, F32), ("index2", 2 * T, I32)):
                    m[name] = [inner.enter_context(nc.sbuf_tensor(f"{name}_{nc.next_id()}", [P, cols], dt)) for j in range(SLOTS)]
                stage_attention_gather(nc, m, sems("att_gather", "going", "gathered indexed copied rows_out"))
            with ExitStack() as inner:
                sb("pairs_in", 2 * COLS, I32, into=inner); sb("sorted_keys", COLS, into=inner); sb("mask", COLS, into=inner)
                sb("tmp_col", COLS, into=inner); sb("edge_cols", 4 * HEADS, into=inner); sb("end_rows", 4 * P, parts=HEADS, into=inner)
                sb("ends", 2 * P, parts=HEADS, into=inner); sb("end_cols", 2 * HEADS, into=inner)
                stage_attention_weights(nc, m, sems("att_max", "loaded step edged turned spread turned_back"))
            with ExitStack() as inner:
                sb("u_in", COLS * HEADS, into=inner)
                stage_attention_exp(nc, m, sems("att_exp", "loaded step weighed stored shifted"))
        with ExitStack() as scope:
            sb("iota", NP, into=scope); sb("keys", COLS, into=scope); sb("onehot", T * P, into=scope)
            with ExitStack() as inner:
                sb("ints", COLS, I32, into=inner); sb("floats", COLS, into=inner); sb("keys_int", COLS, I32, into=inner)
                sb("pairs_in", 2 * COLS, I32, into=inner)
                sb("least", GROUPS, into=inner); sb("most", GROUPS, into=inner)
                sb("wide", SLOTS, into=inner); sb("win", 3 * SLOTS, into=inner); sb("win_int", 3 * SLOTS, I32, into=inner)
                stage_windows(nc, m, True, sems("src_window", "loaded step extremes turned counted prefixed tabled stored"))
            with ExitStack() as inner:
                HF = HEADS * F
                sb("acc", NB * (HF + HEADS), into=inner); sb("total", NB * HEADS, into=inner); sb("slab", SLAB * P, into=inner)
                sb("slab_turned", SLAB * P, into=inner); sb("sb_w_in", F, into=inner); sb("sb_bias", F, into=inner)
                for name, cols in (("rows", T * (HF + HEADS)), ("x_rows", T * F), ("weight", T * HEADS)):
                    m[name] = [inner.enter_context(nc.sbuf_tensor(f"{name}_{nc.next_id()}", [P, cols], F32)) for j in range(SLOTS)]
                stage_attention_sum(nc, m, sems("att_sum", "to_root rooted weights step going slab turned flipped result result_out onehot summed added", "weighed row_in"))
        with ExitStack() as scope:
            sb("iota", NP, into=scope); sb("keys", COLS, into=scope); sb("onehot", T * P, into=scope)
            with ExitStack() as inner:
                sb("ints", COLS, I32, into=inner); sb("floats", COLS, into=inner); sb("keys_int", COLS, I32, into=inner)
                sb("least", GROUPS, into=inner); sb("most", GROUPS, into=inner)
                sb("wide", SLOTS, into=inner); sb("win", 3 * SLOTS, into=inner); sb("win_int", 3 * SLOTS, I32, into=inner)
                stage_windows(nc, m, False, sems("dst_window", "loaded step extremes turned counted prefixed tabled stored"))
            sb("dirs", COLS * 3, into=scope); sb("strength", COLS, into=scope)
            sb("w_tensor", 512, into=scope); sb("w_second", 384, parts=K16, into=scope); sb("w_hidden", 2 * K16, parts=EMB, into=scope)
            with ExitStack() as inner:
                sb("squared", COLS * 3, into=inner); sb("length", COLS, into=inner)
                stage_directions(nc, m, sems("dirs", "loaded step to_root rooted"))
            with ExitStack() as inner:
                for name, parts, cols, dt in (("index2", P, 2 * T, I32), ("emb", EMB, T * P, F32), ("rows_x", P, 2 * T * F, F32),
                                              ("h1", P, T * K16, F32), ("rows", P, T * F, F32)):
                    m[name] = [inner.enter_context(nc.sbuf_tensor(f"{name}_{nc.next_id()}", [parts, cols], dt)) for j in range(SLOTS)]
                m["h2"] = [inner.enter_context(nc.sbuf_tensor(f"h2_{k}", [K16, T * P], F32)) for k in range(3)]
                m["dots"] = [inner.enter_context(nc.sbuf_tensor(f"dots_{nc.next_id()}", [P, T * 24], F32)) for k in range(3)]
                sb("u", T * P, into=inner); sb("u_turned", T * P, into=inner); sb("wide", T * 512, into=inner)
                sb("st", T * ST, into=inner); sb("sums", T * 64, into=inner); sb("unbounded", T * K16, into=inner)
                sb("bounded", T * K16, into=inner); sb("gates", T * U8, into=inner); m["acc"] = m["tmp"]
                stage_tensor_product(nc, m, sems("tp", "step to_root rooted finished stored going going_pool turned copied bent flipped summed_up bounded brackets brackets_used second second_used edge_rows onehot summed added", "gathered indexed emb_in hidden prepared"))


def by_group(a):
    a = np.asarray(a)
    return np.ascontiguousarray(a.reshape(GROUPS, P, T, -1).transpose(1, 0, 2, 3).reshape(P, -1))


def laid_out(x, src, dst, edge_attr_10, edge_attr_3, edge_attr_32, edge_weight, **w):
    x_in = np.zeros((NP, F), np.float32)
    x_in[:N] = x
    col = lambda a: np.ascontiguousarray(np.asarray(a).reshape(-1, 1))
    row = lambda a: np.ascontiguousarray(np.asarray(a).reshape(1, -1))
    l1 = {k[len("L1_gnn_"):]: np.asarray(v) for k, v in w.items() if k.startswith("L1_gnn_m")}
    w1, g1, b1 = l1["m2_w1"], l1["m2_g1"], l1["m2_b1"]
    att_w = np.asarray(w["L2_gnn_w"])
    out = dict(
        x_in=np.ascontiguousarray(x_in.reshape(NB, P, F).transpose(1, 0, 2).reshape(P, -1)),
        src=by_group(src), dst=by_group(dst), pairs=by_group(np.stack([src, dst], 1)),
        src_rows=np.ascontiguousarray(np.asarray(src).reshape(GROUPS, P, T).transpose(0, 2, 1).reshape(GROUPS, -1)),
        edge_attr=by_group(edge_attr_32), edge_vec=by_group(edge_attr_3), edge_weight=by_group(edge_weight),
        edge_emb=np.ascontiguousarray(np.asarray(edge_attr_10).reshape(GROUPS, P, T, EMB).transpose(3, 0, 2, 1).reshape(EMB, -1)),
        m1_c2=row(l1["m1_c2"]), m1_c3=row(l1["m1_c3"]),
        m2_g1a=col(g1[F:]), m2_b1a=col(b1[F:]), m2_w1a=np.ascontiguousarray(w1[F:]),
        m2_g1x=col(g1[:F]), m2_b1x=col(b1[:F]), m2_w1x=np.ascontiguousarray(w1[:F]),
        att_w_out=np.ascontiguousarray(att_w.transpose(2, 0, 1).reshape(F, -1)),
        att_fc=np.ascontiguousarray(np.asarray(w["L2_gnn_fc_w"]).reshape(2, F).T),
        att_fc_b=np.asarray(w["L2_gnn_fc_b"]).reshape(1, 1),
        att_w_in=np.ascontiguousarray(att_w.reshape(-1, F)), att_bias=row(w["L2_gnn_bias"]),
    )
    for k in ("m1_w1", "m1_w2", "m1_w3", "m2_w2", "m2_w3"):
        out[k] = l1[k]
    for k in ("m1_c1", "m1_g1", "m1_b1", "m1_g2", "m1_b2", "m1_g3", "m1_b3", "m2_c1", "m2_g2", "m2_b2", "m2_c2", "m2_g3",
              "m2_b3", "m2_c3"):
        out[k] = col(l1[k])
    t1 = np.asarray(w["L3_gnn_fc1_w2"]).reshape(K16, 4, 2 * U8, U8).transpose(1, 2, 3, 0)
    big = np.zeros((P, 4, U8, K16), np.float32)
    big[0:16, 3], big[16:32, 3] = t1[0], t1[1]
    for c in range(3):
        big[32 + 16 * c:48 + 16 * c, c] = t1[2]
        big[80 + 16 * c:96 + 16 * c, c] = t1[3]
    out["conv_w1"] = big.reshape(P, 512)
    t2 = np.asarray(w["L3_gnn_fc2_w2"]).reshape(K16, 6, U8, U8).transpose(0, 1, 3, 2)
    out["conv_w2"] = np.ascontiguousarray(np.concatenate(
        [np.concatenate([t2[:, 0], t2[:, 1]], 2).reshape(K16, -1), np.concatenate([t2[:, 2], t2[:, 3]], 2).reshape(K16, -1),
         t2[:, 4].reshape(K16, -1), t2[:, 5].reshape(K16, -1)], 1))
    out["conv_hidden"] = np.ascontiguousarray(np.concatenate([w["L3_gnn_fc1_w1"], w["L3_gnn_fc2_w1"]], 1))
    return {k: np.ascontiguousarray(v) for k, v in out.items()}


_INTERNAL = dict(sorted_pairs=((E, 2), I32), x_table=((NP, F), F32), window_dram=((GROUPS, 3), I32),
                 a1_dram=((GROUPS, H, T * P), F32), xa_table=((NP, XA), F32), u_table=((NP, HEADS), F32),
                 x_sorted=((E, F), F32), u_sorted=((P, COLS * HEADS), F32), weight_sorted=((E, HEADS), F32))


def kernel(**inputs):
    import concourse.bacc as bacc
    from concourse.bass_utils import run_bass_kernel_spmd

    nc = bacc.Bacc("TRN2", target_bir_lowering=False, num_devices=1)
    arrays = laid_out(**{k: np.asarray(v) for k, v in inputs.items()})
    d = {k: nc.dram_tensor(f"in_{k}", a.shape, mybir.dt.from_np(a.dtype), kind="ExternalInput").ap() for k, a in arrays.items()}
    for k, (shape, dt) in _INTERNAL.items():
        d[k] = nc.dram_tensor(k, shape, dt, kind="Internal").ap()
    d["out"] = nc.dram_tensor("out", (P, NB * F), F32, kind="ExternalOutput").ap()
    build(nc, d)
    r = run_bass_kernel_spmd(nc, [{f"in_{k}": a for k, a in arrays.items()}], core_ids=[0])
    out = np.asarray(r.results[0]["out"])
    return np.ascontiguousarray(out.reshape(P, NB, F).transpose(1, 0, 2).reshape(NP, F)[:N])
```

```python
from contextlib import ExitStack

import numpy as np

import concourse.bass as bass
from concourse import mybir

P = 128
T = 5
SLOTS = 5
N, E, F = 12500, 400000, 32
NB = -(-N // P)
NP = NB * P
GROUPS = E // (P * T)
ITERS = GROUPS // SLOTS
COLS = E // P
GC = GROUPS // SLOTS
C2 = 2 * F
assert GROUPS * P * T == E and ITERS * SLOTS == GROUPS

ALU = mybir.AluOpType
ACT = mybir.ActivationFunctionType
F32 = mybir.dt.float32
BF16 = mybir.dt.bfloat16
I32 = mybir.dt.int32
AX = mybir.AxisListType
EPS = 1e-5


ONE, FULL = 1, 16
FROM_ZERO = ("loaded", "x_loaded", "attr_in", "stored", "indexed", "row_in", "pair_in", "a1_in", "emb_in", "weights", "step",
             "gathered", "moved")
RECYCLED = ("a1_out", "rows_out")


class Chain:

    def __init__(self, eng, sem):
        self.eng, self.sem, self.n, self.base = eng, sem, 0, 0

    def __call__(self, ins):
        self.n += 1
        ins.then_inc(self.sem, 1)
        self.eng.wait_ge(self.sem, self.base + self.n)


def rep(ap, axis, n):
    a = ap.unsqueeze(axis)
    shape = list(a.shape)
    shape[axis] = n
    return a.broadcast_to(shape)


def cut(ap, **sizes):
    return ap.rearrange("p (t w) -> p t w", **sizes)


def reciprocal_root(nc, dve, link, s, turn, root):
    nc.vector.nop().then_inc(s["to_root"], 1)
    dve.wait_ge(s["rooted"], ONE + turn)
    link(nc.vector.reciprocal(root, root))


def roots_act(nc, act, s, turns, root):
    for turn in range(1, turns + 1):
        act.wait_ge(s["to_root"], ONE + turn)
        nc.scalar.activation(root, root, ACT.Sqrt).then_inc(s["rooted"], 1)


def layer_norm(nc, dve, link, s, turn, x, tmp, mean, root):
    link(nc.vector.tensor_reduce(mean, x, AX.X, ALU.add))
    link(nc.vector.tensor_scalar(mean, mean, 1.0 / F, None, ALU.mult))
    link(nc.vector.tensor_tensor(x, x, rep(mean, 2, F), ALU.subtract))
    link(nc.vector.tensor_tensor(tmp, x, x, ALU.mult))
    link(nc.vector.tensor_reduce(root, tmp, AX.X, ALU.add))
    link(nc.vector.tensor_scalar(root, root, 1.0 / F, EPS, ALU.mult, ALU.add))
    reciprocal_root(nc, dve, link, s, turn, root)
    link(nc.vector.tensor_tensor(x, x, rep(root, 2, F), ALU.mult))




def one_hot(nc, m, g, j, at):
    return nc.vector.scalar_tensor_tensor(cut(m["onehot"][j % 3][:, :], t=T), rep(m["keys"][:, bass.ds(T * g, T)], 2, P),
                                          m["starts"][:, bass.ds(at, 1)], rep(m["ramp"][:, :], 1, T),
                                          ALU.subtract, ALU.is_equal)


def window_of(nc, eng, m, s, g):
    eng.sem_inc(s["windows"], 1)
    word = eng.value_load(m["window"][0:1, bass.ds(g, 1)], min_val=0, max_val=2 ** 30)
    first = nc.s_assert_within(word & 127, 0, NB - 1, skip_runtime_bounds_check_because="a block's number")
    n = nc.s_assert_within((word >> 7) & 127, 1, NB, skip_runtime_bounds_check_because="a group has one visit or more")
    further = nc.s_assert_within(word >> 14, 0, GROUPS * NB, skip_runtime_bounds_check_because="at most NB visits each")
    return first, n, further


def hot_dve(nc, dve, m, s, g, j):
    first, _, _ = window_of(nc, dve, m, s, g)
    one_hot(nc, m, g, j, first).then_inc(s["first_hot"], 1)


def visits_dve(nc, dve, m, s, g, j, acc, width):
    first, n, further = window_of(nc, dve, m, s, g)
    before = further + g

    def add(k, at):
        dve.wait_ge(s["summed"], ONE + before + k + 1)
        block = acc[:, bass.ds(at * width, width)]
        nc.vector.tensor_tensor(block, block, m["ps"][7][:, 0:width], ALU.add).then_inc(s["added"], 1)

    add(0, first)
    with dve.If(n > 1), dve.Fori(1, n) as k:
        at = nc.s_assert_within(first + k, 0, NB - 1, skip_runtime_bounds_check_because="first + n <= NB")
        one_hot(nc, m, g, j, at).then_inc(s["more_hot"], 1)
        add(k, at)


def sums_done(nc, dve, m, s):
    _, n, further = window_of(nc, dve, m, s, GROUPS - 1)
    before = further + GROUPS - 1
    dve.wait_ge(s["added"], ONE + before + n)


def visits_pe(nc, pe, m, s, g, j, rows, width):
    _, n, further = window_of(nc, pe, m, s, g)
    before = further + g

    def product(k):
        pe.wait_ge(s["added"], ONE + before + k)
        for t in range(T):
            mm = nc.tensor.matmul(m["ps"][7][:, 0:width], m["onehot"][j % 3][:, t * P:(t + 1) * P], rows[:, t, :],
                                  start=t == 0, stop=t == T - 1)
        mm.then_inc(s["summed"], 1)

    pe.wait_ge(s["first_hot"], ONE + g + 1)
    product(0)
    with pe.If(n > 1), pe.Fori(1, n) as k:
        pe.wait_ge(s["more_hot"], ONE + further + k)
        product(k)


def in_turn(eng, ahead, behind, own=lambda i, j: None, peeled=0):
    def turn(i, last):
        for j in range(SLOTS):
            own(i, j)
            if not (last and j == SLOTS - 1):
                ahead(i + (j + 1) // SLOTS, (j + 1) % SLOTS)
            behind(i, j)
    ahead(0, 0)
    for i in range(peeled):
        turn(i, False)
    with eng.Fori(peeled, ITERS - 1) as i:
        turn(i, False)
    turn(ITERS - 1, True)


def stage_windows(nc, m, of_pairs, s):
    with nc.Block() as block:

        @block.vector
        def _(dve):
            link = Chain(dve, s["step"])
            keys_int = m["keys_int"][:, :]
            dve.wait_ge(s["loaded"], 16 * SLOTS if of_pairs else 16)
            if of_pairs:
                link(nc.vector.tensor_copy(keys_int, m["pairs_in"][:, :].rearrange("p (c k) -> p c k", k=2)[:, :, 0]))
            link(nc.vector.tensor_single_scalar(m["ints"][:, :], keys_int, 7, ALU.arith_shift_right))
            link(nc.vector.tensor_copy(m["floats"][:, :], m["ints"][:, :]))
            link(nc.vector.tensor_copy(m["keys"][:, :], keys_int))
            grouped = m["floats"][:, :].rearrange("p (g t) -> p g t", t=T)
            nc.vector.tensor_reduce(m["least"][:, :], grouped, AX.X, ALU.min)
            link(nc.vector.tensor_reduce(m["most"][:, :], grouped, AX.X, ALU.max))
            nc.vector.nop().then_inc(s["extremes"], 1)
            dve.wait_ge(s["turned"], ONE + 1)
            for c in range(SLOTS):
                nc.vector.tensor_reduce(m["win"][0:GC, 3 * c + 1:3 * c + 2], m["ps"][c][0:GC, 0:P], AX.X, ALU.min)
                link(nc.vector.tensor_reduce(m["wide"][0:GC, c:c + 1], m["ps"][c][0:GC, P:2 * P], AX.X, ALU.max))
            firsts = m["win"][0:GC, :].rearrange("q (c w) -> q c w", w=3)[:, :, 1]
            counts = m["win"][0:GC, :].rearrange("q (c w) -> q c w", w=3)[:, :, 0]
            link(nc.vector.tensor_tensor(m["wide"][0:GC, :], m["wide"][0:GC, :], firsts, ALU.subtract))
            link(nc.vector.tensor_scalar(counts, m["wide"][0:GC, :], 1.0, None, ALU.add))
            nc.vector.nop().then_inc(s["counted"], 1)
            dve.wait_ge(s["prefixed"], ONE + 1)
            link(nc.vector.tensor_copy(m["wide"][0:GC, :], m["ps"][6][0:GC, 0:SLOTS]))
            for c in range(SLOTS):
                before = m["win"][0:GC, 3 * c + 2:3 * c + 3]
                link(nc.vector.tensor_copy(before, m["ps"][5][0:GC, c:c + 1]))
                for k in range(c):
                    link(nc.vector.tensor_tensor(before, before, m["wide"][0:GC, k:k + 1], ALU.add))
            link(nc.vector.tensor_copy(m["win_int"][0:GC, :], m["win"][0:GC, :]))
            table = m["win_int"][0:GC, :].rearrange("q (c w) -> q c w", w=3)
            link(nc.vector.tensor_single_scalar(table[:, :, 2], table[:, :, 2], 14, ALU.logical_shift_left))
            link(nc.vector.tensor_single_scalar(table[:, :, 0], table[:, :, 0], 7, ALU.logical_shift_left))
            link(nc.vector.tensor_tensor(table[:, :, 0], table[:, :, 0], table[:, :, 1], ALU.bitwise_or))
            nc.vector.tensor_tensor(m["words"][0:GC, :], table[:, :, 0], table[:, :, 2], ALU.bitwise_or).then_inc(s["tabled"], 1)

        @block.tensor
        def _(pe):
            pe.wait_ge(s["extremes"], ONE + 1)
            for c in range(SLOTS):
                cols = slice(c * GC, (c + 1) * GC)
                nc.tensor.transpose(m["ps"][c][0:GC, 0:P], m["least"][:, cols], m["ident"][:, :])
                mm = nc.tensor.transpose(m["ps"][c][0:GC, P:2 * P], m["most"][:, cols], m["ident"][:, :])
            mm.then_inc(s["turned"], 1)
            pe.wait_ge(s["counted"], ONE + 1)
            nc.tensor.matmul(m["ps"][5][0:GC, 0:SLOTS], m["before"][0:GC, 0:GC], m["wide"][0:GC, :], start=True, stop=True)
            nc.tensor.matmul(m["ps"][6][0:GC, 0:SLOTS], m["ones"][0:GC, 0:GC], m["wide"][0:GC, :],
                             start=True, stop=True).then_inc(s["prefixed"], 1)

        @block.sync
        def _(sp):
            if of_pairs:
                with sp.Fori(0, SLOTS) as c:
                    sp.dma_start(m["pairs_in"][:, bass.ds(c * GC * 2 * T, GC * 2 * T)].rearrange("p (g k) -> p g k", g=GC),
                                 m["sorted_pairs"].rearrange("(g p t) k -> p g (t k)", p=P, t=T)[:, bass.ds(c * GC, GC), :]
                                 ).then_inc(s["loaded"], 16)
            else:
                sp.dma_start(m["keys_int"][:, :], m["dst"]).then_inc(s["loaded"], 16)
            sp.wait_ge(s["tabled"], ONE + 1)
            sp.dma_start(m["window_dram"].rearrange("(c q) w -> q (c w)", q=GC), m["words"][0:GC, :],
                         allow_slow_non_contiguous=True).then_inc(s["stored"], 16)
            sp.wait_ge(s["stored"], 16)
            sp.dma_start(m["window"][0:1, :], m["window_dram"].rearrange("g w -> (g w)").unsqueeze(0)).then_inc(s["stored"], 16)
            sp.wait_ge(s["stored"], 32)


def stage_setup(nc, m, s):
    with nc.Block() as block:

        @block.sync
        def _(sp):
            sp.dma_start(m["src_int"][:, :], m["src"]).then_inc(s["loaded"], 16)
            sp.dma_start(m["x"][:, :], m["x_in"]).then_inc(s["x_loaded"], 16)
            sp.wait_ge(s["x_loaded"], 16)
            with sp.Fori(0, ITERS) as i:
                for j in range(SLOTS):
                    sp.wait_ge(s["attr_used"][j], ONE + i)
                    sp.dma_start(m["attr"][j][:, :], m["edge_attr"][:, bass.ds((SLOTS * i + j) * T * F, T * F)]
                                 ).then_inc(s["attr_in"][j], 16)

        @block.scalar
        def _(act):
            with act.Fori(0, ITERS) as i:
                for j in range(SLOTS):
                    act.wait_ge(s["attr_in"][j], 16 * (i + 1))
                    act.wait_ge(s["attr_used"][j], ONE + i)
                    nc.scalar.square(m["attr_square"][j][:, :], m["attr"][j][:, :]).then_inc(s["squared"], 1)

        @block.gpsimd
        def _(pool):
            nc.gpsimd.iota(m["ramp"][:, :], [[1, P]], base=0, channel_multiplier=0,
                           allow_small_or_imprecise_dtypes=True).then_inc(s["iota"], 1)
            nc.gpsimd.iota(m["starts"][:, :], [[P, NB]], base=0, channel_multiplier=0,
                           allow_small_or_imprecise_dtypes=True).then_inc(s["iota"], 1)
            nc.gpsimd.iota(m["part"][:, :], [[0, 1]], base=0, channel_multiplier=1,
                           allow_small_or_imprecise_dtypes=True).then_inc(s["iota"], 1)

        @block.vector
        def _(dve):
            link = Chain(dve, s["step"])
            nc.vector.memset(m["ones"][:, :], 1.0)
            nc.vector.memset(m["zero_row"][:, :], 0.0)
            nc.vector.memset(m["zeros"][:, :], 0.0).then_inc(s["zero"], 1)
            dve.wait_ge(s["iota"], ONE + 3)
            nc.vector.tensor_scalar(m["ident"][:, :], m["ramp"][:, :], m["part"][:, :], None, ALU.is_equal)
            nc.vector.tensor_scalar(m["before"][:, :], m["ramp"][:, :], m["part"][:, :], None, ALU.is_gt)
            dve.wait_ge(s["loaded"], 16)
            link(nc.vector.tensor_single_scalar(m["ints"][:, :], m["src_int"][:, :], P - 1, ALU.bitwise_and))
            link(nc.vector.tensor_copy(m["low"][:, :], m["ints"][:, :]))
            link(nc.vector.tensor_single_scalar(m["ints"][:, :], m["src_int"][:, :], 7, ALU.arith_shift_right))
            link(nc.vector.tensor_copy(m["high"][:, :], m["ints"][:, :]))
            with dve.Fori(0, ITERS) as i:
                for j in range(SLOTS):
                    dve.wait_ge(s["counted"][j], ONE + i)
                    cols = bass.ds((SLOTS * i + j) * T, T)
                    nc.vector.tensor_tensor(cut(m["hot_low"][j][:, :], t=T), rep(m["low"][:, cols], 2, P),
                                            rep(m["ramp"][:, :], 1, T), ALU.is_equal)
                    nc.vector.tensor_tensor(cut(m["hot_high"][j][:, :], t=T), rep(m["high"][:, cols], 2, NB),
                                            rep(m["ramp"][:, 0:NB], 1, T), ALU.is_equal).then_inc(s["hot"], 1)
            dve.wait_ge(s["histogram"], ONE + 1)
            nc.vector.tensor_copy(m["out_deg"][:, :], m["ps"][0][:, 0:NB])
            by_feature = lambda bank: bank[:, 0:T * F].rearrange("p (t f) -> p f t", f=F)
            nc.vector.tensor_reduce(m["attr_sum"][:, 0:F], by_feature(m["ps"][1]), AX.X, ALU.add)
            nc.vector.tensor_reduce(m["attr_sum"][:, F:2 * F], by_feature(m["ps"][2]), AX.X, ALU.add)

        @block.tensor
        def _(pe):
            pe.wait_ge(s["zero"], ONE + 1)
            for k in (1, 2):
                nc.tensor.matmul(m["ps"][k][:, 0:T * F], m["zeros"][:, :], m["zero_row"][:, 0:T * F], start=True, stop=False,
                                 skip_group_check=True)
            nc.tensor.matmul(m["ps"][0][:, 0:NB], m["zeros"][:, :], m["zeros"][:, 0:NB], start=True, stop=False, skip_group_check=True)
            with pe.Fori(0, ITERS) as i:
                for j in range(SLOTS):
                    pe.wait_ge(s["hot"], ONE + SLOTS * i + j + 1)
                    for t in range(T):
                        mm = nc.tensor.matmul(m["ps"][0][:, 0:NB], m["hot_low"][j][:, t * P:(t + 1) * P],
                                              m["hot_high"][j][:, t * NB:(t + 1) * NB],
                                              start=False, stop=False, skip_group_check=True)
                    mm.then_inc(s["counted"][j], 1)
                    pe.wait_ge(s["squared"], ONE + SLOTS * i + j + 1)
                    nc.tensor.matmul(m["ps"][1][:, 0:T * F], m["ones"][:, :], m["attr"][j][:, :],
                                     start=False, stop=False, skip_group_check=True)
                    nc.tensor.matmul(m["ps"][2][:, 0:T * F], m["ones"][:, :], m["attr_square"][j][:, :],
                                     start=False, stop=False, skip_group_check=True).then_inc(s["attr_used"][j], 1)
            nc.tensor.matmul(m["ps"][0][:, 0:NB], m["zeros"][:, :], m["zeros"][:, 0:NB], start=False, stop=True,
                             skip_group_check=True).then_inc(s["histogram"], 1)


def stage_convolve(nc, m, s):
    W = F + 1
    x = m["x"][:, :].rearrange("p (b f) -> p b f", f=F)
    with nc.Block() as block:

        @block.vector
        def _(dve):
            link = Chain(dve, s["step"])
            link(nc.vector.tensor_scalar(m["root"][:, :], m["out_deg"][:, :], 1.0, None, ALU.max))
            reciprocal_root(nc, dve, link, s, 1, m["root"][:, :])
            nc.vector.tensor_tensor(m["tmp"][:, :].rearrange("p (b f) -> p b f", f=F), x, rep(m["root"][:, :], 2, F),
                                    ALU.mult).then_inc(s["scaled"], 1)
            link(nc.vector.memset(m["acc"][:, 0:NB * W], 0.0))
            for j in range(SLOTS):
                nc.vector.memset(m["rows"][j][:, :], 1.0).then_inc(s["cleared"], 1)

            def sums(i, j):
                visits_dve(nc, dve, m, s, SLOTS * i + j, j, m["acc"], W)
                nc.vector.nop().then_inc(s["used"][j], 1)
            in_turn(dve, lambda i, j: hot_dve(nc, dve, m, s, SLOTS * i + j, j), sums)
            sums_done(nc, dve, m, s)
            dve.wait_ge(s["stored"], 16)
            acc = m["acc"][:, 0:NB * W].rearrange("p (b w) -> p b w", w=W)
            link(nc.vector.tensor_copy(m["in_deg"][:, :], acc[:, :, F]))
            link(nc.vector.tensor_scalar(m["root"][:, :], m["in_deg"][:, :], 1.0, None, ALU.max))
            reciprocal_root(nc, dve, link, s, 2, m["root"][:, :])
            tmp = m["tmp"][:, :].rearrange("p (b f) -> p b f", f=F)
            link(nc.vector.tensor_tensor(tmp, acc[:, :, 0:F], rep(m["root"][:, :], 2, F), ALU.mult))
            link(nc.vector.tensor_tensor(x, x, tmp, ALU.add))
            layer_norm(nc, dve, link, s, 3, x, tmp, m["mean"][:, :], m["root"][:, :])

        @block.scalar
        def _(act):
            roots_act(nc, act, s, 3, m["root"][:, :])

        @block.tensor
        def _(pe):
            with pe.Fori(0, ITERS) as i:
                for j in range(SLOTS):
                    pe.wait_ge(s["gathered"][j], 16 * T * (i + 1))
                    visits_pe(nc, pe, m, s, SLOTS * i + j, j, m["rows"][j][:, 0:T * W].rearrange("p (t w) -> p t w", w=W), W)

        @block.sync
        def _(sp):
            sp.wait_ge(s["scaled"], ONE + 1)
            sp.dma_start(m["x_table"].rearrange("(b p) f -> p b f", p=P),
                         m["tmp"][:, :].rearrange("p (b f) -> p b f", f=F)).then_inc(s["stored"], 16)
            with sp.Fori(0, ITERS) as i:
                for j in range(SLOTS):
                    sp.wait_ge(s["used"][j], ONE + i)
                    sp.dma_start(m["index"][j][:, :], m["src"][:, bass.ds((SLOTS * i + j) * T, T)]).then_inc(s["indexed"][j], 16)
            sp.wait_ge(s["stored"], 16)

        @block.gpsimd
        def _(pool):
            pool.wait_ge(s["stored"], 16)
            pool.wait_ge(s["cleared"], ONE + SLOTS)
            with pool.Fori(0, ITERS) as i:
                for j in range(SLOTS):
                    pool.wait_ge(s["indexed"][j], 16 * (i + 1))
                    pool.wait_ge(s["used"][j], ONE + i)
                    pool.sem_inc(s["going"], 1)
                    for t in range(T):
                        nc.gpsimd.indirect_dma_start(
                            out=m["rows"][j][:, t * W:t * W + F], out_offset=None, in_=m["x_table"],
                            in_offset=bass.IndirectOffsetOnAxis(ap=m["index"][j][:, t:t + 1], axis=0),
                        ).then_inc(s["gathered"][j], 16)


H = 64
W96 = F + H
CHUNK = 500
NCHUNKS = N // CHUNK
SLOPE = 0.1


def norm_columns(nc, dve, link, s, turn, c, count, gain, shift_in, d):
    mean, var, scale, shift = (c[0:d, k:k + 1] for k in range(4))
    if count:
        link(nc.vector.tensor_scalar(c[0:d, 0:2], c[0:d, 0:2], 1.0 / count, None, ALU.mult))
        link(nc.vector.tensor_tensor(scale, mean, mean, ALU.mult))
        link(nc.vector.tensor_tensor(var, var, scale, ALU.subtract))
        link(nc.vector.tensor_scalar(var, var, 0.0, None, ALU.max))
    link(nc.vector.tensor_scalar(var, var, EPS, None, ALU.add))
    reciprocal_root(nc, dve, link, s, turn, var)
    link(nc.vector.tensor_tensor(scale, gain, var, ALU.mult))
    link(nc.vector.tensor_tensor(var, mean, scale, ALU.mult))
    link(nc.vector.tensor_tensor(shift, shift_in, var, ALU.subtract))


def stage_edges_first(nc, m, s):
    x = m["x"][:, :].rearrange("p (b f) -> p b f", f=F)
    tmp = m["tmp"][:, :].rearrange("p (b f) -> p b f", f=F)
    with nc.Block() as block:

        @block.sync
        def _(sp):
            sp.dma_start(m["x_table"].rearrange("(b p) f -> p b f", p=P), x).then_inc(s["stored"], 16)
            for k, name in enumerate(("m1_w1", "m1_c1", "m1_g1", "m1_b1")):
                sp.dma_start(m["sb_" + name][:, :], m[name]).then_inc(s["weights"], 16)
            with sp.Fori(0, ITERS) as i:
                for j in range(SLOTS):
                    g = SLOTS * i + j
                    sp.wait_ge(s["turned"][j], ONE + i)
                    sp.dma_start(m["index"][j][:, :], m["src"][:, bass.ds(g * T, T)]).then_inc(s["indexed"][j], 16)
                    sp.dma_start(cut(m["rows"][j][:, :], t=T)[:, :, F:C2],
                                 cut(m["edge_attr"][:, bass.ds(g * T * F, T * F)], t=T)).then_inc(s["attr_in"][j], 16)
            sp.wait_ge(s["stored"], 16)

        @block.gpsimd
        def _(pool):
            pool.wait_ge(s["stored"], 16)
            with pool.Fori(0, ITERS) as i:
                for j in range(SLOTS):
                    pool.wait_ge(s["indexed"][j], 16 * (i + 1))
                    pool.wait_ge(s["turned"][j], ONE + i)
                    pool.sem_inc(s["going"], 1)
                    for t in range(T):
                        nc.gpsimd.indirect_dma_start(
                            out=m["rows"][j][:, t * C2:t * C2 + F], out_offset=None, in_=m["x_table"],
                            in_offset=bass.IndirectOffsetOnAxis(ap=m["index"][j][:, t:t + 1], axis=0),
                        ).then_inc(s["gathered"][j], 16)

        @block.vector
        def _(dve):
            link = Chain(dve, s["step"])
            link(nc.vector.tensor_tensor(tmp, x, rep(m["out_deg"][:, :], 2, F), ALU.mult))
            link(nc.vector.tensor_reduce(m["sums"][:, 0:F], m["tmp"][:, :].rearrange("p (b f) -> p f b", f=F), AX.X, ALU.add))
            link(nc.vector.tensor_tensor(tmp, tmp, x, ALU.mult))
            nc.vector.tensor_reduce(m["sums"][:, F:C2], m["tmp"][:, :].rearrange("p (b f) -> p f b", f=F), AX.X,
                                    ALU.add).then_inc(s["node_sums"], 1)
            dve.wait_ge(s["totals"], ONE + 1)
            for k in range(2):
                row = m["total_row"][0:1, k * C2:(k + 1) * C2]
                nc.vector.tensor_copy(row[:, 0:F], m["ps"][0][0:1, k * F:(k + 1) * F])
                ins = nc.vector.tensor_copy(row[:, F:C2], m["attr_sum"][0:1, k * F:(k + 1) * F])
            ins.then_inc(s["rowed"], 1)
            dve.wait_ge(s["columns"], ONE + 1)
            link(nc.vector.tensor_copy(m["bn"][0:C2, 0:2], m["ps"][0][0:C2, 0:2]))
            dve.wait_ge(s["weights"], 64)
            norm_columns(nc, dve, link, s, 1, m["bn"], E, m["sb_m1_g1"][:, :], m["sb_m1_b1"][:, :], C2)
            nc.vector.tensor_scalar(m["w"][0:C2, 0:H], m["sb_m1_w1"][:, :], m["bn"][0:C2, 2:3], None, ALU.mult).then_inc(s["folded"], 1)
            dve.wait_ge(s["shifted"], ONE + 1)
            nc.vector.tensor_tensor(m["bias"][0:H, :], m["sb_m1_c1"][:, :], m["ps"][0][0:H, 0:1], ALU.add).then_inc(s["biased"], 1)
            with dve.Fori(0, ITERS) as i:
                for j in range(SLOTS):
                    g = SLOTS * i + j
                    dve.wait_ge(s["turned"][j], ONE + i + 1)
                    dve.wait_ge(s["multiplied"], ONE + g)
                    nc.vector.tensor_copy(m["flipped"][:, 0:512], m["ps"][0][0:C2, :])
                    nc.vector.tensor_copy(m["flipped"][:, 512:], m["ps"][1][0:C2, 0:P]).then_inc(s["flipped"], 1)
                    dve.wait_ge(s["lifted"], ONE + g + 1)
                    dve.wait_ge(s["a1_out"][j], FULL + 16 * i)
                    a1 = m["a1"][j]
                    nc.vector.scalar_tensor_tensor(a1[:, :], m["lift"][j % 2][:, :], SLOPE, m["lift"][j % 2][:, :],
                                                   ALU.mult, ALU.max).then_inc(s["a1_made"], 1)
                    dve.wait_ge(s["a1_made"], ONE + g + 1)
                    nc.vector.bn_stats(m["stats"][:, bass.ds(g * 12, 6)], a1[:, 0:512])
                    nc.vector.bn_stats(m["stats"][:, bass.ds(g * 12 + 6, 6)], a1[:, 512:]).then_inc(s["counted"], 1)
            dve.wait_ge(s["counted"], ONE + GROUPS)
            nc.vector.bn_aggr(m["a1_stats"][0:H, 0:2], m["stats"][:, :])

        @block.scalar
        def _(act):
            roots_act(nc, act, s, 1, m["bn"][0:C2, 1:2])
            act.wait_ge(s["biased"], ONE + 1)
            with act.Fori(0, ITERS) as i:
                for j in range(SLOTS):
                    g = SLOTS * i + j
                    act.wait_ge(s["multiplied"], ONE + g + 1)
                    act.wait_ge(s["a1_made"], ONE + (g if j == 0 else SLOTS * i + j - 1))
                    nc.scalar.activation(m["lift"][j % 2][:, 0:512], m["ps"][2][0:H, :], ACT.Identity, bias=m["bias"][0:H, :])
                    nc.scalar.activation(m["lift"][j % 2][:, 512:], m["ps"][3][0:H, 0:P], ACT.Identity,
                                         bias=m["bias"][0:H, :]).then_inc(s["lifted"], 1)
                    act.wait_ge(s["a1_made"], ONE + g + 1)
                    act.dma_start(m["a1_dram"][bass.ds(g, 1)].rearrange("g h e -> (g h) e"), m["a1"][j][:, :]).then_inc(s["a1_out"][j], 16)
            for j in range(SLOTS):
                act.wait_ge(s["a1_out"][j], FULL + 16 * ITERS)

        @block.tensor
        def _(pe):
            pe.wait_ge(s["node_sums"], ONE + 1)
            nc.tensor.matmul(m["ps"][0][:, 0:C2], m["ones"][:, :], m["sums"][:, :], start=True, stop=True).then_inc(s["totals"], 1)
            pe.wait_ge(s["rowed"], ONE + 1)
            for k in range(2):
                mm = nc.tensor.matmul(m["ps"][0][0:C2, k:k + 1], m["total_row"][0:1, k * C2:(k + 1) * C2], m["ones"][0:1, 0:1],
                                      start=True, stop=True)
            mm.then_inc(s["columns"], 1)
            pe.wait_ge(s["folded"], ONE + 1)
            nc.tensor.matmul(m["ps"][0][0:H, 0:1], m["sb_m1_w1"][:, :], m["bn"][0:C2, 3:4], start=True, stop=True).then_inc(s["shifted"], 1)
            pe.wait_ge(s["biased"], ONE + 1)
            with pe.Fori(0, ITERS) as i:
                for j in range(SLOTS):
                    g = SLOTS * i + j
                    pe.wait_ge(s["gathered"][j], 16 * T * (i + 1))
                    pe.wait_ge(s["attr_in"][j], 16 * (i + 1))
                    pe.wait_ge(s["flipped"], ONE + g)
                    pe.sem_inc(s["going"], 1)
                    for t in range(T):
                        to = m["ps"][t // 4][0:C2, (t % 4) * P:(t % 4 + 1) * P]
                        mm = nc.tensor.transpose(to, m["rows"][j][:, t * C2:(t + 1) * C2], m["ident"][:, :])
                    mm.then_inc(s["turned"][j], 1)
                    pe.wait_ge(s["flipped"], ONE + g + 1)
                    pe.wait_ge(s["lifted"], ONE + g)
                    pe.sem_inc(s["going"], 1)
                    nc.tensor.matmul(m["ps"][2][0:H, :], m["w"][0:C2, 0:H], m["flipped"][:, 0:512], start=True, stop=True)
                    nc.tensor.matmul(m["ps"][3][0:H, 0:P], m["w"][0:C2, 0:H], m["flipped"][:, 512:],
                                     start=True, stop=True).then_inc(s["multiplied"], 1)




def sort_begin_dve(nc, dve, link, m, s):
    dve.wait_ge(s["loaded"], 16)
    link(nc.vector.tensor_copy(m["src_float"][:, :], m["src_int"][:, :]))
    link(nc.vector.tensor_single_scalar(m["ints"][:, :], m["src_int"][:, :], P - 1, ALU.bitwise_and))
    link(nc.vector.tensor_copy(m["low"][:, :], m["ints"][:, :]))
    link(nc.vector.tensor_single_scalar(m["ints"][:, :], m["src_int"][:, :], 7, ALU.arith_shift_right))
    link(nc.vector.tensor_copy(m["high"][:, :], m["ints"][:, :]))
    link(nc.vector.tensor_copy(m["ident_half"][:, :], m["ident"][:, :]))
    dve.wait_ge(s["sums"], ONE + 1)
    nc.vector.tensor_copy(m["sums"][0:NB, :], m["ps"][5][0:NB, 0:P]).then_inc(s["sums_out"], 1)
    dve.wait_ge(s["counts_out"], ONE + 1)
    first = m["first_float"][:, :]
    link(nc.vector.tensor_scalar(first, m["starts"][:, :], m["part"][:, :], float(E), ALU.add, ALU.add))
    link(nc.vector.tensor_tensor(first, first, m["counts"][:, :], ALU.subtract))
    link(nc.vector.scalar_tensor_tensor(first, m["out_deg"][:, :], 0.0, first, ALU.is_equal, ALU.mult))
    link(nc.vector.tensor_tensor(first, first, m["counts"][:, :], ALU.add))
    link(nc.vector.tensor_copy(m["first_place"][:, :], first))


def sort_begin_pe(nc, pe, m, s):
    nc.tensor.matmul(m["ps"][5][0:NB, 0:P], m["out_deg"][:, :], m["ones"][:, :], start=True, stop=True).then_inc(s["sums"], 1)
    nc.tensor.matmul(m["ps"][3][:, 0:NB], m["before"][:, :], m["out_deg"][:, :], start=True, stop=False, skip_group_check=True)
    pe.wait_ge(s["sums_out"], ONE + 1)
    nc.tensor.matmul(m["ps"][3][:, 0:NB], m["sums"][0:NB, :], m["before"][0:NB, 0:NB], start=False, stop=False,
                     skip_group_check=True).then_inc(s["begun"], 1)


def sort_rows_dve(nc, dve, m, s, i, j):
    g = SLOTS * i + j
    cols = bass.ds(g * T, T)
    dve.wait_ge(s["placed"][j], ONE + i)
    nc.vector.tensor_tensor(cut(m["hot_low"][j][:, :], t=T), rep(m["low"][:, cols], 2, P),
                            rep(m["ramp"][:, :], 1, T), ALU.is_equal).then_inc(s["hot_lows"], 1)
    nc.vector.tensor_tensor(cut(m["hot_high"][j][:, :], t=T), rep(m["high"][:, cols], 2, NB),
                            rep(m["ramp"][:, 0:NB], 1, T), ALU.is_equal).then_inc(s["hot_highs"], 1)
    dve.wait_ge(s["row_in"][j], 16 * (i + 1))
    for t in range(T):
        ins = nc.vector.scalar_tensor_tensor(
            m["same"][j][:, t * P:(t + 1) * P], m["src_row"][j][:, t * P:(t + 1) * P],
            m["src_float"][:, bass.ds(g * T + t, 1)], m["before"][:, :], ALU.is_equal, ALU.mult)
    ins.then_inc(s["compared"][j], 1)


def sort_pick_dve(nc, dve, m, s, i, j, t):
    dve.wait_ge(s["looked"], ONE + (SLOTS * i + j) * T + t + 1)
    nc.vector.tensor_tensor_reduce(
        m["picked"][:, t * NB:(t + 1) * NB], m["ps"][5 + t % 2][:, 0:NB], m["hot_high"][j][:, t * NB:(t + 1) * NB], 1.0, 0.0,
        ALU.mult, ALU.add, m["place"][j][:, t:t + 1]).then_inc(s["picked"], 1)


def sort_place_dve(nc, dve, m, s, i, j):
    dve.wait_ge(s["picked"], ONE + (SLOTS * i + j + 1) * T)
    dve.wait_ge(s["freed"][j], ONE + i)
    nc.vector.tensor_copy(m["place_int"][j][:, :], m["place"][j][:, :]).then_inc(s["placed"][j], 1)


def sort_turn_pe(nc, pe, m, s, i, j):
    g = SLOTS * i + j
    pe.wait_ge(s["hot_lows"], ONE + g + 1)
    pe.wait_ge(s["turned_out"], ONE + g)
    for t in range(T):
        mm = nc.tensor.transpose(m["ps_turn"][:, t * P:(t + 1) * P], m["hot_low"][j][:, t * P:(t + 1) * P],
                                 m["ident_half"][:, :])
    mm.then_inc(s["turned"], 1)


def sort_tile_pe(nc, pe, m, s, i, j, t):
    g = SLOTS * i + j
    if t == 0:
        pe.wait_ge(s["hot_highs"], ONE + g + 1)
        pe.wait_ge(s["compared"][j], ONE + i + 1)
        pe.wait_ge(s["turned_out"], ONE + g + 1)
    look, tile = m["ps"][5 + t % 2][:, 0:NB], slice(t * P, (t + 1) * P)
    high = m["hot_high"][j][:, t * NB:(t + 1) * NB]
    pe.wait_ge(s["picked"], ONE + g * T + max(t - 1, 0))
    nc.tensor.matmul(look, m["same"][j][:, tile], high, start=True, stop=False)
    pe.wait_ge(s["counts_out"], ONE + g * T + t + 1)
    nc.tensor.matmul(look, m["turned"][:, tile], m["counts"][:, :], start=False, stop=True).then_inc(s["looked"], 1)
    nc.tensor.matmul(m["ps"][3][:, 0:NB], m["hot_low"][j][:, tile], high, start=False, stop=False,
                     skip_group_check=True).then_inc(s["counted"], 1)


def stage_edges_second_and_sort(nc, m, s):
    W = H + 1
    with nc.Block() as block:

        @block.sync
        def _(sp):
            sp.dma_start(m["src_int"][:, :], m["src"]).then_inc(s["loaded"], 16)
            for name in ("m1_w2", "m1_g2", "m1_b2"):
                sp.dma_start(m["sb_" + name][:, :], m[name]).then_inc(s["weights"], 16)
            sp.dma_start(m["sb_m1_c2"][:, :], m["m1_c2"].broadcast_to([P, H])).then_inc(s["weights"], 16)
            with sp.Fori(0, ITERS) as i:
                for j in range(SLOTS):
                    g = SLOTS * i + j
                    sp.wait_ge(s["products"][j], ONE + i)
                    sp.dma_start(m["a1"][j][:, :], m["a1_dram"][bass.ds(g, 1)].rearrange("g h e -> (g h) e")
                                 ).then_inc(s["a1_in"][j], 16)
                    sp.wait_ge(s["compared"][j], ONE + i)
                    sp.dma_start(m["src_row"][j][:, :],
                                 m["src_rows"][bass.ds(g, 1), :].broadcast_to([P, T * P])).then_inc(s["row_in"][j], 16)
                    sp.wait_ge(s["freed"][j], ONE + i)
                    sp.dma_start(m["pair"][j][:, :], m["pairs"][:, bass.ds(g * 2 * T, 2 * T)]).then_inc(s["pair_in"][j], 16)

        @block.scalar
        def _(act):
            act.wait_ge(s["begun"], ONE + 1)
            nc.scalar.copy(m["counts"][:, :], m["ps"][3][:, 0:NB]).then_inc(s["counts_out"], 1)
            roots_act(nc, act, s, 1, m["a1_stats"][0:H, 1:2])
            with act.Fori(0, ITERS) as i:
                for j in range(SLOTS):
                    g = SLOTS * i + j
                    act.wait_ge(s["turned"], ONE + g + 1)
                    nc.scalar.copy(m["turned"][:, :], m["ps_turn"][:, 0:T * P]).then_inc(s["turned_out"], 1)
                    act.wait_ge(s["a2_made"], ONE + g + 1)
                    act.wait_ge(s["squares_used"], ONE + g)
                    nc.scalar.square(cut(m["squares"][:, :], t=T), cut(m["rows"][j][:, 0:T * W], t=T)[:, :, 0:H]).then_inc(s["squared"], 1)
                    for t in range(T):
                        act.wait_ge(s["counted"], ONE + g * T + t + 1)
                        nc.scalar.copy(m["counts"][:, :], m["ps"][3][:, 0:NB]).then_inc(s["counts_out"], 1)

        @block.vector
        def _(dve):
            link = Chain(dve, s["step"])
            link(nc.vector.memset(m["acc"][:, 0:NB * W], 0.0))
            for j in range(SLOTS):
                link(nc.vector.memset(m["rows"][j][:, 0:T * W], 1.0))
            dve.wait_ge(s["weights"], 64)
            sort_begin_dve(nc, dve, link, m, s)
            norm_columns(nc, dve, link, s, 1, m["a1_stats"], None, m["sb_m1_g2"][:, :], m["sb_m1_b2"][:, :], H)
            link(nc.vector.tensor_scalar(m["w"][0:H, 0:H], m["sb_m1_w2"][:, :], m["a1_stats"][0:H, 2:3], None, ALU.mult))
            nc.vector.tensor_copy(m["wide_shift"][0:H, :], m["a1_stats"][0:H, 3:4].broadcast_to([H, P])).then_inc(s["folded"], 1)
            dve.wait_ge(s["shifted"], ONE + 1)
            link(nc.vector.tensor_tensor(m["bias_row"][:, :], m["sb_m1_c2"][:, :], m["ps"][0][:, 0:H], ALU.add))
            nc.vector.nop().then_inc(s["biased"], 1)

            def ahead(i, j):
                g = SLOTS * i + j
                sort_rows_dve(nc, dve, m, s, i, j)
                dve.wait_ge(s["products"][j], ONE + i + 1)
                dve.wait_ge(s["a2_made"], ONE + g)
                nc.vector.tensor_tensor(cut(m["lift2"][:, :], t=T), cut(m["ps"][j % 2][:, 0:T * H], t=T),
                                        rep(m["bias_row"][:, :], 1, T), ALU.add).then_inc(s["lifted"], 1)
                hot_dve(nc, dve, m, s, g, j)
                dve.wait_ge(s["lifted"], ONE + g + 1)
                lift = cut(m["lift2"][:, :], t=T)
                nc.vector.scalar_tensor_tensor(cut(m["rows"][j][:, 0:T * W], t=T)[:, :, 0:H], lift, SLOPE, lift,
                                               ALU.mult, ALU.max).then_inc(s["a2_made"], 1)

            def behind(i, j):
                for t in range(T):
                    sort_pick_dve(nc, dve, m, s, i, j, t)
                    if t == 1:
                        visits_dve(nc, dve, m, s, SLOTS * i + j, j, m["acc"], W)
                sort_place_dve(nc, dve, m, s, i, j)
            in_turn(dve, ahead, behind)
            sums_done(nc, dve, m, s)
            dve.wait_ge(s["squares_used"], ONE + GROUPS)
            nc.vector.tensor_copy(m["square_sum"][0:H, :], m["ps"][2][0:H, 0:1])

        @block.tensor
        def _(pe):
            sort_begin_pe(nc, pe, m, s)
            pe.wait_ge(s["folded"], ONE + 1)
            nc.tensor.matmul(m["ps"][0][:, 0:H], m["wide_shift"][0:H, :], m["sb_m1_w2"][:, :], start=True, stop=True).then_inc(s["shifted"], 1)
            nc.tensor.matmul(m["ps"][2][0:H, 0:1], m["zeros"][:, 0:H], m["zero_row"][:, 0:1], start=True, stop=False, skip_group_check=True)
            pe.wait_ge(s["biased"], ONE + 1)

            def ahead(i, j):
                pe.wait_ge(s["a1_in"][j], 16 * (i + 1))
                pe.wait_ge(s["lifted"], ONE + (SLOTS * i + max(j - 1, 0)))
                for t in range(T):
                    mm = nc.tensor.matmul(m["ps"][j % 2][:, t * H:(t + 1) * H], m["a1"][j][:, t * P:(t + 1) * P],
                                          m["w"][0:H, 0:H], start=True, stop=True)
                mm.then_inc(s["products"][j], 1)

            def behind(i, j):
                g = SLOTS * i + j
                sort_tile_pe(nc, pe, m, s, i, j, 0)
                pe.wait_ge(s["squared"], ONE + g + 1)
                for t in range(T):
                    mm = nc.tensor.matmul(m["ps"][2][0:H, 0:1], m["squares"][:, t * H:(t + 1) * H], m["ones"][:, 0:1],
                                          start=False, stop=False, skip_group_check=True)
                mm.then_inc(s["squares_used"], 1)
                sort_tile_pe(nc, pe, m, s, i, j, 1)
                pe.wait_ge(s["a2_made"], ONE + g + 1)
                visits_pe(nc, pe, m, s, g, j, cut(m["rows"][j][:, 0:T * W], t=T), W)
                for t in range(2, T):
                    sort_tile_pe(nc, pe, m, s, i, j, t)
            in_turn(pe, ahead, behind, lambda i, j: sort_turn_pe(nc, pe, m, s, i, j))

        @block.gpsimd
        def _(pool):
            with pool.Fori(0, ITERS) as i:
                for j in range(SLOTS):
                    pool.wait_ge(s["placed"][j], ONE + i + 1)
                    pool.wait_ge(s["pair_in"][j], 16 * (i + 1))
                    pool.sem_inc(s["going"], 1)
                    for t in range(T):
                        nc.gpsimd.indirect_dma_start(
                            out=m["sorted_pairs"], out_offset=bass.IndirectOffsetOnAxis(ap=m["place_int"][j][:, t:t + 1], axis=0),
                            in_=m["pair"][j][:, 2 * t:2 * t + 2], in_offset=None,
                        ).then_inc(s["moved"][j], 16)
                    for slot in ([j - 1] if j else []) + ([j] if j == SLOTS - 1 else []):
                        pool.wait_ge(s["moved"][slot], 16 * T * (i + 1))
                        pool.sem_inc(s["freed"][slot], 1)


SLAB = 7
SLABS = NB // SLAB
assert SLABS * SLAB == NB and NCHUNKS * CHUNK == N


def stage_nodes(nc, m, s):
    W = H + 1
    SW = SLAB * P
    with nc.Block() as block:

        @block.sync
        def _(sp):
            for name in m["node_weights"]:
                sp.dma_start(m["sb_" + name][:, :], m[name]).then_inc(s["weights"], 16)
            sp.wait_ge(s["cleared"], ONE + 1)
            sp.dma_start(m["c3_row"][H:H + 1, :], m["m1_c3"]).then_inc(s["weights"], 16)

        @block.scalar
        def _(act):
            roots_act(nc, act, s, 1, m["bn3"][0:H, 1:2])
            with act.Fori(0, SLABS) as i:
                act.wait_ge(s["turned"], ONE + i)
                nc.scalar.copy(m["acc_slab"][:, :], m["acc"][:, bass.ds(i * SLAB * W, SLAB * W)])
                nc.scalar.copy(m["x_slab"][:, :], m["x"][:, bass.ds(i * SLAB * F, SLAB * F)]).then_inc(s["slab"], 1)
            roots = [m["bn_agg"][0:H, 1:2], m["bn_x"][0:F, 1:2], m["bn_h"][0:W96, 1:2], m["bn_h"][0:W96, 1:2]]
            for layer in range(3):
                for turn in ((2, 3), (4,), (5,))[layer]:
                    act.wait_ge(s["to_root"], ONE + turn)
                    nc.scalar.activation(roots[turn - 2], roots[turn - 2], ACT.Sqrt).then_inc(s["rooted"], 1)
                act.wait_ge(s["biased"], ONE + layer + 1)
                with act.Fori(0, NCHUNKS) as c:
                    act.wait_ge(s["product"], ONE + layer * NCHUNKS + c + 1)
                    if layer < 2:
                        act.wait_ge(s["bent"], ONE + layer * NCHUNKS + c)
                        nc.scalar.activation(m["node_lift"][:, :], m["ps"][0][0:W96, 0:CHUNK], ACT.Identity,
                                             bias=m["bias96"][0:W96, :]).then_inc(s["lifted"], 1)
                    else:
                        nc.scalar.activation(m["x_turned"][:, bass.ds(c * CHUNK, CHUNK)], m["ps"][0][0:F, 0:CHUNK],
                                             ACT.Identity, bias=m["bias96"][0:F, :]).then_inc(s["lifted"], 1)
            act.wait_ge(s["lifted"], ONE + 3 * NCHUNKS)
            with act.Fori(0, SLABS) as i:
                act.wait_ge(s["turned_back"], ONE + i)
                nc.scalar.copy(m["out_slab"][:, :], m["x_turned"][:, bass.ds(i * SW, SW)]).then_inc(s["slab"], 1)
            act.wait_ge(s["to_root"], ONE + 6)
            nc.scalar.activation(m["root"][:, :], m["root"][:, :], ACT.Sqrt).then_inc(s["rooted"], 1)

        @block.vector
        def _(dve):
            link = Chain(dve, s["step"])
            nc.vector.memset(m["c3_row"][:, :], 0.0).then_inc(s["cleared"], 1)
            nc.vector.tensor_reduce(m["sums"][:, 0:H], m["acc"][:, :].rearrange("p (b w) -> p w b", w=W)[:, 0:H, :], AX.X,
                                    ALU.add).then_inc(s["summed"], 1)
            dve.wait_ge(s["totals"], ONE + 1)
            link(nc.vector.tensor_copy(m["bn3"][0:H, 0:1], m["ps"][0][0:H, 0:1]))
            link(nc.vector.tensor_copy(m["bn3"][0:H, 1:2], m["square_sum"][0:H, :]))
            dve.wait_ge(s["weights"], 16 * (len(m["node_weights"]) + 1))
            norm_columns(nc, dve, link, s, 1, m["bn3"], E, m["sb_m1_g3"][:, :], m["sb_m1_b3"][:, :], H)
            link(nc.vector.tensor_scalar(m["fold3"][:, 0:H], m["ident"][0:H, 0:H], m["bn3"][0:H, 2:3], None, ALU.mult))
            link(nc.vector.tensor_copy(m["fold3"][:, H:W], m["bn3"][0:H, 3:4]))
            nc.vector.nop().then_inc(s["folded"], 1)
            dve.wait_ge(s["w3_made"], ONE + 1)
            nc.vector.tensor_tensor(m["w3"][0:W, :], m["ps"][0][0:W, 0:H], m["c3_row"][0:W, :], ALU.add).then_inc(s["w3_out"], 1)
            with dve.Fori(0, SLABS) as i:
                dve.wait_ge(s["turned"], ONE + i + 1)
                dve.wait_ge(s["agged"], ONE + i)
                nc.vector.tensor_copy(m["acc_turned"][0:W, 0:512], m["ps"][0][0:W, :])
                nc.vector.tensor_copy(m["acc_turned"][0:W, 512:], m["ps"][1][0:W, 0:SW - 512])
                nc.vector.tensor_copy(m["x_turned"][:, bass.ds(i * SW, 512)], m["ps"][2][0:F, :])
                nc.vector.tensor_copy(m["x_turned"][:, bass.ds(i * SW + 512, SW - 512)], m["ps"][3][0:F, 0:SW - 512]
                                      ).then_inc(s["flipped"], 1)
                dve.wait_ge(s["agged"], ONE + i + 1)
                nc.vector.tensor_copy(m["h"][0:H, bass.ds(i * SW, 512)], m["ps"][4][0:H, :])
                nc.vector.tensor_copy(m["h"][0:H, bass.ds(i * SW + 512, SW - 512)], m["ps"][5][0:H, 0:SW - 512]
                                      ).then_inc(s["agg_out"], 1)
            dve.wait_ge(s["agg_out"], ONE + SLABS)
            with dve.Fori(0, NCHUNKS) as c:
                nc.vector.bn_stats(m["stats"][0:H, bass.ds(c * 6, 6)], m["h"][0:H, bass.ds(c * CHUNK, CHUNK)])
                nc.vector.bn_stats(m["stats_x"][0:F, bass.ds(c * 6, 6)], m["x_turned"][:, bass.ds(c * CHUNK, CHUNK)]
                                   ).then_inc(s["measured"], 1)
            dve.wait_ge(s["measured"], ONE + NCHUNKS)
            link(nc.vector.bn_aggr(m["bn_agg"][0:H, 0:2], m["stats"][0:H, :]))
            link(nc.vector.bn_aggr(m["bn_x"][0:F, 0:2], m["stats_x"][0:F, :]))
            norm_columns(nc, dve, link, s, 2, m["bn_agg"], None, m["sb_m2_g1a"][:, :], m["sb_m2_b1a"][:, :], H)
            norm_columns(nc, dve, link, s, 3, m["bn_x"], None, m["sb_m2_g1x"][:, :], m["sb_m2_b1x"][:, :], F)
            link(nc.vector.tensor_scalar(m["wa"][:, :], m["sb_m2_w1a"][:, :], m["bn_agg"][0:H, 2:3], None, ALU.mult))
            link(nc.vector.tensor_scalar(m["wx"][:, :], m["sb_m2_w1x"][:, :], m["bn_x"][0:F, 2:3], None, ALU.mult))
            nc.vector.nop().then_inc(s["folded"], 1)
            for layer in range(3):
                wide = W96 if layer < 2 else F
                dve.wait_ge(s["shifted"], ONE + layer + 1)
                c_in = (m["sb_m2_c1"], m["sb_m2_c2"], m["sb_m2_c3"])[layer]
                nc.vector.tensor_tensor(m["bias96"][0:wide, :], m["ps"][6][0:wide, 0:1], c_in[:, :], ALU.add).then_inc(s["biased"], 1)
                if layer == 2:
                    break
                with dve.Fori(0, NCHUNKS) as c:
                    n = layer * NCHUNKS + c
                    dve.wait_ge(s["lifted"], ONE + n + 1)
                    here = m["h"][:, bass.ds(c * CHUNK, CHUNK)]
                    nc.vector.scalar_tensor_tensor(here, m["node_lift"][:, :], SLOPE, m["node_lift"][:, :], ALU.mult,
                                                   ALU.max).then_inc(s["bent"], 1)
                    dve.wait_ge(s["bent"], ONE + n + 1)
                    nc.vector.bn_stats(m["stats"][0:W96, bass.ds(c * 6, 6)], here).then_inc(s["measured"], 1)
                dve.wait_ge(s["measured"], ONE + (layer + 2) * NCHUNKS)
                link(nc.vector.bn_aggr(m["bn_h"][0:W96, 0:2], m["stats"][0:W96, :]))
                gain, shift, w = ((m["sb_m2_g2"], m["sb_m2_b2"], m["sb_m2_w2"]), (m["sb_m2_g3"], m["sb_m2_b3"], m["sb_m2_w3"]))[layer]
                norm_columns(nc, dve, link, s, 4 + layer, m["bn_h"], None, gain[:, :], shift[:, :], W96)
                link(nc.vector.tensor_scalar(m["wh"][:, 0:w.shape[1]], w[:, :], m["bn_h"][0:W96, 2:3], None, ALU.mult))
                nc.vector.nop().then_inc(s["folded"], 1)
            with dve.Fori(0, SLABS) as i:
                dve.wait_ge(s["turned_back"], ONE + i + 1)
                here = m["x"][:, bass.ds(i * SLAB * F, SLAB * F)]
                nc.vector.tensor_tensor(here, here, m["ps"][1][:, 0:SLAB * F], ALU.add).then_inc(s["added"], 1)
            dve.wait_ge(s["added"], ONE + SLABS)
            cubed = lambda t: t[:, :].rearrange("p (b f) -> p b f", f=F)
            layer_norm(nc, dve, link, s, 6, cubed(m["x"]), cubed(m["tmp"]), m["mean"][:, :], m["root"][:, :])

        @block.tensor
        def _(pe):
            pe.wait_ge(s["summed"], ONE + 1)
            nc.tensor.matmul(m["ps"][0][0:H, 0:1], m["sums"][:, 0:H], m["ones"][:, 0:1], start=True, stop=True).then_inc(s["totals"], 1)
            pe.wait_ge(s["folded"], ONE + 1)
            nc.tensor.matmul(m["ps"][0][0:W, 0:H], m["fold3"][:, :], m["sb_m1_w3"][:, :], start=True, stop=True).then_inc(s["w3_made"], 1)
            pe.wait_ge(s["w3_out"], ONE + 1)
            with pe.Fori(0, SLABS) as i:
                pe.wait_ge(s["slab"], ONE + i + 1)
                pe.wait_ge(s["flipped"], ONE + i)
                pe.sem_inc(s["going"], 1)
                for b in range(SLAB):
                    cols = slice(b % 4 * P, (b % 4 + 1) * P)
                    nc.tensor.transpose(m["ps"][b // 4][0:W, cols], m["acc_slab"][:, b * W:(b + 1) * W], m["ident"][:, :])
                    mm = nc.tensor.transpose(m["ps"][2 + b // 4][0:F, cols], m["x_slab"][:, b * F:(b + 1) * F], m["ident"][:, :])
                mm.then_inc(s["turned"], 1)
                pe.wait_ge(s["flipped"], ONE + i + 1)
                pe.wait_ge(s["agg_out"], ONE + i)
                pe.sem_inc(s["going"], 1)
                nc.tensor.matmul(m["ps"][4][0:H, :], m["w3"][0:W, :], m["acc_turned"][0:W, 0:512], start=True, stop=True)
                nc.tensor.matmul(m["ps"][5][0:H, 0:SW - 512], m["w3"][0:W, :], m["acc_turned"][0:W, 512:],
                                 start=True, stop=True).then_inc(s["agged"], 1)
            for layer in range(3):
                wide = W96 if layer < 2 else F
                pe.wait_ge(s["folded"], ONE + layer + 2)
                if layer == 0:
                    nc.tensor.matmul(m["ps"][6][0:wide, 0:1], m["sb_m2_w1a"][:, :], m["bn_agg"][0:H, 3:4], start=True, stop=False)
                    mm = nc.tensor.matmul(m["ps"][6][0:wide, 0:1], m["sb_m2_w1x"][:, :], m["bn_x"][0:F, 3:4], start=False, stop=True)
                else:
                    w = (m["sb_m2_w2"], m["sb_m2_w3"])[layer - 1]
                    mm = nc.tensor.matmul(m["ps"][6][0:wide, 0:1], w[:, :], m["bn_h"][0:W96, 3:4], start=True, stop=True)
                mm.then_inc(s["shifted"], 1)
                with pe.Fori(0, NCHUNKS) as c:
                    cols = bass.ds(c * CHUNK, CHUNK)
                    pe.wait_ge(s["lifted"], ONE + layer * NCHUNKS + c)
                    pe.sem_inc(s["going"], 1)
                    to = m["ps"][0][0:wide, 0:CHUNK]
                    if layer == 0:
                        nc.tensor.matmul(to, m["wa"][:, :], m["h"][0:H, cols], start=True, stop=False)
                        mm = nc.tensor.matmul(to, m["wx"][:, :], m["x_turned"][:, cols], start=False, stop=True)
                    else:
                        mm = nc.tensor.matmul(to, m["wh"][:, 0:wide], m["h"][:, cols], start=True, stop=True)
                    mm.then_inc(s["product"], 1)
            with pe.Fori(0, SLABS) as i:
                pe.wait_ge(s["slab"], ONE + SLABS + i + 1)
                pe.wait_ge(s["added"], ONE + i)
                pe.sem_inc(s["going"], 1)
                for b in range(SLAB):
                    mm = nc.tensor.transpose(m["ps"][1][:, b * F:(b + 1) * F], m["out_slab"][:, b * P:(b + 1) * P], m["ident"][0:F, 0:F])
                mm.then_inc(s["turned_back"], 1)


HEADS = 4
XA = F + HEADS
ATT_SLOPE = 0.2
BIG = 1e30


def stage_attention_tables(nc, m, s):
    with nc.Block() as block:

        @block.sync
        def _(sp):
            sp.dma_start(m["sb_w_out"][:, :], m["att_w_out"]).then_inc(s["weights"], 16)
            sp.dma_start(m["sb_fc"][:, :], m["att_fc"]).then_inc(s["weights"], 16)
            sp.dma_start(m["sb_fc_b"][:, :], m["att_fc_b"].broadcast_to([P, 1])).then_inc(s["weights"], 16)
            sp.wait_ge(s["built"], ONE + 2)
            sp.dma_start(m["xa_table"].rearrange("(b p) f -> p b f", p=P), m["xa"][:, :].rearrange("p (b f) -> p b f", f=XA)).then_inc(s["stored"], 16)
            sp.wait_ge(s["blank"], ONE + 1)
            sp.dma_start(m["u_firsts"][0:E, :].rearrange("(p c) h -> p (c h)", p=P), m["logit"][:, :]).then_inc(s["stored"], 16)
            sp.wait_ge(s["stored"], 32)

        @block.tensor
        def _(pe):
            pe.wait_ge(s["weights"], 48)
            for h in range(HEADS):
                mm = nc.tensor.matmul(m["ps"][0][0:F, 2 * h:2 * h + 2], m["sb_w_out"][:, h * F:(h + 1) * F], m["sb_fc"][:, :],
                                      start=True, stop=True)
            mm.then_inc(s["vectors"], 1)
            pe.wait_ge(s["vectors_out"], ONE + 1)
            with pe.Fori(0, SLABS) as i:
                pe.wait_ge(s["slab"], ONE + i + 1)
                pe.wait_ge(s["flipped"], ONE + i)
                pe.sem_inc(s["going"], 1)
                for b in range(SLAB):
                    mm = nc.tensor.transpose(m["ps"][2 + b // 4][0:F, b % 4 * P:(b % 4 + 1) * P],
                                             m["x_slab"][:, b * F:(b + 1) * F], m["ident"][:, :])
                mm.then_inc(s["turned"], 1)
                pe.wait_ge(s["flipped"], ONE + i + 1)
                pe.wait_ge(s["logits_out"], ONE + i)
                pe.sem_inc(s["going"], 1)
                for b in range(SLAB):
                    mm = nc.tensor.matmul(m["ps"][1][:, b * 8:(b + 1) * 8], m["x_turned_slab"][:, b * P:(b + 1) * P], m["vectors"][:, :],
                                          start=True, stop=True)
                mm.then_inc(s["logits"], 1)

        @block.gpsimd
        def _(pool):
            pool.wait_ge(s["stored"], 32)
            pool.sem_inc(s["going_pool"], 1)
            for b in range(NB):
                nc.gpsimd.indirect_dma_start(
                    out=m["u_firsts"], out_offset=bass.IndirectOffsetOnAxis(ap=m["first_place"][:, b:b + 1], axis=0),
                    in_=m["u"][:, b * HEADS:(b + 1) * HEADS], in_offset=None).then_inc(s["moved"], 16)
            pool.wait_ge(s["moved"], 16 * NB)

        @block.scalar
        def _(act):
            with act.Fori(0, SLABS) as i:
                act.wait_ge(s["turned"], ONE + i)
                nc.scalar.copy(m["x_slab"][:, :], m["x"][:, bass.ds(i * SLAB * F, SLAB * F)]).then_inc(s["slab"], 1)
                act.wait_ge(s["turned"], ONE + i + 1)
                act.wait_ge(s["logits"], ONE + i)
                nc.scalar.copy(m["x_turned_slab"][:, 0:512], m["ps"][2][0:F, :])
                nc.scalar.copy(m["x_turned_slab"][:, 512:], m["ps"][3][0:F, 0:SLAB * P - 512]).then_inc(s["flipped"], 1)

        @block.vector
        def _(dve):
            nc.vector.memset(m["logit"][:, :], -BIG).then_inc(s["blank"], 1)
            dve.wait_ge(s["vectors"], ONE + 1)
            nc.vector.tensor_copy(m["vectors"][:, :], m["ps"][0][0:F, 0:8]).then_inc(s["vectors_out"], 1)
            dve.wait_ge(s["weights"], 48)
            with dve.Fori(0, SLABS) as i:
                dve.wait_ge(s["logits"], ONE + i + 1)
                logits = m["ps"][1][:, 0:8 * SLAB].rearrange("p (b h k) -> p b h k", b=SLAB, k=2)
                nc.vector.tensor_scalar(m["u"][:, bass.ds(i * SLAB * HEADS, SLAB * HEADS)].rearrange("p (b h) -> p b h", h=HEADS),
                                        logits[:, :, :, 0], m["sb_fc_b"][:, :], None, ALU.add)
                nc.vector.tensor_copy(m["xa"][:, bass.ds(i * SLAB * XA, SLAB * XA)].rearrange("p (b f) -> p b f", f=XA)[:, :, F:XA],
                                      logits[:, :, :, 1]).then_inc(s["logits_out"], 1)
            dve.wait_ge(s["logits_out"], ONE + SLABS)
            nc.vector.nop().then_inc(s["built"], 1)
            nc.vector.tensor_copy(m["xa"][:, :].rearrange("p (b f) -> p b f", f=XA)[:, :, 0:F],
                                  m["x"][:, :].rearrange("p (b f) -> p b f", f=F)).then_inc(s["built"], 1)


def spread_maxima(nc, link, keys, values, mask, tmp, n, parts, width):
    for back in (False, True):
        d = 1
        while d < n:
            near, far = (slice(0, n - d), slice(d, n)) if back else (slice(d, n), slice(0, n - d))
            link(nc.vector.tensor_tensor(mask[0:parts, 0:n - d], keys[:, near], keys[:, far], ALU.is_equal))
            link(nc.vector.tensor_scalar(mask[0:parts, 0:n - d], mask[0:parts, 0:n - d], 0.5, 2 * BIG, ALU.subtract, ALU.mult))
            for h in range(width):
                link(nc.vector.tensor_tensor(tmp[0:parts, 0:n - d], values[:, far, h], mask[0:parts, 0:n - d], ALU.min))
                link(nc.vector.tensor_tensor(values[:, near, h], values[:, near, h], tmp[0:parts, 0:n - d], ALU.max))
            d *= 2


def run_maxima_pe(nc, pe, m, s):
    pe.wait_ge(s["edged"], ONE + 1)
    for k in range(4):
        mm = nc.tensor.transpose(m["ps"][0][0:HEADS, k * P:(k + 1) * P], m["edge_cols"][:, k * HEADS:(k + 1) * HEADS], m["ident"][:, :])
    mm.then_inc(s["turned"], 1)
    pe.wait_ge(s["spread"], ONE + 1)
    for k in range(2):
        mm = nc.tensor.transpose(m["ps"][1][:, k * HEADS:(k + 1) * HEADS], m["ends"][0:HEADS, k * P:(k + 1) * P],
                                 m["ident"][0:HEADS, 0:HEADS])
    mm.then_inc(s["turned_back"], 1)


def run_maxima_dve(nc, dve, link, m, s, values):
    most = values[:, :].rearrange("p (c h) -> p c h", h=HEADS)
    keys = m["sorted_keys"]
    spread_maxima(nc, link, keys, most, m["mask"], m["tmp_col"], COLS, P, HEADS)
    for k, col in enumerate((most[:, 0, :], most[:, COLS - 1, :], keys[:, 0:1].broadcast_to([P, HEADS]),
                             keys[:, COLS - 1:COLS].broadcast_to([P, HEADS]))):
        link(nc.vector.tensor_copy(m["edge_cols"][:, k * HEADS:(k + 1) * HEADS], col))
    nc.vector.nop().then_inc(s["edged"], 1)
    dve.wait_ge(s["turned"], ONE + 1)
    row = m["end_rows"][:, :].rearrange("h (k n e) -> h k n e", k=2, e=2)
    for k in range(4):
        link(nc.vector.tensor_copy(row[:, k // 2, :, k % 2], m["ps"][0][0:HEADS, k * P:(k + 1) * P]))
    spread_maxima(nc, link, m["end_rows"][:, 2 * P:4 * P], m["end_rows"][:, 0:2 * P].unsqueeze(2), m["mask"], m["tmp_col"],
                  2 * P, HEADS, 1)
    for k in range(2):
        link(nc.vector.tensor_copy(m["ends"][0:HEADS, k * P:(k + 1) * P], row[:, 0, :, k]))
    nc.vector.nop().then_inc(s["spread"], 1)
    dve.wait_ge(s["turned_back"], ONE + 1)
    link(nc.vector.tensor_copy(m["end_cols"][:, :], m["ps"][1][:, 0:2 * HEADS]))
    for k in range(2):
        end_key = m["edge_cols"][:, (2 + k) * HEADS:(2 + k) * HEADS + 1]
        link(nc.vector.tensor_scalar(m["mask"][:, 0:COLS], keys[:, :], end_key, None, ALU.is_equal))
        link(nc.vector.tensor_scalar(m["mask"][:, 0:COLS], m["mask"][:, 0:COLS], 0.5, 2 * BIG, ALU.subtract, ALU.mult))
        for h in range(HEADS):
            end = m["end_cols"][:, k * HEADS + h:k * HEADS + h + 1]
            link(nc.vector.tensor_scalar(m["tmp_col"][:, 0:COLS], m["mask"][:, 0:COLS], end, None, ALU.min))
            link(nc.vector.tensor_tensor(most[:, :, h], most[:, :, h], m["tmp_col"][:, 0:COLS], ALU.max))


def stage_attention_gather(nc, m, s):
    pairs = m["sorted_pairs"].rearrange("(p c) k -> p (c k)", p=P)
    with nc.Block() as block:

        @block.sync
        def _(sp):
            sp.dma_start(m["pairs_in"][:, :], pairs).then_inc(s["loaded"], 16)
            sp.dma_start(m["u_in"][:, :], m["u_firsts"][0:E, :].rearrange("(p c) h -> p (c h)", p=P)).then_inc(s["loaded"], 16)
            with sp.Fori(0, ITERS) as i:
                for j in range(SLOTS):
                    sp.wait_ge(s["copied"][j], ONE + i)
                    sp.dma_start(m["index2"][j][:, :], pairs[:, bass.ds((SLOTS * i + j) * 2 * T, 2 * T)]).then_inc(s["indexed"][j], 16)
            sp.wait_ge(s["spread_out"], ONE + 1)
            sp.dma_start(m["u_sorted"], m["u_in"][:, :]).then_inc(s["stored"], 16)
            sp.wait_ge(s["stored"], 16)

        @block.tensor
        def _(pe):
            run_maxima_pe(nc, pe, m, s)

        @block.vector
        def _(dve):
            link = Chain(dve, s["step"])
            dve.wait_ge(s["loaded"], 32)
            link(nc.vector.tensor_copy(m["sorted_keys"][:, :], m["pairs_in"][:, :].rearrange("p (c k) -> p c k", k=2)[:, :, 0]))
            run_maxima_dve(nc, dve, link, m, s, m["u_in"])
            nc.vector.nop().then_inc(s["spread_out"], 1)

        @block.gpsimd
        def _(pool):
            with pool.Fori(0, ITERS) as i:
                for j in range(SLOTS):
                    pool.wait_ge(s["indexed"][j], 16 * (i + 1))
                    pool.wait_ge(s["copied"][j], ONE + i)
                    pool.wait_ge(s["rows_out"][j], FULL + 16 * i)
                    pool.sem_inc(s["going"], 1)
                    for t in range(T):
                        nc.gpsimd.indirect_dma_start(
                            out=m["rows"][j][:, t * XA:(t + 1) * XA], out_offset=None, in_=m["xa_table"],
                            in_offset=bass.IndirectOffsetOnAxis(ap=m["index2"][j][:, 2 * t + 1:2 * t + 2], axis=0),
                        ).then_inc(s["gathered"][j], 16)

        @block.scalar
        def _(act):
            with act.Fori(0, ITERS) as i:
                for j in range(SLOTS):
                    g = SLOTS * i + j
                    act.wait_ge(s["gathered"][j], 16 * T * (i + 1))
                    rows = cut(m["rows"][j][:, :], t=T)
                    act.dma_start(cut(m["x_sorted"].rearrange("(p c) f -> p (c f)", p=P)[:, bass.ds(g * T * F, T * F)], t=T),
                                  rows[:, :, 0:F]).then_inc(s["rows_out"][j], 16)
                    nc.scalar.copy(cut(m["logit"][:, bass.ds(g * T * HEADS, T * HEADS)], t=T), rows[:, :, F:XA]).then_inc(s["copied"][j], 1)
            for j in range(SLOTS):
                act.wait_ge(s["rows_out"][j], FULL + 16 * ITERS)


def stage_attention_maxima(nc, m, s):
    with nc.Block() as block:

        @block.tensor
        def _(pe):
            run_maxima_pe(nc, pe, m, s)

        @block.vector
        def _(dve):
            link = Chain(dve, s["step"])
            link(nc.vector.tensor_copy(m["most"][:, :], m["logit"][:, :]))
            run_maxima_dve(nc, dve, link, m, s, m["most"])


def stage_attention_exp(nc, m, s):
    with nc.Block() as block:

        @block.sync
        def _(sp):
            sp.dma_start(m["u_in"][:, :], m["u_sorted"]).then_inc(s["loaded"], 16)
            sp.wait_ge(s["weighed"], ONE + 1)
            sp.dma_start(m["weight_sorted"].rearrange("(p c) h -> p (c h)", p=P), m["logit"][:, :]).then_inc(s["stored"], 16)
            sp.wait_ge(s["stored"], 16)

        @block.vector
        def _(dve):
            link = Chain(dve, s["step"])
            dve.wait_ge(s["loaded"], 16)
            for part in (m["logit"], m["most"]):
                link(nc.vector.tensor_tensor(part[:, :], part[:, :], m["u_in"][:, :], ALU.add))
                link(nc.vector.scalar_tensor_tensor(part[:, :], part[:, :], ATT_SLOPE, part[:, :], ALU.mult, ALU.max))
            nc.vector.tensor_tensor(m["logit"][:, :], m["logit"][:, :], m["most"][:, :], ALU.subtract).then_inc(s["shifted"], 1)

        @block.scalar
        def _(act):
            act.wait_ge(s["shifted"], ONE + 1)
            nc.scalar.activation(m["logit"][:, :], m["logit"][:, :], ACT.Exp).then_inc(s["weighed"], 1)


def stage_attention_sum(nc, m, s):
    HF = HEADS * F
    W = HF + HEADS
    with nc.Block() as block:

        @block.sync
        def _(sp):
            sp.dma_start(m["sb_w_in"][:, :], m["att_w_in"]).then_inc(s["weights"], 16)
            sp.dma_start(m["sb_bias"][:, :], m["att_bias"].broadcast_to([P, F])).then_inc(s["weights"], 16)
            with sp.Fori(0, ITERS) as i:
                for j in range(SLOTS):
                    g = SLOTS * i + j
                    sp.wait_ge(s["weighed"][j], ONE + i)
                    sp.dma_start(m["x_rows"][j][:, :], m["x_sorted"].rearrange("(g p t) f -> g p (t f)", p=P, t=T)[bass.ds(g, 1)]
                                 .rearrange("g p f -> (g p) f")).then_inc(s["row_in"][j], 16)
                    sp.dma_start(m["weight"][j][:, :], m["weight_sorted"].rearrange("(g p t) h -> g p (t h)", p=P, t=T)[bass.ds(g, 1)]
                                 .rearrange("g p f -> (g p) f")).then_inc(s["row_in"][j], 16)

        @block.vector
        def _(dve):
            link = Chain(dve, s["step"])
            link(nc.vector.memset(m["acc"][:, :], 0.0))

            def weigh(i, j):
                dve.wait_ge(s["row_in"][j], 32 * (i + 1))
                rows = cut(m["rows"][j][:, :], t=T)
                weight = cut(m["weight"][j][:, :], t=T)
                nc.vector.tensor_copy(rows[:, :, HF:W], weight)
                nc.vector.tensor_tensor(rows[:, :, 0:HF].rearrange("p t (h f) -> p t h f", f=F),
                                        rep(cut(m["x_rows"][j][:, :], t=T), 2, HEADS), rep(weight, 3, F),
                                        ALU.mult).then_inc(s["weighed"][j], 1)
                hot_dve(nc, dve, m, s, SLOTS * i + j, j)
            in_turn(dve, weigh, lambda i, j: visits_dve(nc, dve, m, s, SLOTS * i + j, j, m["acc"], W))
            sums_done(nc, dve, m, s)
            acc = m["acc"][:, :].rearrange("p (b w) -> p b w", w=W)
            total = m["total"][:, :].rearrange("p (b h) -> p b h", h=HEADS)
            link(nc.vector.tensor_scalar(total, acc[:, :, HF:W], 0.5, float(HEADS), ALU.max, ALU.mult))
            link(nc.vector.reciprocal(m["total"][:, :], m["total"][:, :]))
            dve.wait_ge(s["weights"], 32)
            with dve.Fori(0, SLABS) as i:
                dve.wait_ge(s["turned"], ONE + i)
                sums = m["acc"][:, bass.ds(i * SLAB * W, SLAB * W)].rearrange("p (b w) -> p b w", w=W)
                for h in range(HEADS):
                    ins = nc.vector.tensor_tensor(
                        m["slab"][:, :].rearrange("p (b f) -> p b f", b=SLAB)[:, :, h * F:(h + 1) * F],
                        sums[:, :, h * F:(h + 1) * F],
                        rep(m["total"][:, bass.ds(i * SLAB * HEADS, SLAB * HEADS)].rearrange("p (b h) -> p b h", h=HEADS)[:, :, h], 2, F),
                        ALU.mult)
                ins.then_inc(s["slab"], 1)
                dve.wait_ge(s["result"], ONE + i + 1)
                here = m["x"][:, bass.ds(i * SLAB * F, SLAB * F)]
                nc.vector.tensor_tensor(here, here, m["ps"][2][:, 0:SLAB * F], ALU.add).then_inc(s["result_out"], 1)
            dve.wait_ge(s["result_out"], ONE + SLABS)
            cubed = lambda t: t[:, :].rearrange("p (b f) -> p b f", f=F)
            link(nc.vector.tensor_tensor(cubed(m["x"]), cubed(m["x"]), rep(m["sb_bias"][:, :], 1, NB), ALU.add))
            layer_norm(nc, dve, link, s, 1, cubed(m["x"]), cubed(m["tmp"]), m["mean"][:, :], m["root"][:, :])

        @block.scalar
        def _(act):
            with act.Fori(0, SLABS) as i:
                act.wait_ge(s["turned"], ONE + i + 1)
                act.wait_ge(s["result"], ONE + i)
                nc.scalar.copy(m["slab_turned"][:, 0:512], m["ps"][0][:, :])
                nc.scalar.copy(m["slab_turned"][:, 512:], m["ps"][1][:, 0:SLAB * P - 512]).then_inc(s["flipped"], 1)
            roots_act(nc, act, s, 1, m["root"][:, :])

        @block.tensor
        def _(pe):
            with pe.Fori(0, ITERS) as i:
                for j in range(SLOTS):
                    pe.wait_ge(s["weighed"][j], ONE + i + 1)
                    visits_pe(nc, pe, m, s, SLOTS * i + j, j, cut(m["rows"][j][:, :], t=T), W)
            pe.wait_ge(s["weights"], 32)
            with pe.Fori(0, SLABS) as i:
                pe.wait_ge(s["slab"], ONE + i + 1)
                pe.wait_ge(s["flipped"], ONE + i)
                pe.sem_inc(s["going"], 1)
                for b in range(SLAB):
                    mm = nc.tensor.transpose(m["ps"][b // 4][:, b % 4 * P:(b % 4 + 1) * P], m["slab"][:, b * P:(b + 1) * P], m["ident"][:, :])
                mm.then_inc(s["turned"], 1)
                pe.wait_ge(s["flipped"], ONE + i + 1)
                pe.wait_ge(s["result_out"], ONE + i)
                pe.sem_inc(s["going"], 1)
                for b in range(SLAB):
                    mm = nc.tensor.matmul(m["ps"][2][:, b * F:(b + 1) * F], m["slab_turned"][:, b * P:(b + 1) * P], m["sb_w_in"][:, :],
                                          start=True, stop=True)
                mm.then_inc(s["result"], 1)


U8, K16 = 8, 16
EMB = 10
SCALE1 = 1.0 / (EMB ** 0.5 * K16 ** 0.5 * (4 * U8) ** 0.5)
SCALE2 = 1.0 / (EMB ** 0.5 * K16 ** 0.5 * (2 * U8) ** 0.5)
ROOT3 = 3.0 ** 0.5
ST = 5 * U8


def stage_directions(nc, m, s):
    with nc.Block() as block:

        @block.sync
        def _(sp):
            sp.dma_start(m["dirs"][:, :], m["edge_vec"]).then_inc(s["loaded"], 16)
            sp.dma_start(m["strength"][:, :], m["edge_weight"]).then_inc(s["loaded"], 16)
            sp.dma_start(m["x_table"].rearrange("(b p) f -> p b f", p=P), m["x"][:, :].rearrange("p (b f) -> p b f", f=F)).then_inc(s["loaded"], 16)
            sp.dma_start(m["w_tensor"][:, :], m["conv_w1"]).then_inc(s["loaded"], 16)
            sp.dma_start(m["w_second"][:, :], m["conv_w2"]).then_inc(s["loaded"], 16)
            sp.dma_start(m["w_hidden"][:, :], m["conv_hidden"]).then_inc(s["loaded"], 16)
            sp.wait_ge(s["loaded"], 96)

        @block.vector
        def _(dve):
            link = Chain(dve, s["step"])
            dve.wait_ge(s["loaded"], 96)
            dirs = m["dirs"][:, :].rearrange("p (c k) -> p c k", k=3)
            link(nc.vector.tensor_tensor(m["squared"][:, :], m["dirs"][:, :], m["dirs"][:, :], ALU.mult))
            link(nc.vector.tensor_reduce(m["length"][:, :], m["squared"][:, :].rearrange("p (c k) -> p c k", k=3), AX.X, ALU.add))
            reciprocal_root(nc, dve, link, s, 1, m["length"][:, :])
            link(nc.vector.tensor_tensor(dirs, dirs, rep(m["length"][:, :], 2, 3), ALU.mult))
            link(nc.vector.tensor_scalar(m["w_tensor"][32:64, :], m["w_tensor"][32:64, :], ROOT3, None, ALU.mult))
            link(nc.vector.tensor_scalar(m["w_tensor"][64:80, :], m["w_tensor"][64:80, :], ROOT3, None, ALU.mult))
            link(nc.vector.tensor_scalar(m["w_second"][:, 256:320], m["w_second"][:, 256:320], ROOT3, None, ALU.mult))

        @block.scalar
        def _(act):
            roots_act(nc, act, s, 1, m["length"][:, :])


def stage_tensor_product(nc, m, s):
    W = F

    def sp_group(sp, i, j):
        g = SLOTS * i + j
        sp.wait_ge(s["prepared"][j], ONE + i)
        sp.dma_start(m["index2"][j][:, :], m["pairs"][:, bass.ds(g * 2 * T, 2 * T)]).then_inc(s["indexed"][j], 16)
        sp.wait_ge(s["hidden"][j], ONE + i)
        sp.dma_start(m["emb"][j][:, :], m["edge_emb"][:, bass.ds(g * T * P, T * P)]).then_inc(s["emb_in"][j], 16)

    def act_front(act, i, j):
        g = SLOTS * i + j
        act.wait_ge(s["gathered"][j], 32 * T * (i + 1))
        act.wait_ge(s["turned"], ONE + g)
        u = cut(m["u"][:, :], t=T)
        for half in range(2):
            rows = m["rows_x"][j][:, half * T * F:(half + 1) * T * F].rearrange("p (t f) -> p t f", t=T)
            nc.scalar.copy(u[:, :, half * U8:(half + 1) * U8], rows[:, :, 0:U8])
            ins = nc.scalar.copy(u[:, :, 80:128].rearrange("p t (c w) -> p t c w", c=3)[:, :, :, half * U8:(half + 1) * U8],
                                 rows[:, :, U8:F].rearrange("p t (w c) -> p t c w", c=3))
        ins.then_inc(s["copied"], 1)
        act.wait_ge(s["hidden"][j], ONE + i + 1)
        if not (isinstance(i, int) and i + j == 0):
            act.wait_ge(s["second"], ONE + T * (SLOTS * i + j - 1))
        nc.scalar.activation(m["h1"][j][:, :], m["ps"][1][:, P:P + T * K16], ACT.Relu, scale=SCALE1)
        nc.scalar.activation(m["h2"][j % 3][:, 0:512], m["ps"][2][0:K16, :], ACT.Relu, scale=SCALE2)
        nc.scalar.activation(m["h2"][j % 3][:, 512:], m["ps"][1][0:K16, 256:256 + P], ACT.Relu, scale=SCALE2).then_inc(s["bent"], 1)
        act.wait_ge(s["turned"], ONE + g + 1)
        nc.scalar.copy(m["u_turned"][:, 0:512], m["ps"][0][:, :])
        nc.scalar.copy(m["u_turned"][:, 512:], m["ps"][1][:, 0:P]).then_inc(s["flipped"], 1)

    def act_tanh(act, i, j):
        g = SLOTS * i + j
        act.wait_ge(s["summed_up"], ONE + g + 1)
        nc.scalar.activation(m["bounded"][:, :], m["unbounded"][:, :], ACT.Tanh).then_inc(s["bounded"], 1)

    def dve_front(dve, link, i, j):
        g = SLOTS * i + j
        dve.wait_ge(s["copied"], ONE + g + 1)
        u = cut(m["u"][:, :], t=T)
        r = m["dirs"][:, bass.ds(g * 3 * T, 3 * T)].rearrange("p (t c) -> p t c", c=3)
        parts = []
        for half in range(2):
            rows = m["rows_x"][j][:, half * T * F:(half + 1) * T * F].rearrange("p (t f) -> p t f", t=T)
            part = m["dots"][half][:, :].rearrange("p (t w c) -> p t w c", t=T, c=3)
            parts.append(part)
            ins = nc.vector.tensor_tensor(part, rows[:, :, U8:F].rearrange("p t (w c) -> p t w c", c=3), rep(r, 2, U8), ALU.mult)
        link(ins)
        for half in range(2):
            nc.vector.tensor_reduce(u[:, :, K16 + half * U8:K16 + (half + 1) * U8], parts[half], AX.X, ALU.add)
        nc.vector.tensor_tensor(u[:, :, 32:80].rearrange("p t (c w) -> p t c w", c=3), rep(u[:, :, 0:K16], 2, 3),
                                rep(r, 3, K16), ALU.mult).then_inc(s["prepared"][j], 1)

    def dve_first(dve, link, i, j):
        g = SLOTS * i + j
        st = cut(m["st"][:, :], t=T)
        dve.wait_ge(s["bent"], ONE + g + 1)

        def channels_sum(t):
            dve.wait_ge(s["brackets_used"], ONE + g * T + t + 1)
            return nc.vector.tensor_reduce(st[:, t, 0:32], m["wide"][:, t % 3 * 512:(t % 3 + 1) * 512].rearrange("p (w k) -> p w k", k=K16),
                                           AX.X, ALU.add).then_inc(s["reduced"], 1)

        for t in range(T):
            dve.wait_ge(s["brackets"], ONE + g * T + t + 1)
            if t >= 3:
                dve.wait_ge(s["reduced"], ONE + 2 * T * g + t - 2)
            nc.vector.tensor_tensor(m["wide"][:, t % 3 * 512:(t % 3 + 1) * 512].rearrange("p (w k) -> p w k", k=K16),
                                    m["ps"][3 + t % 2][:, :].rearrange("p (w k) -> p w k", k=K16),
                                    rep(m["h1"][j][:, t * K16:(t + 1) * K16], 1, 32), ALU.mult).then_inc(s["brackets_used"], 1)
            if t:
                channels_sum(t - 1)
        channels_sum(T - 1)
        dve.wait_ge(s["reduced"], ONE + 2 * T * g + T)
        hot_dve(nc, dve, m, s, g, j)

    def dve_dots(dve, link, i, j):
        g = SLOTS * i + j
        r = m["dirs"][:, bass.ds(g * 3 * T, 3 * T)].rearrange("p (t c) -> p t c", c=3)
        st = cut(m["st"][:, :], t=T)
        v = st[:, :, 0:24].rearrange("p t (c w) -> p t c w", c=3)
        part = m["dots"][2][:, :].rearrange("p (t w c) -> p t w c", t=T, c=3)
        link(nc.vector.tensor_tensor(part.rearrange("p t w c -> p t c w"), v, rep(r, 3, U8), ALU.mult))
        link(nc.vector.tensor_reduce(st[:, :, 32:40], part, AX.X, ALU.add))

    def dve_second(dve, link, i, j):
        g = SLOTS * i + j
        r = m["dirs"][:, bass.ds(g * 3 * T, 3 * T)].rearrange("p (t c) -> p t c", c=3)

        def channels_sum(t):
            dve.wait_ge(s["second_used"], ONE + g * T + t + 1)
            return nc.vector.tensor_reduce(m["sums"][:, t * 64:(t + 1) * 64],
                                           m["wide"][:, t % 3 * 512:(t % 3 + 1) * 512].rearrange("p (n w) -> p n w", w=U8), AX.X, ALU.add
                                           ).then_inc(s["reduced"], 1)

        for t in range(T):
            dve.wait_ge(s["second"], ONE + g * T + t + 1)
            if t >= 3:
                dve.wait_ge(s["reduced"], ONE + 2 * T * g + T + t - 2)
            bank, wide = m["ps"][5 + t % 2], m["wide"][:, t % 3 * 512:(t % 3 + 1) * 512]
            st = m["st"][:, t * ST:(t + 1) * ST]
            nc.vector.tensor_tensor(wide[:, 0:256].rearrange("p (o k) -> p o k", k=K16), bank[:, 0:256].rearrange("p (o k) -> p o k", k=K16),
                                    rep(st[:, 24:40], 1, K16), ALU.mult)
            nc.vector.tensor_tensor(wide[:, 256:448].rearrange("p (c o w) -> p c o w", c=3, w=U8),
                                    rep(bank[:, 320:384].rearrange("p (o w) -> p o w", w=U8), 1, 3),
                                    rep(st[:, 0:24].rearrange("p (c w) -> p c w", c=3), 2, U8), ALU.mult)
            nc.vector.tensor_tensor(wide[:, 448:512].rearrange("p (o w) -> p o w", w=U8),
                                    bank[:, 256:320].rearrange("p (o w) -> p o w", w=U8),
                                    rep(st[:, 24:32], 1, U8), ALU.mult).then_inc(s["second_used"], 1)
            if t:
                channels_sum(t - 1)
        channels_sum(T - 1)
        dve.wait_ge(s["reduced"], ONE + 2 * T * g + 2 * T)
        sums = cut(m["sums"][:, :], t=T)
        nc.vector.tensor_reduce(cut(m["unbounded"][:, :], t=T), sums[:, :, 0:32].rearrange("p t (o e) -> p t o e", e=2), AX.X,
                                ALU.add).then_inc(s["summed_up"], 1)
        part = m["dots"][2][:, :].rearrange("p (t c w) -> p t c w", t=T, c=3)
        link(nc.vector.tensor_tensor(part, rep(sums[:, :, 56:64], 2, 3), rep(r, 3, U8), ALU.mult))
        link(nc.vector.tensor_tensor(m["vectors"][:, :].rearrange("p (t c w) -> p t c w", t=T, c=3), part,
                                     sums[:, :, 32:56].rearrange("p t (c w) -> p t c w", c=3), ALU.add))

    def dve_rows(dve, link, i, j):
        g = SLOTS * i + j
        dve.wait_ge(s["bounded"], ONE + g + 1)
        strength = m["strength"][:, bass.ds(g * T, T)]
        rows = cut(m["rows"][j][:, :], t=T)
        link(nc.vector.tensor_tensor(cut(m["gates"][:, :], t=T), cut(m["bounded"][:, :], t=T)[:, :, U8:K16], rep(strength, 2, U8), ALU.mult))
        nc.vector.tensor_tensor(rows[:, :, 0:U8], cut(m["bounded"][:, :], t=T)[:, :, 0:U8], rep(strength, 2, U8), ALU.mult)
        nc.vector.tensor_tensor(rows[:, :, U8:F].rearrange("p t (w c) -> p t c w", c=3),
                                m["vectors"][:, :].rearrange("p (t c w) -> p t c w", t=T, c=3),
                                rep(cut(m["gates"][:, :], t=T), 2, 3), ALU.mult).then_inc(s["edge_rows"], 1)

    def pe_front(pe, i, j):
        g = SLOTS * i + j
        pe.wait_ge(s["emb_in"][j], 16 * (i + 1))
        pe.wait_ge(s["bent"], ONE + g)
        pe.wait_ge(s["flipped"], ONE + g)
        pe.sem_inc(s["going"], 1)
        for t in range(T):
            nc.tensor.matmul(m["ps"][1][:, P + t * K16:P + (t + 1) * K16], m["emb"][j][:, t * P:(t + 1) * P], m["w_hidden"][:, 0:K16],
                             start=True, stop=True)
        nc.tensor.matmul(m["ps"][2][0:K16, :], m["w_hidden"][:, K16:2 * K16], m["emb"][j][:, 0:512], start=True, stop=True)
        nc.tensor.matmul(m["ps"][1][0:K16, 256:256 + P], m["w_hidden"][:, K16:2 * K16], m["emb"][j][:, 512:],
                         start=True, stop=True).then_inc(s["hidden"][j], 1)
        pe.wait_ge(s["prepared"][j], ONE + i + 1)
        pe.wait_ge(s["bent"], ONE + g + 1)
        pe.sem_inc(s["going"], 1)
        for t in range(T):
            mm = nc.tensor.transpose(m["ps"][t // 4][:, t % 4 * P:(t % 4 + 1) * P], m["u"][:, t * P:(t + 1) * P], m["ident"][:, :])
        mm.then_inc(s["turned"], 1)

    def pe_first(pe, i, j):
        g = SLOTS * i + j
        pe.wait_ge(s["flipped"], ONE + g + 1)
        for t in range(T):
            pe.wait_ge(s["brackets_used"], ONE + g * T + max(t - 1, 0))
            pe.sem_inc(s["going"], 1)
            nc.tensor.matmul(m["ps"][3 + t % 2][:, :], m["u_turned"][:, t * P:(t + 1) * P], m["w_tensor"][:, :],
                             start=True, stop=True).then_inc(s["brackets"], 1)

    def pe_second(pe, i, j, tiles):
        g = SLOTS * i + j
        pe.wait_ge(s["bent"], ONE + g + 1)
        for t in tiles:
            pe.wait_ge(s["second_used"], ONE + g * T + max(t - 1, 0))
            pe.sem_inc(s["going"], 1)
            mm = nc.tensor.matmul(m["ps"][5 + t % 2][:, 0:384], m["h2"][j % 3][:, t * P:(t + 1) * P], m["w_second"][:, :],
                                  start=True, stop=True)
            mm.then_inc(s["second"], 1)

    def pe_sums(pe, i, j):
        pe.wait_ge(s["edge_rows"], ONE + SLOTS * i + j + 1)
        visits_pe(nc, pe, m, s, SLOTS * i + j, j, cut(m["rows"][j][:, :], t=T), W)

    def before(i, j, step):
        if not (isinstance(i, int) and i + j == 0):
            step(i - (j == 0), (j - 1) % SLOTS)

    with nc.Block() as block:

        @block.sync
        def _(sp):
            with sp.Fori(0, ITERS) as i:
                for j in range(SLOTS):
                    sp_group(sp, i, j)
            sp.wait_ge(s["finished"], ONE + 1)
            sp.dma_start(m["out"], m["x"][:, :]).then_inc(s["stored"], 16)
            sp.wait_ge(s["stored"], 16)

        @block.gpsimd
        def _(pool):
            with pool.Fori(0, ITERS) as i:
                for j in range(SLOTS):
                    pool.wait_ge(s["indexed"][j], 16 * (i + 1))
                    pool.wait_ge(s["prepared"][j], ONE + i)
                    pool.sem_inc(s["going_pool"], 1)
                    for t in range(T):
                        for half in range(2):
                            to = half * T * F + t * F
                            nc.gpsimd.indirect_dma_start(
                                out=m["rows_x"][j][:, to:to + F], out_offset=None, in_=m["x_table"],
                                in_offset=bass.IndirectOffsetOnAxis(ap=m["index2"][j][:, 2 * t + half:2 * t + half + 1], axis=0),
                            ).then_inc(s["gathered"][j], 16)

        @block.scalar
        def _(act):
            in_turn(act, lambda i, j: act_front(act, i, j), lambda i, j: act_tanh(act, i, j))
            roots_act(nc, act, s, 1, m["root"][:, :])

        @block.vector
        def _(dve):
            link = Chain(dve, s["step"])
            link(nc.vector.memset(m["acc"][:, :], 0.0))
            LINKS = 6

            def own(i, j):
                begins = 2 if isinstance(i, int) and i + j == 0 else 1
                link.base, link.n = (SLOTS * i + j) * LINKS + begins, 0
                dve_first(dve, link, i, j)

            def behind(i, j):
                before(i, j, lambda i, j: dve_rows(dve, link, i, j))
                dve_dots(dve, link, i, j)
                dve_second(dve, link, i, j)
                before(i, j, lambda i, j: visits_dve(nc, dve, m, s, SLOTS * i + j, j, m["acc"], W))
            in_turn(dve, lambda i, j: dve_front(dve, link, i, j), behind, own, peeled=1)
            link.base, link.n = GROUPS * LINKS, 0
            dve_rows(dve, link, ITERS - 1, SLOTS - 1)
            visits_dve(nc, dve, m, s, GROUPS - 1, SLOTS - 1, m["acc"], W)
            sums_done(nc, dve, m, s)
            cubed = lambda t: t[:, :].rearrange("p (b f) -> p b f", f=F)
            link(nc.vector.tensor_tensor(m["x"][:, :], m["x"][:, :], m["acc"][:, :], ALU.add))
            layer_norm(nc, dve, link, s, 1, cubed(m["x"]), cubed(m["tmp"]), m["mean"][:, :], m["root"][:, :])
            nc.vector.nop().then_inc(s["finished"], 1)

        @block.tensor
        def _(pe):
            def behind(i, j):
                pe_second(pe, i, j, range(2, T))
                before(i, j, lambda i, j: pe_sums(pe, i, j))

            def own(i, j):
                pe_first(pe, i, j)
                pe_second(pe, i, j, range(2))
            in_turn(pe, lambda i, j: pe_front(pe, i, j), behind, own, peeled=1)
            pe_sums(pe, ITERS - 1, SLOTS - 1)


def build(nc, d):
    with ExitStack() as ctx:
        m = dict(d)

        def sb(name, cols, dt=F32, parts=P, into=None):
            t = (into or ctx).enter_context(nc.sbuf_tensor(f"{name}_{nc.next_id()}", [parts, cols], dt))
            m[name] = t
            return t

        taken, primed = [], [0]

        def sems(stage, plain, slotted=""):
            if taken:
                nc.clear_and_free_semaphores(list(taken))
                nc.all_engine_barrier()
                taken.clear()

            def sem(name, slot=""):
                taken.append(nc.alloc_semaphore(name=f"{stage}_{name}{slot}"))
                if name in RECYCLED:
                    cell = primed[0]
                    primed[0] += 1
                    nc.sync.dma_start(m["scrap"][0:1, cell:cell + 1], m["dst"][0:1, 0:1]).then_inc(taken[-1], FULL)
                elif name not in FROM_ZERO:
                    nc.sync.sem_inc(taken[-1], ONE)
                return taken[-1]

            s = {}
            for n in plain.split():
                s[n] = sem(n)
            for n in slotted.split():
                s[n] = [sem(n, j) for j in range(SLOTS)]
            nc.all_engine_barrier()
            return s

        m["ps"] = [ctx.enter_context(nc.psum_tensor(f"bank{k}", [P, 512], F32)) for k in range(8)]
        sb("x", NB * F); sb("tmp", NB * F); sb("mean", NB); sb("root", NB)
        sb("out_deg", NB); sb("in_deg", NB); sb("first_place", NB, I32)
        sb("part", 1); sb("scrap", 64, I32, parts=1); sb("ramp", P); sb("starts", NB); sb("ident", P); sb("before", P); sb("ones", P); sb("zeros", P, BF16); sb("zero_row", 512, BF16); sb("attr_sum", 2 * F)
        sb("window", GROUPS, I32)
        sb("a1_stats", 8); sb("square_sum", 1); sb("w", P)

        whole = ctx.enter_context(ExitStack())
        sb("acc", NB * (H + 1), into=whole)
        with ExitStack() as scope:
            sb("keys", COLS, into=scope); m["onehot"] = [scope.enter_context(nc.sbuf_tensor(f"onehot_{nc.next_id()}", [P, T * P], F32)) for k in range(3)]
            with ExitStack() as inner:
                sb("ints", COLS, I32, into=inner); sb("src_int", COLS, I32, into=inner)
                sb("low", COLS, into=inner); sb("high", COLS, into=inner)
                m["hot_low"] = [inner.enter_context(nc.sbuf_tensor(f"hot_low{j}", [P, T * P], BF16)) for j in range(SLOTS)]
                m["hot_high"] = [inner.enter_context(nc.sbuf_tensor(f"hot_high{j}", [P, T * NB], BF16)) for j in range(SLOTS)]
                m["attr"] = [inner.enter_context(nc.sbuf_tensor(f"attr{j}", [P, T * F], F32)) for j in range(SLOTS)]
                m["attr_square"] = [inner.enter_context(nc.sbuf_tensor(f"attr_square{j}", [P, T * F], F32)) for j in range(SLOTS)]
                stage_setup(nc, m, sems("setup", "squared step zero loaded x_loaded iota hot histogram", "counted attr_in attr_used"))
            with ExitStack() as inner:
                sb("ints", COLS, I32, into=inner); sb("floats", COLS, into=inner); sb("keys_int", COLS, I32, into=inner)
                sb("least", GROUPS, into=inner); sb("most", GROUPS, into=inner)
                sb("wide", SLOTS, into=inner); sb("win", 3 * SLOTS, into=inner); sb("win_int", 3 * SLOTS, I32, into=inner); sb("words", SLOTS, I32, into=inner)
                stage_windows(nc, m, False, sems("window", "loaded step extremes turned counted prefixed tabled stored"))
            with ExitStack() as inner:
                m["rows"] = [inner.enter_context(nc.sbuf_tensor(f"rows{j}", [P, T * (F + 1)], F32)) for j in range(SLOTS)]
                m["index"] = [inner.enter_context(nc.sbuf_tensor(f"index{j}", [P, T], I32)) for j in range(SLOTS)]
                stage_convolve(nc, m, sems("conv", "to_root rooted going step scaled cleared stored windows first_hot more_hot summed added", "gathered indexed used"))
            for name, shape in (("m1_w1", [C2, H]), ("m1_c1", [H, 1]), ("m1_g1", [C2, 1]), ("m1_b1", [C2, 1]),
                                ("m1_w2", [H, H]), ("m1_g2", [H, 1]), ("m1_b2", [H, 1]), ("m1_c2", [P, H])):
                sb("sb_" + name, shape[1], parts=shape[0], into=scope)
            with ExitStack() as inner:
                def slots(name, cols, dt=F32, parts=P):
                    m[name] = [inner.enter_context(nc.sbuf_tensor(f"{name}_{nc.next_id()}", [parts, cols], dt))
                               for _ in range(SLOTS)]
                slots("rows", T * C2); slots("index", T, I32); slots("a1", T * P, parts=H)
                m["lift"] = [inner.enter_context(nc.sbuf_tensor(f"lift{j}", [H, T * P], F32)) for j in range(2)]
                sb("flipped", T * P, parts=C2, into=inner); sb("stats", GROUPS * 12, parts=H, into=inner)
                sb("bn", 8, into=inner); sb("bias", 1, into=inner); sb("sums", C2, into=inner); sb("total_row", 2 * C2, into=inner)
                stage_edges_first(nc, m, sems("first", "step to_root rooted going stored weights node_sums totals rowed columns folded shifted biased multiplied flipped lifted a1_made counted", "gathered indexed turned attr_in a1_out"))
            with ExitStack() as inner:
                slots("rows", T * (H + 1)); slots("a1", T * P, parts=H)
                sb("squares", T * H, into=inner); sb("lift2", T * H, into=inner)
                sb("wide_shift", P, into=inner); sb("bias_row", H, into=inner)
                slots("hot_low", T * P, BF16); slots("hot_high", T * NB, BF16); slots("same", T * P, BF16)
                slots("src_row", T * P, I32); slots("pair", 2 * T, I32); slots("place", T); slots("place_int", T, I32)
                sb("src_float", COLS, into=inner); sb("low", COLS, BF16, into=inner); sb("high", COLS, BF16, into=inner)
                sb("src_int", COLS, I32, into=inner); sb("ints", COLS, I32, into=inner)
                sb("turned", T * P, into=inner); sb("counts", NB, into=inner); sb("first_float", NB, into=inner)
                sb("sums", P, into=inner); sb("picked", T * NB, into=inner); sb("ident_half", P, BF16, into=inner)
                m["ps_turn"] = m["ps"][4][:, :].bitcast(BF16)
                stage_edges_second_and_sort(nc, m, sems(
                    "second", "step to_root rooted weights folded shifted biased lifted a2_made squared squares_used windows first_hot "
                    "more_hot summed added loaded sums sums_out begun counts_out counted turned turned_out hot_lows hot_highs "
                    "looked picked going", "products a1_in compared moved freed placed row_in pair_in"))
        with ExitStack() as inner:
            shapes = dict(m1_w3=[H, H], m1_g3=[H, 1], m1_b3=[H, 1], m2_g1a=[H, 1], m2_b1a=[H, 1], m2_w1a=[H, W96],
                          m2_g1x=[F, 1], m2_b1x=[F, 1], m2_w1x=[F, W96], m2_c1=[W96, 1], m2_g2=[W96, 1], m2_b2=[W96, 1],
                          m2_w2=[W96, W96], m2_c2=[W96, 1], m2_g3=[W96, 1], m2_b3=[W96, 1], m2_w3=[W96, F], m2_c3=[F, 1])
            m["node_weights"] = tuple(shapes)
            for name, (parts, cols) in shapes.items():
                sb("sb_" + name, cols, parts=parts, into=inner)
            sb("h", NP, parts=W96, into=inner); sb("x_turned", NP, parts=F, into=inner)
            sb("acc_slab", SLAB * (H + 1), into=inner); sb("x_slab", SLAB * F, into=inner); sb("out_slab", SLAB * P, parts=F, into=inner)
            sb("acc_turned", SLAB * P, into=inner); sb("node_lift", CHUNK, parts=W96, into=inner)
            sb("stats", NCHUNKS * 6, into=inner); sb("stats_x", NCHUNKS * 6, into=inner)
            for name in ("bn3", "bn_agg", "bn_x", "bn_h"):
                sb(name, 8, into=inner)
            sb("fold3", H + 1, parts=H, into=inner); sb("w3", H, into=inner); sb("c3_row", H, into=inner)
            sb("wa", W96, parts=H, into=inner); sb("wx", W96, parts=F, into=inner); sb("wh", W96, parts=W96, into=inner)
            sb("bias96", 1, into=inner); sb("sums", H, into=inner)
            stage_nodes(nc, m, sems("nodes", "step to_root rooted going weights cleared turned slab product bent lifted biased turned_back summed totals folded w3_made w3_out flipped agged agg_out measured shifted added"))
        whole.close()
        with ExitStack() as outer:
            sb("logit", COLS * HEADS, into=outer); sb("most", COLS * HEADS, into=outer)
            m["u_in"] = m["most"]
            with ExitStack() as keyed:
                sb("sorted_keys", COLS, into=keyed); sb("mask", COLS, into=keyed); sb("tmp_col", COLS, into=keyed)
                sb("edge_cols", 4 * HEADS, into=keyed); sb("end_rows", 4 * P, parts=HEADS, into=keyed)
                sb("ends", 2 * P, parts=HEADS, into=keyed); sb("end_cols", 2 * HEADS, into=keyed)
                with ExitStack() as inner:
                    sb("sb_w_out", HEADS * F, parts=F, into=inner); sb("sb_fc", 2, parts=F, into=inner); sb("sb_fc_b", 1, into=inner)
                    sb("vectors", 8, parts=F, into=inner); sb("x_slab", SLAB * F, into=inner); sb("x_turned_slab", SLAB * P, parts=F, into=inner)
                    sb("u", NB * HEADS, into=inner); sb("xa", NB * XA, into=inner)
                    stage_attention_tables(nc, m, sems("tables", "weights built blank stored vectors vectors_out slab flipped going going_pool moved turned logits logits_out"))
                with ExitStack() as inner:
                    sb("pairs_in", 2 * COLS, I32, into=inner)
                    for name, cols, dt in (("rows", T * XA, F32), ("index2", 2 * T, I32)):
                        m[name] = [inner.enter_context(nc.sbuf_tensor(f"{name}_{nc.next_id()}", [P, cols], dt)) for j in range(SLOTS)]
                    stage_attention_gather(nc, m, sems("att_gather", "going loaded step edged turned spread turned_back spread_out stored", "gathered indexed copied rows_out"))
                stage_attention_maxima(nc, m, sems("att_max", "step edged turned spread turned_back"))
            with ExitStack() as inner:
                sb("u_in", COLS * HEADS, into=inner)
                stage_attention_exp(nc, m, sems("att_exp", "loaded step weighed stored shifted"))
        with ExitStack() as scope:
            sb("keys", COLS, into=scope); m["onehot"] = [scope.enter_context(nc.sbuf_tensor(f"onehot_{nc.next_id()}", [P, T * P], F32)) for k in range(3)]
            with ExitStack() as inner:
                sb("ints", COLS, I32, into=inner); sb("floats", COLS, into=inner); sb("keys_int", COLS, I32, into=inner)
                sb("pairs_in", 2 * COLS, I32, into=inner)
                sb("least", GROUPS, into=inner); sb("most", GROUPS, into=inner)
                sb("wide", SLOTS, into=inner); sb("win", 3 * SLOTS, into=inner); sb("win_int", 3 * SLOTS, I32, into=inner); sb("words", SLOTS, I32, into=inner)
                stage_windows(nc, m, True, sems("src_window", "loaded step extremes turned counted prefixed tabled stored"))
            with ExitStack() as inner:
                HF = HEADS * F
                sb("acc", NB * (HF + HEADS), into=inner); sb("total", NB * HEADS, into=inner); sb("slab", SLAB * P, into=inner)
                sb("slab_turned", SLAB * P, into=inner); sb("sb_w_in", F, into=inner); sb("sb_bias", F, into=inner)
                for name, cols in (("rows", T * (HF + HEADS)), ("x_rows", T * F), ("weight", T * HEADS)):
                    m[name] = [inner.enter_context(nc.sbuf_tensor(f"{name}_{nc.next_id()}", [P, cols], F32)) for j in range(SLOTS)]
                stage_attention_sum(nc, m, sems("att_sum", "to_root rooted weights step going slab turned flipped result result_out windows first_hot more_hot summed added", "weighed row_in"))
        with ExitStack() as scope:
            sb("keys", COLS, into=scope); m["onehot"] = [scope.enter_context(nc.sbuf_tensor(f"onehot_{nc.next_id()}", [P, T * P], F32)) for k in range(3)]
            with ExitStack() as inner:
                sb("ints", COLS, I32, into=inner); sb("floats", COLS, into=inner); sb("keys_int", COLS, I32, into=inner)
                sb("least", GROUPS, into=inner); sb("most", GROUPS, into=inner)
                sb("wide", SLOTS, into=inner); sb("win", 3 * SLOTS, into=inner); sb("win_int", 3 * SLOTS, I32, into=inner); sb("words", SLOTS, I32, into=inner)
                stage_windows(nc, m, False, sems("dst_window", "loaded step extremes turned counted prefixed tabled stored"))
            sb("dirs", COLS * 3, into=scope); sb("strength", COLS, into=scope)
            sb("w_tensor", 512, into=scope); sb("w_second", 384, parts=K16, into=scope); sb("w_hidden", 2 * K16, parts=EMB, into=scope)
            with ExitStack() as inner:
                sb("squared", COLS * 3, into=inner); sb("length", COLS, into=inner)
                stage_directions(nc, m, sems("dirs", "loaded step to_root rooted"))
            with ExitStack() as inner:
                for name, parts, cols, dt in (("index2", P, 2 * T, I32), ("emb", EMB, T * P, F32), ("rows_x", P, 2 * T * F, F32),
                                              ("h1", P, T * K16, F32), ("rows", P, T * F, F32)):
                    m[name] = [inner.enter_context(nc.sbuf_tensor(f"{name}_{nc.next_id()}", [parts, cols], dt))
                               for _ in range(SLOTS)]
                m["h2"] = [inner.enter_context(nc.sbuf_tensor(f"h2_{k}", [K16, T * P], F32)) for k in range(3)]
                m["dots"] = [inner.enter_context(nc.sbuf_tensor(f"dots_{nc.next_id()}", [P, T * 24], F32)) for k in range(3)]
                sb("u", T * P, into=inner); sb("u_turned", T * P, into=inner); sb("wide", 3 * 512, into=inner)
                sb("st", T * ST, into=inner); sb("sums", T * 64, into=inner); sb("unbounded", T * K16, into=inner)
                sb("bounded", T * K16, into=inner); sb("gates", T * U8, into=inner); sb("vectors", T * 24, into=inner); m["acc"] = m["tmp"]
                stage_tensor_product(nc, m, sems("tp", "reduced step to_root rooted finished stored going going_pool turned copied bent flipped summed_up bounded brackets brackets_used second second_used edge_rows windows first_hot more_hot summed added", "gathered indexed emb_in hidden prepared"))


def by_group(a):
    a = np.asarray(a)
    return np.ascontiguousarray(a.reshape(GROUPS, P, T, -1).transpose(1, 0, 2, 3).reshape(P, -1))


def laid_out(x, src, dst, edge_attr_10, edge_attr_3, edge_attr_32, edge_weight, **w):
    x_in = np.zeros((NP, F), np.float32)
    x_in[:N] = x
    col = lambda a: np.ascontiguousarray(np.asarray(a).reshape(-1, 1))
    row = lambda a: np.ascontiguousarray(np.asarray(a).reshape(1, -1))
    l1 = {k[len("L1_gnn_"):]: np.asarray(v) for k, v in w.items() if k.startswith("L1_gnn_m")}
    w1, g1, b1 = l1["m2_w1"], l1["m2_g1"], l1["m2_b1"]
    att_w = np.asarray(w["L2_gnn_w"])
    out = dict(
        x_in=np.ascontiguousarray(x_in.reshape(NB, P, F).transpose(1, 0, 2).reshape(P, -1)),
        src=by_group(src), dst=by_group(dst), pairs=by_group(np.stack([src, dst], 1)),
        src_rows=np.ascontiguousarray(np.asarray(src).reshape(GROUPS, P, T).transpose(0, 2, 1).reshape(GROUPS, -1)),
        edge_attr=by_group(edge_attr_32), edge_vec=by_group(edge_attr_3), edge_weight=by_group(edge_weight),
        edge_emb=np.ascontiguousarray(np.asarray(edge_attr_10).reshape(GROUPS, P, T, EMB).transpose(3, 0, 2, 1).reshape(EMB, -1)),
        m1_c2=row(l1["m1_c2"]), m1_c3=row(l1["m1_c3"]),
        m2_g1a=col(g1[F:]), m2_b1a=col(b1[F:]), m2_w1a=np.ascontiguousarray(w1[F:]),
        m2_g1x=col(g1[:F]), m2_b1x=col(b1[:F]), m2_w1x=np.ascontiguousarray(w1[:F]),
        att_w_out=np.ascontiguousarray(att_w.transpose(2, 0, 1).reshape(F, -1)),
        att_fc=np.ascontiguousarray(np.asarray(w["L2_gnn_fc_w"]).reshape(2, F).T),
        att_fc_b=np.asarray(w["L2_gnn_fc_b"]).reshape(1, 1),
        att_w_in=np.ascontiguousarray(att_w.reshape(-1, F)), att_bias=row(w["L2_gnn_bias"]),
    )
    for k in ("m1_w1", "m1_w2", "m1_w3", "m2_w2", "m2_w3"):
        out[k] = l1[k]
    for k in ("m1_c1", "m1_g1", "m1_b1", "m1_g2", "m1_b2", "m1_g3", "m1_b3", "m2_c1", "m2_g2", "m2_b2", "m2_c2", "m2_g3",
              "m2_b3", "m2_c3"):
        out[k] = col(l1[k])
    t1 = np.asarray(w["L3_gnn_fc1_w2"]).reshape(K16, 4, 2 * U8, U8).transpose(1, 2, 3, 0)
    big = np.zeros((P, 4, U8, K16), np.float32)
    big[0:16, 3], big[16:32, 3] = t1[0], t1[1]
    for c in range(3):
        big[32 + 16 * c:48 + 16 * c, c] = t1[2]
        big[80 + 16 * c:96 + 16 * c, c] = t1[3]
    out["conv_w1"] = big.reshape(P, 512)
    t2 = np.asarray(w["L3_gnn_fc2_w2"]).reshape(K16, 6, U8, U8).transpose(0, 1, 3, 2)
    out["conv_w2"] = np.ascontiguousarray(np.concatenate(
        [np.concatenate([t2[:, 0], t2[:, 1]], 2).reshape(K16, -1), np.concatenate([t2[:, 2], t2[:, 3]], 2).reshape(K16, -1),
         t2[:, 4].reshape(K16, -1), t2[:, 5].reshape(K16, -1)], 1))
    out["conv_hidden"] = np.ascontiguousarray(np.concatenate([w["L3_gnn_fc1_w1"], w["L3_gnn_fc2_w1"]], 1))
    return {k: np.ascontiguousarray(v) for k, v in out.items()}


_INTERNAL = dict(sorted_pairs=((E, 2), I32), x_table=((NP, F), F32), window_dram=((GROUPS, 1), I32),
                 a1_dram=((GROUPS, H, T * P), F32), xa_table=((NP, XA), F32), u_firsts=((E + NP, HEADS), F32),
                 x_sorted=((E, F), F32), u_sorted=((P, COLS * HEADS), F32), weight_sorted=((E, HEADS), F32))


def kernel(**inputs):
    import concourse.bacc as bacc
    from concourse.bass_utils import run_bass_kernel_spmd

    nc = bacc.Bacc("TRN2", target_bir_lowering=False, num_devices=1)
    arrays = laid_out(**{k: np.asarray(v) for k, v in inputs.items()})
    d = {k: nc.dram_tensor(f"in_{k}", a.shape, mybir.dt.from_np(a.dtype), kind="ExternalInput").ap() for k, a in arrays.items()}
    for k, (shape, dt) in _INTERNAL.items():
        d[k] = nc.dram_tensor(k, shape, dt, kind="Internal").ap()
    d["out"] = nc.dram_tensor("out", (P, NB * F), F32, kind="ExternalOutput").ap()
    build(nc, d)
    r = run_bass_kernel_spmd(nc, [{f"in_{k}": a for k, a in arrays.items()}], core_ids=[0])
    out = np.asarray(r.results[0]["out"])
    return np.ascontiguousarray(out.reshape(P, NB, F).transpose(1, 0, 2).reshape(NP, F)[:N])
```
